# Optimizing a Trainium2 kernel written in Bass

```python
import numpy as np
import jax
import jax.numpy as jnp

def _softmax(x, axis=-1):
    return jax.nn.softmax(x, axis=axis)

def _gelu(x):
    return jax.nn.gelu(x, approximate=True)

def _silu(x):
    return jax.nn.silu(x)

def _sigmoid(x):
    return jax.nn.sigmoid(x)

def _layernorm(x, axis=-1, eps=1e-05):
    m = jnp.mean(x, axis=axis, keepdims=True)
    v = jnp.var(x, axis=axis, keepdims=True)
    return (x - m) / jnp.sqrt(v + eps)

def _scatter_add(tgt, idx, src, axis=0):
    return tgt.at[idx].add(src)

def _segment_sum(src, seg, n):
    return jax.ops.segment_sum(src, seg, n)
kernel_name = 'mk_flamingo_gated_d2_seqx_r4_fdd3f1'

def setup_inputs(seed: int=0):
    np.random.seed(seed)
    _w = jnp.asarray

    def _rec_inputs():
        import jax
        import jax.numpy as jnp
        _rk = jax.random.key(seed)
        x = 7.22e-05 + 1 * jax.random.normal(jax.random.fold_in(_rk, 1), (32, 128, 256), jnp.float32)
        _lenS = 128 - jax.random.randint(jax.random.fold_in(_rk, 7), (32,), 0, max(1, 128 // 4) + 1, jnp.int32)
        _lenS2 = 128 - jax.random.randint(jax.random.fold_in(_rk, 8), (32,), 0, max(1, 128 // 4) + 1, jnp.int32)
        _ctx_1024P = jax.random.normal(jax.random.fold_in(_rk, 11), (32, 16, 256), jnp.float32)
        _ctx_1024c = jax.random.dirichlet(jax.random.fold_in(_rk, 511), 0.3 * jnp.ones((16,), jnp.float32), (32, 128))
        _ctx_1024t = jnp.einsum('bsk,bkd->bsd', _ctx_1024c, _ctx_1024P)
        _ctx_1024t = _ctx_1024t * jax.lax.rsqrt(jnp.mean(jnp.square(_ctx_1024t)) + 1e-12) * 0.953939
        ctx_1024 = 4.13588e-05 + 0.999923 * (_ctx_1024t + 0.3 * jax.random.normal(jax.random.fold_in(_rk, 611), (32, 128, 256), jnp.float32))
        _validS = jnp.arange(128)[None, :] < _lenS[:, None]
        _validS2 = jnp.arange(128)[None, :] < _lenS2[:, None]
        _causal = jnp.tril(jnp.ones((128, 128), dtype=bool))
        mask_BxS2_ik0 = jnp.where(jnp.broadcast_to(_validS2[:, :], (32, 128)), 0, 1).astype(jnp.int32)
        _g = jax.random.normal(jax.random.fold_in(_rk, 9001), (2, 2), jnp.float32)
        _g = jnp.sign(_g) * jnp.maximum(jnp.abs(_g), 1.0) + (_g == 0) * 1.0
        g_xattn = _g[0]
        g_ffn = _g[1]
        return (x, ctx_1024, mask_BxS2_ik0, g_xattn, g_ffn)
    x, ctx_1024, mask_BxS2_ik0, g_xattn, g_ffn = _rec_inputs()

    def _L0_xattn_setup():
        import jax, jax.numpy as jnp
        import numpy as np
        import math
        N_HEADS = 16
        HDIM = 256
        NEG_INF = -1e+20
        key = jax.random.key(seed)
        ks = jax.random.split(key, 12)
        B, Q, K, D = (4, 512, 512, 256)
        xavier = lambda k, shape: jax.random.normal(k, shape, jnp.float32) * math.sqrt(2.0 / (shape[0] + shape[1]))
        return {'query': jax.random.normal(ks[0], (B, Q, D), jnp.float32), 'key': jax.random.normal(ks[1], (B, K, D), jnp.float32), 'value': jax.random.normal(ks[2], (B, K, D), jnp.float32), 'mask': jax.random.randint(ks[3], (B, K), 0, 2, jnp.int32), 'Wq': xavier(ks[4], (D, HDIM)), 'bq': jnp.zeros((HDIM,), jnp.float32), 'Wk': xavier(ks[5], (D, HDIM)), 'bk': jnp.zeros((HDIM,), jnp.float32), 'Wv': xavier(ks[6], (D, HDIM)), 'bv': jnp.zeros((HDIM,), jnp.float32), 'Wo': xavier(ks[7], (HDIM, HDIM)), 'bo': jnp.zeros((HDIM,), jnp.float32)}
    _L0_xattn_all = _L0_xattn_setup()
    _L0_xattn_in = {k: v for k, v in _L0_xattn_all.items() if k in ('Wq', 'bq', 'Wk', 'bk', 'Wv', 'bv', 'Wo', 'bo')}
    del _L0_xattn_all

    def _L0_ffn_setup():
        import jax, jax.numpy as jnp
        import numpy as np
        B, S, H = (4, 512, 256)
        E = 8
        GS = 2
        NG = E // GS
        F = int(H * 4 * (2.0 / 3.0))
        key = jax.random.key(seed)
        ks = jax.random.split(key, 7)
        sc_h = 1.0 / np.sqrt(H)
        sc_f = 1.0 / np.sqrt(F)
        return {'x': jax.random.normal(ks[0], (B, S, H), dtype=jnp.float32), 'Wr': jax.random.normal(ks[1], (H, E), dtype=jnp.float32) * sc_h, 'br': jnp.zeros((E,), dtype=jnp.float32), 'W_up': jax.random.normal(ks[2], (NG, H, F), dtype=jnp.float32) * sc_h, 'b_up': jax.random.normal(ks[3], (NG, F), dtype=jnp.float32) * 0.01, 'W_down': jax.random.normal(ks[4], (E, F, H), dtype=jnp.float32) * sc_f, 'b_down': jax.random.normal(ks[5], (E, H), dtype=jnp.float32) * 0.01}
    _L0_ffn_all = _L0_ffn_setup()
    _L0_ffn_in = {k: v for k, v in _L0_ffn_all.items() if k in ('Wr', 'br', 'W_up', 'b_up', 'W_down', 'b_down')}
    del _L0_ffn_all

    def _L1_xattn_setup():
        import jax, jax.numpy as jnp
        import numpy as np
        B, L_ENC, L_DEC, D = (16, 128, 128, 256)
        key = jax.random.key(seed)
        k1, k2, k3, k4, k5, k6 = jax.random.split(key, 6)
        encoder_hc = jax.random.normal(k1, (B, L_ENC, D), dtype=jnp.float32)
        decoder_hq = jax.random.normal(k2, (B, L_DEC, D), dtype=jnp.float32)
        w_sim = jax.random.normal(k3, (3 * D,), dtype=jnp.float32) * 0.02
        b_sim = jax.random.normal(k4, (1,), dtype=jnp.float32) * 0.02
        W_qv = jax.random.normal(k5, (4 * D, D), dtype=jnp.float32) * 0.02
        b_qv = jax.random.normal(k6, (D,), dtype=jnp.float32) * 0.02
        return {'encoder_hc': encoder_hc, 'decoder_hq': decoder_hq, 'w_sim': w_sim, 'b_sim': b_sim, 'W_qv': W_qv, 'b_qv': b_qv}
    _L1_xattn_all = _L1_xattn_setup()
    _L1_xattn_in = {k: v for k, v in _L1_xattn_all.items() if k in ('w_sim', 'b_sim', 'W_qv', 'b_qv')}
    del _L1_xattn_all

    def _L1_ffn_setup():
        import jax, jax.numpy as jnp
        import numpy as np
        H = 256
        E = 8
        B, S = (4, 512)
        key = jax.random.key(seed)
        k1, k2, k3, k4 = jax.random.split(key, 4)
        x = jax.random.normal(k1, (B, S, H), dtype=jnp.float32)
        wg = jax.random.normal(k2, (H, E), dtype=jnp.float32) * 0.02
        W = jax.random.normal(k3, (E, H, H), dtype=jnp.float32) * 0.02
        b = jax.random.normal(k4, (E, H), dtype=jnp.float32) * 0.02
        return {'x': x, 'wg': wg, 'W': W, 'b': b}
    _L1_ffn_all = _L1_ffn_setup()
    _L1_ffn_in = {k: v for k, v in _L1_ffn_all.items() if k in ('wg', 'W', 'b')}
    del _L1_ffn_all
    return {'x': x, 'ctx_1024': ctx_1024, 'mask_BxS2_ik0': mask_BxS2_ik0, 'g_xattn': g_xattn, 'g_ffn': g_ffn, 'L0_xattn_Wq': _L0_xattn_in['Wq'], 'L0_xattn_bq': _L0_xattn_in['bq'], 'L0_xattn_Wk': _L0_xattn_in['Wk'], 'L0_xattn_bk': _L0_xattn_in['bk'], 'L0_xattn_Wv': _L0_xattn_in['Wv'], 'L0_xattn_bv': _L0_xattn_in['bv'], 'L0_xattn_Wo': _L0_xattn_in['Wo'], 'L0_xattn_bo': _L0_xattn_in['bo'], 'L0_ffn_Wr': _L0_ffn_in['Wr'], 'L0_ffn_br': _L0_ffn_in['br'], 'L0_ffn_W_up': _L0_ffn_in['W_up'], 'L0_ffn_b_up': _L0_ffn_in['b_up'], 'L0_ffn_W_down': _L0_ffn_in['W_down'], 'L0_ffn_b_down': _L0_ffn_in['b_down'], 'L1_xattn_w_sim': _L1_xattn_in['w_sim'], 'L1_xattn_b_sim': _L1_xattn_in['b_sim'], 'L1_xattn_W_qv': _L1_xattn_in['W_qv'], 'L1_xattn_b_qv': _L1_xattn_in['b_qv'], 'L1_ffn_wg': _L1_ffn_in['wg'], 'L1_ffn_W': _L1_ffn_in['W'], 'L1_ffn_b': _L1_ffn_in['b']}

def reference(x, ctx_1024, mask_BxS2_ik0, g_xattn, g_ffn, L0_xattn_Wq, L0_xattn_bq, L0_xattn_Wk, L0_xattn_bk, L0_xattn_Wv, L0_xattn_bv, L0_xattn_Wo, L0_xattn_bo, L0_ffn_Wr, L0_ffn_br, L0_ffn_W_up, L0_ffn_b_up, L0_ffn_W_down, L0_ffn_b_down, L1_xattn_w_sim, L1_xattn_b_sim, L1_xattn_W_qv, L1_xattn_b_qv, L1_ffn_wg, L1_ffn_W, L1_ffn_b):
    import jax
    import jax.numpy as jnp

    def _L0_xattn_ref(query, key, value, mask, Wq, bq, Wk, bk, Wv, bv, Wo, bo):
        import jax, jax.numpy as jnp
        import numpy as np
        import math
        N_HEADS = 16
        HDIM = 256
        NEG_INF = -1e+20
        B, Qlen, _ = query.shape
        Klen = key.shape[1]
        H = N_HEADS
        dh = HDIM // H
        scale = math.sqrt(dh)

        def heads(x):
            return x.reshape(B, x.shape[1], H, dh).transpose(0, 2, 1, 3)
        q = heads(query @ Wq + bq) / scale
        k = heads(key @ Wk + bk)
        v = heads(value @ Wv + bv)
        scores = jnp.einsum('bhqd,bhkd->bhqk', q, k)
        scores = jnp.where(mask[:, None, None, :] == 0, NEG_INF, scores)
        attn = jax.nn.softmax(scores, axis=-1)
        ctx = jnp.einsum('bhqk,bhkd->bhqd', attn, v)
        ctx = ctx.transpose(0, 2, 1, 3).reshape(B, Qlen, HDIM)
        out = ctx @ Wo + bo
        return jnp.squeeze(out, axis=1) if Qlen == 1 else out

    def _L0_ffn_ref(x, Wr, br, W_up, b_up, W_down, b_down):
        import jax, jax.numpy as jnp
        import numpy as np
        B, S, H = (4, 512, 256)
        E = 8
        GS = 2
        NG = E // GS
        F = int(H * 4 * (2.0 / 3.0))
        b, s, h = x.shape
        n_tok = b * s
        k = n_tok // E
        xf = x.reshape(n_tok, h)
        logits = xf @ Wr + br
        Sm = jax.nn.softmax(logits, axis=-1)
        G_t, idx_t = jax.lax.top_k(Sm.T, k)
        G = G_t.T
        idx = idx_t.T
        tokens = xf[idx]
        group = jnp.arange(E) // GS
        Wu = W_up[group]
        bu = b_up[group]
        mid = jax.nn.silu(jnp.einsum('keh,ehf->kef', tokens, Wu) + bu)
        out = jnp.einsum('kef,efh->keh', mid, W_down) + b_down
        y = jnp.zeros_like(xf).at[idx].add(G[..., None] * out)
        return y.reshape(b, s, h)

    def _L1_xattn_ref(encoder_hc, decoder_hq, w_sim, b_sim, W_qv, b_qv):
        import jax, jax.numpy as jnp
        import numpy as np
        B, L_ENC, L_DEC, D = (16, 128, 128, 256)
        d = encoder_hc.shape[-1]
        w1, w2, w3 = (w_sim[:d], w_sim[d:2 * d], w_sim[2 * d:])
        Sim = (encoder_hc @ w1)[:, :, None] + (decoder_hq @ w2)[:, None, :] + jnp.einsum('bid,bjd->bij', encoder_hc * w3, decoder_hq) + b_sim[0]
        A = jax.nn.softmax(Sim, axis=2)
        hq_hat = jnp.einsum('bij,bjd->bid', A, decoder_hq)
        Batt = jax.nn.softmax(jnp.max(Sim, axis=2), axis=1)
        hc_bar = jnp.einsum('bi,bid->bd', Batt, encoder_hc)[:, None, :]
        hc_hat = jnp.broadcast_to(hc_bar, encoder_hc.shape)
        feats = jnp.concatenate([encoder_hc, hq_hat, encoder_hc * hq_hat, encoder_hc * hc_hat], axis=-1)
        hcq = feats @ W_qv + b_qv
        return hcq

    def _L1_ffn_ref(x, wg, W, b):
        import jax, jax.numpy as jnp
        import numpy as np
        H = 256
        E = 8
        B, S = (4, 512)
        Bb, Ss, Hh = x.shape
        Ee = wg.shape[1]
        T = Bb * Ss
        C = T // Ee
        xt = x.reshape(T, Hh)
        logits = xt @ wg
        probs = jax.nn.softmax(logits, axis=-1)
        idx = jnp.argmax(probs, axis=-1)
        mask = jax.nn.one_hot(idx, Ee, dtype=xt.dtype)
        locations = jnp.cumsum(mask, axis=0) - mask
        mask = mask * (locations < C).astype(xt.dtype)
        gate = jnp.sum(probs * mask, axis=-1)
        loc_s = jnp.sum(locations * mask, axis=-1).astype(jnp.int32)
        loc_oh = jax.nn.one_hot(loc_s, C, dtype=xt.dtype)
        dispatch = mask[:, :, None] * loc_oh[:, None, :]
        combine = gate[:, None, None] * dispatch
        exp_in = jnp.einsum('tec,th->ech', dispatch, xt)
        exp_out = jnp.einsum('ech,efh->ecf', exp_in, W) + b[:, None, :]
        out = jnp.einsum('tec,ecf->tf', combine, exp_out)
        return out.reshape(Bb, Ss, Hh)
    x = x + jnp.tanh(g_xattn[0]) * _L0_xattn_ref(_layernorm(x, axis=-1), ctx_1024, ctx_1024, mask_BxS2_ik0, L0_xattn_Wq, L0_xattn_bq, L0_xattn_Wk, L0_xattn_bk, L0_xattn_Wv, L0_xattn_bv, L0_xattn_Wo, L0_xattn_bo)
    x = x + jnp.tanh(g_ffn[0]) * _L0_ffn_ref(_layernorm(x, axis=-1), L0_ffn_Wr, L0_ffn_br, L0_ffn_W_up, L0_ffn_b_up, L0_ffn_W_down, L0_ffn_b_down)
    x = x + jnp.tanh(g_xattn[1]) * _L1_xattn_ref(_layernorm(x, axis=-1), ctx_1024, L1_xattn_w_sim, L1_xattn_b_sim, L1_xattn_W_qv, L1_xattn_b_qv)
    x = x + jnp.tanh(g_ffn[1]) * _L1_ffn_ref(_layernorm(x, axis=-1), L1_ffn_wg, L1_ffn_W, L1_ffn_b)
    return x

_drawn_inputs = setup_inputs


def setup_inputs(seed=0):
    import zlib

    import numpy as np

    out = dict(_drawn_inputs(seed))
    spreads = {'g_ffn': (-1.0, 0.6),
     'L0_xattn_bq': (0.0, 0.292),
     'L0_xattn_bk': (0.0, 2.0),
     'L0_xattn_bv': (0.0, 0.1),
     'L0_xattn_bo': (0.0, 0.1),
     'L0_ffn_br': (0.0, 0.1)}
    factors = {'L0_ffn_b_up': 32.723, 'L0_ffn_b_down': 8.0, 'L1_xattn_b_qv': 3.224, 'L1_ffn_b': 8.0}
    for name, (base, spread) in spreads.items():
        noise = np.random.default_rng([zlib.crc32(name.encode()), seed]).standard_normal(out[name].shape)
        drawn = base * np.exp(spread * noise) if base else spread * noise
        out[name] = jnp.asarray(drawn.astype(out[name].dtype))
    for name, factor in factors.items():
        out[name] = (out[name] * factor).astype(out[name].dtype)
    return out
```

```python
import numpy as np
import concourse.bass as bass
from concourse import mybir
from contextlib import ExitStack

F32 = mybir.dt.float32
BF16 = mybir.dt.bfloat16
I32 = mybir.dt.int32
ALU = mybir.AluOpType
ACT = mybir.ActivationFunctionType
AX = mybir.AxisListType
REDUCE_MAX = bass.bass_isa.ReduceOp.max

P = 128
BATCHES, SEQ, D = 32, 128, 256
TOKENS = BATCHES * SEQ
QUAD = 4
QT = QUAD * P
QUADS = TOKENS // QT
HALVES = D // P
HEADS, HD = 16, 16
EXPERTS = 8
CAP = TOKENS // EXPERTS
FFN = 682
LN_EPS = 1e-5
MASKED = -4e20


class Semaphores:

    def __init__(self, nc):
        self.nc, self.made = nc, []

    def __enter__(self):
        return self

    def new(self, name):
        self.made.append(self.nc.alloc_semaphore(name))
        return self.made[-1]

    def __exit__(self, *exc):
        if exc[0] is None:
            self.nc.clear_and_free_semaphores(self.made)
            self.nc.all_engine_barrier()


def settle(nc, S, dve, semaphore, value):
    dve.wait_ge(semaphore, value)
    nc.vector.memset(S["spare"][:], 0.0)


def setup(nc, S, T):
    with ExitStack() as ctx:
        sem = ctx.enter_context(Semaphores(nc)).new
        mask_i = ctx.enter_context(nc.sbuf_tensor("mask_i", [BATCHES, SEQ], I32))
        mask_add = ctx.enter_context(nc.sbuf_tensor("mask_add", [BATCHES, SEQ], BF16))
        gates = ctx.enter_context(nc.sbuf_tensor("gates", [P, 4], F32))
        loaded, made, masked, stored, tanhed = (sem(n) for n in
            ("su_loaded", "su_made", "su_masked", "su_stored", "su_tanhed"))
        zeroed, cleared = sem("su_zeroed"), sem("su_cleared")
        block = ctx.enter_context(nc.Block())

        @block.sync
        def _(sp):
            sp.dma_start(mask_i[:], T["mask"]).then_inc(loaded, 16)
            sp.dma_start(gates[:, 0:2], T["g_xattn"].partition_broadcast(P)).then_inc(loaded, 16)
            sp.dma_start(gates[:, 2:4], T["g_ffn"].partition_broadcast(P)).then_inc(loaded, 16)
            sp.wait_ge(masked, 1)
            sp.dma_start(T["mask_row"].rearrange("(b s) -> b s", s=SEQ), mask_add[:]).then_inc(stored, 16)
            sp.wait_ge(zeroed, 1)
            sp.dma_start(T["slots"].rearrange("(t p) d -> p t d", p=P),
                         S["zero"][:].unsqueeze(1).broadcast_to([P, TOKENS // P, D])).then_inc(cleared, 16)
            sp.wait_ge(stored, 16)
            sp.wait_ge(cleared, 16)

        @block.gpsimd
        def _(pool):
            nc.gpsimd.memset(S["zero"][:], 0.0).then_inc(zeroed, 1)
            nc.gpsimd.memset(S["ident"][:], 0.0).then_inc(made, 1)
            nc.gpsimd.memset(S["ident_b"][:], 0.0).then_inc(made, 1)
            nc.gpsimd.memset(S["minus_half"][:], -0.5).then_inc(made, 1)
            nc.gpsimd.memset(S["eps"][:], LN_EPS).then_inc(made, 1)
            pool.wait_ge(made, 4)
            for m in (S["ident"], S["ident_b"]):
                nc.gpsimd.affine_select(out=m[:], in_=m[:], compare_op=ALU.not_equal, fill=1.0, base=0,
                                        pattern=[[-1, P]], channel_multiplier=1).then_inc(made, 1)

        @block.vector
        def _(dve):
            dve.wait_ge(loaded, 48)
            nc.vector.tensor_scalar(mask_add[:], mask_i[:], 0.0, MASKED, ALU.is_equal, ALU.mult).then_inc(masked, 1)

        @block.scalar
        def _(act):
            act.wait_ge(loaded, 48)
            nc.scalar.activation(S["tanh_g"][:], gates[:], ACT.Tanh).then_inc(tanhed, 1)


def project_qkv(nc, S, T):
    with ExitStack() as ctx:
        sb = lambda n, s, d=F32: ctx.enter_context(nc.sbuf_tensor(n, s, d))
        sem = ctx.enter_context(Semaphores(nc)).new
        ident = S["ident"]
        wq, wk, wv = (sb(n, [P, HALVES, D]) for n in ("wq", "wk", "wv"))
        bias_qk = sb("bias_qk", [P, 2, HALVES])
        bias_v = sb("bias_v", [P, 2, D])
        x_in = [sb(f"x_in{i}", [P, QUAD, D]) for i in range(2)]
        c_in = [sb(f"c_in{i}", [P, QUAD, D]) for i in range(2)]
        xn = [sb(f"xn{i}", [P, QUAD, D]) for i in range(2)]
        stats = sb("stats", [P, QUAD, 6])
        moments = sb("moments", [P, QUAD, 2])
        vareps = sb("vareps", [P, QUAD])
        rstd = sb("rstd", [P, QUAD])
        xT = [sb(f"xT{i}", [P, HALVES, QT]) for i in range(2)]
        cT = [sb(f"cT{i}", [P, HALVES, QT]) for i in range(2)]
        parts = [sb(f"parts{i}", [P, 2, HALVES, 2, QT], BF16) for i in range(2)]
        v_out = [sb(f"v_out{i}", [P, QUAD, D]) for i in range(2)]
        banks = [ctx.enter_context(nc.psum_tensor(f"pa{i}", [P, 512], F32)) for i in range(8)]
        ps_x, ps_c, ps_q, ps_k = banks[0:2], banks[2:4], banks[4:6], banks[6:8]
        ps_v = ps_x
        weights = sem("pa_weights")
        x_in_s = [sem(f"pa_x{i}") for i in range(2)]
        c_in_s = [sem(f"pa_c{i}") for i in range(2)]
        stats_s, moments_s, rstd_s, xn_s = (sem(n) for n in ("pa_stats", "pa_moments", "pa_rstd", "pa_xn"))
        vareps_s = sem("pa_vareps")
        xt_ps, ct_ps, q_ps, k_ps, v_ps = (sem(n) for n in ("pa_xt_ps", "pa_ct_ps", "pa_q_ps", "pa_k_ps", "pa_v_ps"))
        xt_s, ct_s, hi_s, lo_s, v_s = (sem(n) for n in ("pa_xt", "pa_ct", "pa_hi", "pa_lo", "pa_v"))
        qk_out = [sem(f"pa_qk_out{i}") for i in range(2)]
        v_outs = [sem(f"pa_v_out{i}") for i in range(2)]
        block = ctx.enter_context(nc.Block())
        x_t = T["x"].rearrange("(t p) d -> p t d", p=P)
        c_t = T["ctx"].rearrange("(t p) d -> p t d", p=P)
        v_t = T["v"].rearrange("(t p) d -> p t d", p=P)

        @block.sync
        def _(sp):
            for i, w in enumerate(("Wq", "Wk", "Wv")):
                sp.dma_start((wq, wk, wv)[i][:], T[w].rearrange("(h p) n -> p h n", p=P)).then_inc(weights, 16)
            for j in range(2):
                sp.dma_start(bias_v[:, j, :], T["bv"].partition_broadcast(P)).then_inc(weights, 16)
                sp.dma_start(bias_qk[:, j, :], T[("bq", "bk")[j]].rearrange("(h p) -> p h", p=P), allow_slow_non_contiguous=True).then_inc(weights, 16)

            def load(q, par, first):
                if not first:
                    sp.wait_ge(ct_ps, q - 1)
                    sp.wait_ge(xt_ps, q - 1)
                sp.dma_start(x_in[par][:], x_t[:, bass.ds(q * QUAD, QUAD), :]).then_inc(x_in_s[par], 16)
                sp.dma_start(c_in[par][:], c_t[:, bass.ds(q * QUAD, QUAD), :]).then_inc(c_in_s[par], 16)

            def store(q, par):
                sp.wait_ge(lo_s, 4 * q + 4)
                for j, name in enumerate(("qparts", "kparts")):
                    for h in range(HALVES):
                        sp.dma_start(T[name][:, h * P:(h + 1) * P, bass.ds(q * QT, QT)].rearrange("s p t -> p s t"),
                                     parts[par][:, j, h]).then_inc(qk_out[par], 16)
                sp.wait_ge(v_s, 2 * q + 2)
                sp.dma_start(v_t[:, bass.ds(q * QUAD, QUAD), :], v_out[par][:]).then_inc(v_outs[par], 16)

            for par in range(2):
                load(par, par, True)
            with sp.Fori(0, QUADS // 2 - 1) as pair:
                for par in range(2):
                    load(pair * 2 + (par + 2), par, False)
                    store(pair * 2 + par, par)
            for par in range(2):
                store(QUADS - 2 + par, par)
            for par in range(2):
                sp.wait_ge(qk_out[par], 64 * QUADS // 2)
                sp.wait_ge(v_outs[par], 16 * QUADS // 2)

        @block.gpsimd
        def _(pool):
            with pool.Fori(0, QUADS) as q:
                pool.wait_ge(moments_s, q + 1)
                nc.gpsimd.tensor_tensor(vareps[:], moments[:, :, 1], S["eps"][:], ALU.add).then_inc(vareps_s, 1)
                pool.wait_ge(vareps_s, q + 1)
                nc.gpsimd.tensor_tensor(rstd[:], vareps[:], S["minus_half"][:, 0:QUAD], ALU.pow).then_inc(rstd_s, 1)

        @block.vector
        def _(dve):
            def norm(q, par, n16, first):
                dve.wait_ge(x_in_s[par], n16)
                if not first:
                    dve.wait_ge(xt_ps, q - 1)
                for t in range(QUAD):
                    nc.vector.bn_stats(stats[:, t, :], x_in[par][:, t, :]).then_inc(stats_s, 1)
                settle(nc, S, dve, stats_s, q * QUAD + QUAD)
                for t in range(QUAD):
                    ins = nc.vector.bn_aggr(moments[:, t, :], stats[:, t, :])
                ins.then_inc(moments_s, 1)
                dve.wait_ge(rstd_s, q + 1)
                dve.wait_ge(moments_s, q + 1)
                for t in range(QUAD):
                    ins = nc.vector.tensor_scalar(xn[par][:, t, :], x_in[par][:, t, :], moments[:, t, 0:1], rstd[:, t:t + 1],
                                                  ALU.subtract, ALU.mult)
                ins.then_inc(xn_s, 1)

            def quad(q, par, first, fresh):
                for h in range(HALVES):
                    dve.wait_ge(ct_ps, q + 1)
                    if not first:
                        dve.wait_ge(k_ps, q)
                    nc.vector.tensor_copy(cT[par][:, h, :], ps_c[h][:]).then_inc(ct_s, 1)
                for h in range(HALVES):
                    dve.wait_ge(hi_s, 4 * q + (h + 1))
                    nc.vector.scalar_tensor_tensor(parts[par][:, 0, h, 1, :], ps_q[h][:], bias_qk[:, 0, h:h + 1],
                                                   parts[par][:, 0, h, 0, :], ALU.add, ALU.subtract).then_inc(lo_s, 1)
                for j in range(2):
                    dve.wait_ge(v_ps, 2 * q + (j + 1))
                    if not fresh:
                        dve.wait_ge(v_outs[par], out16(q, par))
                    nc.vector.tensor_tensor(v_out[par][:, 2 * j:2 * j + 2, :], ps_v[j][:].rearrange("p (a d) -> p a d", a=2),
                                            bias_v[:], ALU.add).then_inc(v_s, 1)
                for h in range(HALVES):
                    dve.wait_ge(hi_s, 4 * q + (h + 3))
                    nc.vector.scalar_tensor_tensor(parts[par][:, 1, h, 1, :], ps_k[h][:], bias_qk[:, 1, h:h + 1],
                                                   parts[par][:, 1, h, 0, :], ALU.add, ALU.subtract).then_inc(lo_s, 1)

            def out16(q, par):
                return (q - par) * 8

            dve.wait_ge(weights, 16 * 7)
            norm(0, 0, 16, True)
            norm(1, 1, 16, True)
            quad(0, 0, True, True)
            norm(2, 0, 32, False)
            quad(1, 1, False, True)
            with dve.Fori(1, QUADS // 2 - 1) as pair:
                norm(pair * 2 + 1, 1, pair * 16 + 16, False)
                quad(pair * 2, 0, False, False)
                norm(pair * 2 + 2, 0, pair * 16 + 32, False)
                quad(pair * 2 + 1, 1, False, False)
            norm(QUADS - 1, 1, 8 * QUADS, False)
            quad(QUADS - 2, 0, False, False)
            quad(QUADS - 1, 1, False, False)

        @block.scalar
        def _(act):
            def quad(q, par, first):
                for h in range(HALVES):
                    act.wait_ge(xt_ps, q + 1)
                    if not first:
                        act.wait_ge(q_ps, q - 1)
                    nc.scalar.activation(xT[par][:, h, :], ps_x[h][:], ACT.Copy).then_inc(xt_s, 1)
                for h in range(HALVES):
                    act.wait_ge(q_ps, q + 1)
                    if not first:
                        act.wait_ge(qk_out[par], (q - par) * 32)
                    nc.scalar.activation(parts[par][:, 0, h, 0, :], ps_q[h][:], ACT.Identity,
                                         bias=bias_qk[:, 0, h:h + 1]).then_inc(hi_s, 1)
                for h in range(HALVES):
                    act.wait_ge(k_ps, q + 1)
                    nc.scalar.activation(parts[par][:, 1, h, 0, :], ps_k[h][:], ACT.Identity,
                                         bias=bias_qk[:, 1, h:h + 1]).then_inc(hi_s, 1)

            act.wait_ge(weights, 16 * 7)
            for par in range(2):
                quad(par, par, True)
            with act.Fori(1, QUADS // 2) as pair:
                for par in range(2):
                    quad(pair * 2 + par, par, False)

        @block.tensor
        def _(pe):
            def quad(q, par, n16, first):
                pe.wait_ge(xn_s, q + 1)
                if not first:
                    pe.wait_ge(v_s, 2 * q)
                for h in range(HALVES):
                    for t in range(QUAD):
                        ins = nc.tensor.transpose(ps_x[h][:, t * P:(t + 1) * P], xn[par][:, t, h * P:(h + 1) * P], ident[:])
                ins.then_inc(xt_ps, 1)
                pe.wait_ge(c_in_s[par], n16)
                if not first:
                    pe.wait_ge(ct_s, 2 * q)
                for h in range(HALVES):
                    for t in range(QUAD):
                        ins = nc.tensor.transpose(ps_c[h][:, t * P:(t + 1) * P], c_in[par][:, t, h * P:(h + 1) * P], ident[:])
                ins.then_inc(ct_ps, 1)
                pe.wait_ge(xt_s, 2 * q + 2)
                if not first:
                    pe.wait_ge(lo_s, 4 * q)
                for m in range(HALVES):
                    for h in range(HALVES):
                        ins = nc.tensor.matmul(ps_q[m][:], wq[:, h, m * P:(m + 1) * P], xT[par][:, h, :],
                                               start=(h == 0), stop=(h == HALVES - 1))
                ins.then_inc(q_ps, 1)
                pe.wait_ge(ct_s, 2 * q + 2)
                for t in range(QUAD):
                    for h in range(HALVES):
                        ins = nc.tensor.matmul(ps_v[t // 2][:, (t % 2) * D:(t % 2 + 1) * D], cT[par][:, h, t * P:(t + 1) * P],
                                               wv[:, h, :], start=(h == 0), stop=(h == HALVES - 1))
                    if t % 2:
                        ins.then_inc(v_ps, 1)
                for m in range(HALVES):
                    for h in range(HALVES):
                        ins = nc.tensor.matmul(ps_k[m][:], wk[:, h, m * P:(m + 1) * P], cT[par][:, h, :],
                                               start=(h == 0), stop=(h == HALVES - 1))
                ins.then_inc(k_ps, 1)

            pe.wait_ge(weights, 16 * 7)
            for par in range(2):
                quad(par, par, 16, par == 0)
            with pe.Fori(1, QUADS // 2) as pair:
                for par in range(2):
                    quad(pair * 2 + par, par, pair * 16 + 16, False)


TILES = TOKENS // P
STACK = 3 * HD + 1
SLOTW = 32


class Step:

    def __init__(self, base, k):
        self.base, self.k = base, k

    def plus(self, d):
        return Step(self.base, self.k + d)

    def count(self, per, extra):
        return self.base * (4 * per) + (self.k * per + extra)

    def dma(self, slots, per=1):
        return self.base * (4 // slots * 16 * per) + 16 * per * (self.k // slots + 1)

    def exists(self):
        return not isinstance(self.base, int) or 0 <= self.base * 4 + self.k < TILES

    def tile(self):
        return self.base * 4 + self.k


def wait(engine, semaphore, value):
    if not isinstance(value, int) or value > 0:
        engine.wait_ge(semaphore, value)


def steps(engine, emit, tail):
    for k in range(4):
        emit(Step(0, k))
    with engine.Fori(1, TILES // 4 - 1) as base:
        for k in range(4):
            emit(Step(base, k))
    for k in range(4 + tail):
        emit(Step(TILES // 4 - 1, k))


def attention(nc, S, T):
    with ExitStack() as ctx:
        sb = lambda n, s, d=F32: ctx.enter_context(nc.sbuf_tensor(n, s, d))
        sem = ctx.enter_context(Semaphores(nc)).new
        ident, ident_b = S["ident"], S["ident_b"]
        wo, wr = sb("wo", [P, HALVES, D]), sb("wr", [P, HALVES, EXPERTS])
        bo = sb("bo", [P, D])
        br = sb("br", [EXPERTS, 1])
        pick = sb("pick", [2 * HEADS, HEADS, P], BF16)
        qs = [sb(f"qs{i}", [64, HEADS, 2 * P], BF16) for i in range(2)]
        ks = [sb(f"ks{i}", [64, HEADS, 2 * P], BF16) for i in range(2)]
        v_in = [sb(f"v_in{i}", [P, D]) for i in range(2)]
        v_wide = [sb(f"v_wide{i}", [P, HEADS, SLOTW]) for i in range(2)]
        x_res = [sb(f"x_res{i}", [P, D]) for i in range(2)]
        neg_max = sb("neg_max", [P, HEADS])
        nm_parts = sb("nm_parts", [P, 2, HEADS], BF16)
        nmT = sb("nmT", [2 * HEADS, P], BF16)
        probs = [sb(f"probs{i}", [P, 4, P]) for i in range(2)]
        ctxT = sb("ctxT", [P, 4 * P])
        inv_sum = sb("inv_sum", [P, HEADS])
        attn = sb("attn", [P, D])
        attnT = sb("attnT", [P, HALVES, P])
        x1 = [sb(f"x1_{i}", [P, D]) for i in range(2)]
        stats, moments = sb("b_stats", [P, 6]), [sb(f"b_moments{i}", [P, 2]) for i in range(2)]
        vareps, rstd = sb("b_vareps", [P, 1]), sb("b_rstd", [P, 1])
        xn = [sb(f"b_xn{i}", [P, D]) for i in range(2)]
        xnT = sb("b_xnT", [P, HALVES, P])
        ps = [ctx.enter_context(nc.psum_tensor(f"pb{i}", [P, 512], F32)) for i in range(6)]
        ps_s, ps_st, ps_ctx, ps_ctxT = ps[0:2], ps[2:4], ps[4], ps[5]
        ps6 = ctx.enter_context(nc.psum_tensor("pb6", [P, 512], F32))
        ps7 = ctx.enter_context(nc.psum_tensor("pb7", [P, 512], F32))
        ps_aT, ps_nmT = ps6[:, 0:D], ps6[0:2 * HEADS, D:D + P // 2].bitcast(BF16)
        ps_o, ps_xnT = ps7[:, 0:D], ps7[:, D:2 * D]
        ps_lg = ps_ctxT[0:EXPERTS, 0:P]
        w_s, thbo_s, pick_s, ones_s = sem("pb_w"), sem("pb_thbo"), sem("pb_pick"), sem("pb_ones")
        q_in = [sem(f"pb_q{i}") for i in range(2)]
        k_in = [sem(f"pb_k{i}") for i in range(2)]
        v_in_s = [sem(f"pb_vin{i}") for i in range(2)]
        x_in_s = [sem(f"pb_xin{i}") for i in range(2)]
        x1_out = [sem(f"pb_x1out{i}") for i in range(2)]
        xn_out = [sem(f"pb_xnout{i}") for i in range(2)]
        (s_ps, max_s, nm_hi_s, nm_s, nmT_ps, nmT_s, st_ps, exp_s, ctx_ps, ctxT_s, ctxT_ps, inv_s, attn_s, aT_ps, aT_s,
         o_ps, x1_s, stats_s, mom_s, ve_s, rstd_s, xn_s, xnT_ps, xnT_s, lg_ps, lg_s, vw_s, xb_s) = (
            sem("pb_" + n) for n in (
                "s_ps", "max", "nm_hi", "nm", "nmT_ps", "nmT", "st_ps", "exp", "ctx_ps", "ctxT", "ctxT_ps", "inv",
                "attn", "aT_ps", "aT", "o_ps", "x1", "stats", "mom", "ve", "rstd", "xn", "xnT_ps", "xnT", "lg_ps", "lg",
                "vw", "xb"))
        av_s = sem("pb_av")
        block = ctx.enter_context(nc.Block())
        v_t = T["v"].rearrange("(t p) d -> p t d", p=P)
        x_t = T["x"].rearrange("(t p) d -> p t d", p=P)
        x1_t = T["resid"].rearrange("(t p) d -> p t d", p=P)
        xn_t = T["rows0"].rearrange("(t p) d -> p t d", p=P)

        @block.sync
        def _(sp):
            sp.dma_start(wo[:], T["Wo"].rearrange("(h p) n -> p h n", p=P)).then_inc(w_s, 16)
            sp.dma_start(wr[:], T["Wr"].rearrange("(h p) n -> p h n", p=P)).then_inc(w_s, 16)
            sp.dma_start(bo[:], T["bo"].partition_broadcast(P)).then_inc(w_s, 16)
            sp.dma_start(br[:], T["br"].rearrange("(e a) -> e a", a=1)).then_inc(w_s, 16)
            sp.wait_ge(ones_s, 2)

            def load_stacks(s):
                slot = s.k // 2 % 2
                wait(sp, st_ps, s.count(4, -8))
                toks = bass.ds(s.tile() * P, 2 * P)
                for i, part in enumerate((0, 1, 0)):
                    sp.dma_start(qs[slot][i * HD:(i + 1) * HD, :, :],
                                 T["qparts"][part, :, toks].rearrange("(h r) t -> r h t", r=HD)).then_inc(q_in[slot], 16)
                for i, part in enumerate((0, 0, 1)):
                    sp.dma_start(ks[slot][i * HD:(i + 1) * HD, :, :],
                                 T["kparts"][part, :, toks].rearrange("(h r) t -> r h t", r=HD)).then_inc(k_in[slot], 16)
                sp.dma_start(ks[slot][3 * HD:STACK, :, :],
                             T["mask_row"][toks].unsqueeze(0).unsqueeze(0).broadcast_to([1, HEADS, 2 * P])
                             ).then_inc(k_in[slot], 16)

            def load_tiles(s):
                slot = s.k % 2
                wait(sp, vw_s, s.count(1, -1))
                sp.dma_start(v_in[slot][:], v_t[:, bass.ds(s.tile(), 1), :].rearrange("p a d -> p (a d)")).then_inc(v_in_s[slot], 16)
                wait(sp, x1_s, s.count(1, -1))
                sp.dma_start(x_res[slot][:], x_t[:, bass.ds(s.tile(), 1), :].rearrange("p a d -> p (a d)")).then_inc(x_in_s[slot], 16)

            def emit(s):
                if s.k % 2 == 0 and s.plus(2).exists():
                    load_stacks(s.plus(2))
                if s.plus(1).exists():
                    load_tiles(s.plus(1))
                if s.plus(-1).exists():
                    sp.wait_ge(x1_s, s.count(1, 0))
                    sp.dma_start(x1_t[:, bass.ds(s.plus(-1).tile(), 1), :].rearrange("p a d -> p (a d)"),
                                 x1[(s.k - 1) % 2][:]).then_inc(x1_out[(s.k - 1) % 2], 16)
                if s.plus(-2).exists():
                    sp.wait_ge(xn_s, s.count(1, -1))
                    sp.dma_start(xn_t[:, bass.ds(s.plus(-2).tile(), 1), 0:D].rearrange("p a d -> p (a d)"),
                                 xn[s.k % 2][:]).then_inc(xn_out[s.k % 2], 16)

            load_stacks(Step(0, 0))
            load_tiles(Step(0, 0))
            steps(sp, emit, 2)
            for i in range(2):
                sp.wait_ge(x1_out[i], 16 * TILES // 2)
                sp.wait_ge(xn_out[i], 16 * TILES // 2)

        @block.gpsimd
        def _(pool):
            nc.gpsimd.memset(pick[:], 0.0).then_inc(pick_s, 1)
            for t in range(2):
                nc.gpsimd.memset(v_wide[t][:], 1.0).then_inc(pick_s, 1)
            pool.wait_ge(w_s, 64)
            nc.gpsimd.tensor_scalar(bo[:], bo[:], S["tanh_g"][:, 0:1], None, ALU.mult).then_inc(thbo_s, 1)
            for r in range(2):
                pool.wait_ge(pick_s, 3 + r)
                nc.gpsimd.affine_select(out=pick[:], in_=pick[:], compare_op=ALU.not_equal, fill=1.0, base=-HEADS * r,
                                        pattern=[[-1, HEADS], [0, P]], channel_multiplier=1).then_inc(pick_s, 1)
            pool.wait_ge(thbo_s, 1)

            def widen(s):
                slot = s.k % 2
                pool.wait_ge(v_in_s[slot], s.dma(2))
                wait(pool, ctx_ps, s.count(1, -1))
                nc.gpsimd.tensor_tensor(v_wide[slot][:, :, 0:HD], v_in[slot][:].rearrange("p (h d) -> p h d", h=HEADS),
                                        S["zero"][:].rearrange("p (h d) -> p h d", h=HEADS), ALU.add).then_inc(vw_s, 1)

            def emit(s):
                if s.plus(1).exists():
                    widen(s.plus(1))
                if s.exists():
                    slot = s.k % 2
                    pool.wait_ge(x_in_s[slot], s.dma(2))
                    nc.gpsimd.tensor_tensor(x_res[slot][:], x_res[slot][:], bo[:], ALU.add).then_inc(xb_s, 1)
                if s.plus(-1).exists():
                    pool.wait_ge(mom_s, s.count(1, 0))
                    nc.gpsimd.tensor_tensor(vareps[:], moments[(s.k - 1) % 2][:, 1:2], S["eps"][:, 0:1], ALU.add).then_inc(ve_s, 1)
                    pool.wait_ge(ve_s, s.count(1, 0))
                    wait(pool, xn_s, s.count(1, -1))
                    nc.gpsimd.tensor_tensor(rstd[:], vareps[:], S["minus_half"][:, 0:1], ALU.pow).then_inc(rstd_s, 1)

            widen(Step(0, 0))
            steps(pool, emit, 1)

        @block.vector
        def _(dve):
            def row_max(s, g):
                dve.wait_ge(s_ps, s.count(4, g + 1))
                wait(dve, nm_s, s.count(1, 0))
                nc.vector.tensor_reduce(neg_max[:, 4 * g:4 * g + 4], ps_s[g % 2][:].rearrange("p (h k) -> p h k", h=4),
                                        AX.X, ALU.max, negate=True).then_inc(max_s, 1)

            def split_max(s):
                dve.wait_ge(max_s, s.count(4, 4))
                wait(dve, nmT_ps, s.count(1, 0))
                nc.vector.tensor_copy(nm_parts[:, 0, :], neg_max[:]).then_inc(nm_hi_s, 1)
                dve.wait_ge(nm_hi_s, s.count(1, 1))
                nc.vector.tensor_tensor(nm_parts[:, 1, :], neg_max[:], nm_parts[:, 0, :], ALU.subtract).then_inc(nm_s, 1)

            def max_out(s):
                dve.wait_ge(nmT_ps, s.count(1, 1))
                wait(dve, st_ps, s.count(4, 0))
                nc.vector.tensor_copy(nmT[:], ps_nmT).then_inc(nmT_s, 1)

            def normalise(s):
                heads = ps_ctxT[:].rearrange("p (h c) -> p h c", h=HEADS)
                dve.wait_ge(ctxT_ps, s.count(1, 1))
                nc.vector.reciprocal(inv_sum[:], heads[:, :, HD]).then_inc(inv_s, 1)
                dve.wait_ge(inv_s, s.count(1, 1))
                wait(dve, aT_ps, s.count(1, 0))
                nc.vector.tensor_tensor(attn[:].rearrange("p (h d) -> p h d", h=HEADS), heads[:, :, 0:HD],
                                        inv_sum[:].unsqueeze(2).broadcast_to([P, HEADS, HD]), ALU.mult).then_inc(attn_s, 1)

            def residual(s):
                slot = s.k % 2
                dve.wait_ge(o_ps, s.count(1, 1))
                dve.wait_ge(xb_s, s.count(1, 1))
                if s.plus(-2).exists():
                    dve.wait_ge(x1_out[slot], s.plus(-2).dma(2))
                nc.vector.scalar_tensor_tensor(x1[slot][:], ps_o, S["tanh_g"][:, 0:1], x_res[slot][:],
                                               ALU.mult, ALU.add).then_inc(x1_s, 1)
                dve.wait_ge(x1_s, s.count(1, 1))
                nc.vector.bn_stats(stats[:], x1[slot][:]).then_inc(stats_s, 1)
                settle(nc, S, dve, stats_s, s.count(1, 1))
                nc.vector.bn_aggr(moments[slot][:], stats[:]).then_inc(mom_s, 1)

            def norm(s):
                slot = s.k % 2
                dve.wait_ge(rstd_s, s.count(1, 1))
                wait(dve, xnT_ps, s.count(1, -1))
                if s.plus(-2).exists():
                    dve.wait_ge(xn_out[slot], s.plus(-2).dma(2))
                nc.vector.tensor_scalar(xn[slot][:], x1[slot][:], moments[slot][:, 0:1], rstd[:],
                                        ALU.subtract, ALU.mult).then_inc(xn_s, 1)

            def emit(s):
                if s.plus(1).exists():
                    row_max(s.plus(1), 0)
                    row_max(s.plus(1), 1)
                if s.plus(-2).exists():
                    norm(s.plus(-2))
                if s.plus(1).exists():
                    row_max(s.plus(1), 2)
                    row_max(s.plus(1), 3)
                    split_max(s.plus(1))
                if s.plus(-1).exists():
                    normalise(s.plus(-1))
                    residual(s.plus(-1))
                if s.plus(1).exists():
                    max_out(s.plus(1))

            for t in qs:
                nc.vector.memset(t[32:64, :, :], 1.0).then_inc(ones_s, 1)
            for g in range(4):
                row_max(Step(0, 0), g)
            split_max(Step(0, 0))
            max_out(Step(0, 0))
            steps(dve, emit, 2)

        @block.scalar
        def _(act):
            act.wait_ge(w_s, 64)

            def emit(s):
                if s.plus(-1).exists():
                    act.wait_ge(ctx_ps, s.count(1, 0))
                    wait(act, ctxT_ps, s.count(1, -1))
                    nc.scalar.activation(ctxT[:], ps_ctx[:], ACT.Copy).then_inc(ctxT_s, 1)
                if s.exists():
                    for g in range(4):
                        act.wait_ge(st_ps, s.count(4, g + 1))
                        if g < 2:
                            wait(act, ctx_ps, s.count(1, 0))
                        else:
                            act.wait_ge(av_s, s.count(3, g - 1))
                        nc.scalar.activation(probs[g % 2][:], ps_st[g % 2][:].rearrange("p (h q) -> p h q", h=4),
                                             ACT.Exp, scale=1.0 / HD ** 0.5).then_inc(exp_s, 1)
                if s.plus(-2).exists():
                    act.wait_ge(xnT_ps, s.count(1, -1))
                    wait(act, lg_ps, s.count(1, -2))
                    nc.scalar.activation(xnT[:], ps_xnT.rearrange("p (h t) -> p h t", h=HALVES), ACT.Copy).then_inc(xnT_s, 1)
                if s.plus(-1).exists():
                    act.wait_ge(aT_ps, s.count(1, 0))
                    wait(act, o_ps, s.count(1, -1))
                    nc.scalar.activation(attnT[:], ps_aT.rearrange("p (h t) -> p h t", h=HALVES), ACT.Copy).then_inc(aT_s, 1)
                if s.plus(-2).exists():
                    act.wait_ge(lg_ps, s.count(1, -1))
                    nc.scalar.activation(S["logitsT"][:, bass.ds(s.plus(-2).tile() * P, P)], ps_lg, ACT.Identity,
                                         bias=br[:]).then_inc(lg_s, 1)

            steps(act, emit, 2)

        @block.tensor
        def _(pe):
            pe.wait_ge(w_s, 64)
            pe.wait_ge(pick_s, 5)

            def operand(t, s, h, rows):
                return t[s.k // 2 % 2][0:rows, h, s.k % 2 * P:(s.k % 2 + 1) * P]

            def scores(s, g):
                if g == 0 and s.k % 2 == 0:
                    pe.wait_ge(q_in[s.k // 2 % 2], s.dma(4, 3))
                    pe.wait_ge(k_in[s.k // 2 % 2], s.dma(4, 4))
                wait(pe, max_s, s.count(4, g - 1))
                for j in range(4):
                    ins = nc.tensor.matmul(ps_s[g % 2][:, j * P:(j + 1) * P], operand(qs, s, 4 * g + j, STACK),
                                           operand(ks, s, 4 * g + j, STACK), start=True, stop=True)
                ins.then_inc(s_ps, 1)

            def shifted(s, g):
                if g == 0:
                    pe.wait_ge(nmT_s, s.count(1, 1))
                wait(pe, exp_s, s.count(4, g - 1))
                for j in range(4):
                    out = ps_st[g % 2][:, j * P:(j + 1) * P]
                    nc.tensor.matmul(out, operand(ks, s, 4 * g + j, STACK), operand(qs, s, 4 * g + j, STACK), start=True, stop=False)
                    ins = nc.tensor.matmul(out, pick[:, 4 * g + j, :], nmT[:], start=False, stop=True)
                ins.then_inc(st_ps, 1)

            def context(s, g):
                pe.wait_ge(exp_s, s.count(4, g + 1))
                if g == 0:
                    pe.wait_ge(vw_s, s.count(1, 1))
                    wait(pe, ctxT_s, s.count(1, 0))
                for j in range(4):
                    ins = nc.tensor.matmul(ps_ctx[32 * j:32 * j + SLOTW, g * P:(g + 1) * P], v_wide[s.k % 2][:, 4 * g + j, :],
                                           probs[g % 2][:, j, :], start=True, stop=True)
                ins.then_inc(av_s if g < 3 else ctx_ps, 1)

            def emit(s):
                one = s.plus(1).exists()
                if s.exists():
                    shifted(s, 0)
                    if one:
                        scores(s.plus(1), 0)
                        scores(s.plus(1), 1)
                    shifted(s, 1)
                    context(s, 0)
                    shifted(s, 2)
                    if one:
                        scores(s.plus(1), 2)
                    context(s, 1)
                    shifted(s, 3)
                    if one:
                        scores(s.plus(1), 3)
                    context(s, 2)
                if s.plus(-1).exists():
                    pe.wait_ge(ctxT_s, s.count(1, 0))
                    wait(pe, lg_s, s.count(1, -2))
                    for g in range(4):
                        ins = nc.tensor.transpose(ps_ctxT[:, g * P:(g + 1) * P], ctxT[:, g * P:(g + 1) * P], ident[:])
                    ins.then_inc(ctxT_ps, 1)
                if s.plus(-2).exists():
                    pe.wait_ge(xn_s, s.count(1, -1))
                    wait(pe, x1_s, s.count(1, -1))
                    for h in range(HALVES):
                        ins = nc.tensor.transpose(ps_xnT[:, h * P:(h + 1) * P], xn[s.k % 2][:, h * P:(h + 1) * P], ident[:])
                    ins.then_inc(xnT_ps, 1)
                if s.exists():
                    context(s, 3)
                if s.plus(-1).exists():
                    pe.wait_ge(attn_s, s.count(1, 0))
                    wait(pe, nmT_s, min_tile(s.count(1, 1)))
                    for h in range(HALVES):
                        ins = nc.tensor.transpose(ps_aT[:, h * P:(h + 1) * P], attn[:, h * P:(h + 1) * P], ident[:])
                    ins.then_inc(aT_ps, 1)
                if s.plus(-2).exists():
                    pe.wait_ge(xnT_s, s.count(1, -1))
                    for h in range(HALVES):
                        ins = nc.tensor.matmul(ps_lg, wr[:, h, :], xnT[:, h, :], start=(h == 0), stop=(h == HALVES - 1))
                    ins.then_inc(lg_ps, 1)
                if s.plus(-1).exists():
                    pe.wait_ge(aT_s, s.count(1, 0))
                    if s.plus(-2).exists():
                        pe.wait_ge(xnT_s, s.count(1, -1))
                    for h in range(HALVES):
                        ins = nc.tensor.matmul(ps_o, attnT[:, h, :], wo[:, h, :], start=(h == 0), stop=(h == HALVES - 1))
                    ins.then_inc(o_ps, 1)
                if one:
                    max_T(s.plus(1))

            def min_tile(v):
                return min(v, TILES) if isinstance(v, int) else v

            def max_T(s):
                pe.wait_ge(nm_s, s.count(1, 1))
                wait(pe, aT_s, s.count(1, -1))
                nc.tensor.transpose(ps_nmT, nm_parts[:].rearrange("p a h -> p (a h)"), ident_b[:]).then_inc(nmT_ps, 1)

            for g in range(4):
                scores(Step(0, 0), g)
            max_T(Step(0, 0))
            steps(pe, emit, 2)


ROW0 = D + EXPERTS
KEY_BITS = 30
SEG = P // EXPERTS
TOK_T = TOKENS // P


def running_count(nc, mask, tri, ones, ps):
    nc.tensor.matmul(ps[:, 0:EXPERTS * TOK_T], tri[:], mask, start=True, stop=True)
    return nc.tensor.matmul(ps[:, EXPERTS * TOK_T:], ones[:], mask, start=True, stop=True)


def route_top_k(nc, S, T):
    E, TT, N = EXPERTS, TOK_T, EXPERTS * TOK_T
    with ExitStack() as ctx:
        sb = lambda n, s, d=F32: ctx.enter_context(nc.sbuf_tensor(n, s, d))
        sem = ctx.enter_context(Semaphores(nc)).new
        score = S["score"]
        s_et = score[:].rearrange("p t e -> p e t")
        tmax, tsum = sb("tmax", [P, TT]), sb("tsum", [P, TT])
        ex = sb("ex", [P, TT, E])
        keys = sb("keys", [P, 2 * P])
        junk = sb("junk", [P, 2 * P], BF16)
        diff_i = sb("diff_i", [P, P], I32)
        same = sb("same", [P, P], BF16)
        shift_i, one_i, bit_i = (sb(n, [P, KEY_BITS], I32) for n in ("shift_i", "one_i", "bit_i"))
        bit_f = sb("bit_f", [P, KEY_BITS])
        thr, cand, step = (sb(n, [P, 1], I32) for n in ("thr", "cand", "step"))
        count = sb("count", [P, 1], BF16)
        count_f = sb("count_f", [P, 1])
        thr_row = sb("thr_row", [E, P])
        thr_b = sb("thr_b", [P, E])
        above, equal, chosen, early = (sb(n, [P, E, TT], BF16) for n in ("above", "equal", "chosen", "early"))
        scan = sb("scan", [P, E, TT])
        rank = sb("rank", [P, E, TT])
        n_above = sb("n_above", [P, E])
        pos_i, dig_i = sb("pos_i", [P, E, TT], I32), sb("dig_i", [P, 2, E, TT], I32)
        dig = sb("dig", [P, 2, E, TT], BF16)
        ramp_i, ramp = sb("ramp_i", [P, 32], I32), sb("ramp", [P, 32], BF16)
        tile_i, tile_no = sb("tile_i", [P, TT, 16], I32), sb("tile_no", [P, TT, 16], BF16)
        part_i, part_no = sb("part_i", [P, 1], I32), sb("part_no", [P, 1])
        hot_a = [sb(f"hot_a{i}", [P, TT, 32], BF16) for i in range(2)]
        hot_b = [sb(f"hot_b{i}", [P, TT, 16], BF16) for i in range(2)]
        hot_v = [sb(f"hot_v{i}", [P, TT, 2, 16], BF16) for i in range(2)]
        idx_f = sb("idx_f", [32, E, 2, 16])
        idx_i = sb("idx_i", [32, E, 16], I32)
        ps = [ctx.enter_context(nc.psum_tensor(f"pc{i}", [P, 512], F32)) for i in range(6)]
        ps_l, ps_k, ps_n, ps_t, ps_c, ps_i = ps
        (lg_s, mx_s, sub_s, ex_s, sum_s, rec_s, sc_s, keyT_s, key_s, iota_s, tab_s, bit_s, thr0_s, cand_s, cnt_s, cntb_s, tot_s,
         step_s, thr_s, row_s, thrT_s, thrb_s, cmp_s, cnt1_s, red_s, scan_s, off_s, rank_s, early_s, mix_s, ch_s, cnt2_s, pos_s,
         posi_s, dg_s, dgb_s, hot_s, hotb_s, hotv_s, hott_s, idx_ps, idxf_s, idxi_s, out_s, in_s) = (
            sem("pc_" + n) for n in (
                "lg", "mx", "sub", "ex", "sum", "rec", "sc", "keyT", "key", "iota", "tab", "bit", "thr0", "cand", "cnt", "cntb",
                "tot", "step", "thr", "row", "thrT", "thrb", "cmp", "cnt1", "red", "scan", "off", "rank", "early", "mix",
                "ch", "cnt2", "pos", "posi", "dg", "dgb", "hot", "hotb", "hotv", "hott", "idx_ps", "idxf", "idxi", "out", "in"))
        block = ctx.enter_context(nc.Block())

        @block.sync
        def _(sp):
            sp.wait_ge(sc_s, 1)
            sp.dma_start(T["rows0"].rearrange("(t p) d -> p t d", p=P)[:, :, D:ROW0], score[:]).then_inc(out_s, 16)
            sp.wait_ge(out_s, 16)
            sp.wait_ge(idxi_s, 1)
            sp.dma_start(T["idx"].rearrange("(e a b) -> a e b", e=E, a=32), idx_i[:]).then_inc(in_s, 16)
            sp.wait_ge(in_s, 16)
            sp.dma_start(S["idx"][:], T["idx"].rearrange("(e p c) -> p e c", e=E, p=P)).then_inc(in_s, 16)
            sp.wait_ge(in_s, 32)

        @block.gpsimd
        def _(pool):
            nc.gpsimd.iota(diff_i[:], [[-1, P]], base=P, channel_multiplier=1).then_inc(iota_s, 1)
            nc.gpsimd.iota(shift_i[:], [[-1, KEY_BITS]], base=KEY_BITS - 1, channel_multiplier=0).then_inc(iota_s, 1)
            nc.gpsimd.iota(one_i[:], [[0, KEY_BITS]], base=1, channel_multiplier=0).then_inc(iota_s, 1)
            nc.gpsimd.iota(ramp_i[:], [[1, 32]], base=0, channel_multiplier=0).then_inc(iota_s, 1)
            nc.gpsimd.iota(tile_i[:], [[1, TT], [0, 16]], base=0, channel_multiplier=0).then_inc(iota_s, 1)
            nc.gpsimd.iota(part_i[:], [[0, 1]], base=0, channel_multiplier=1).then_inc(iota_s, 1)
            nc.gpsimd.memset(S["ones_b"][:], 1.0).then_inc(tab_s, 1)
            nc.gpsimd.memset(S["before"][:], 1.0).then_inc(tab_s, 1)
            nc.gpsimd.memset(S["keep"][:], 1.0).then_inc(tab_s, 1)
            pool.wait_ge(tab_s, 3)
            nc.gpsimd.affine_select(out=S["before"][:], in_=S["before"][:], compare_op=ALU.is_gt, fill=0.0, base=0,
                                    pattern=[[1, P]], channel_multiplier=-1).then_inc(tab_s, 1)
            nc.gpsimd.affine_select(out=S["keep"][:], in_=S["keep"][:], compare_op=ALU.is_gt, fill=0.0, base=0,
                                    pattern=[[0, E], [1, TT]], channel_multiplier=0).then_inc(tab_s, 1)
            for e in range(E):
                pool.wait_ge(hotb_s, e + 1)
                if e >= 2:
                    pool.wait_ge(idx_ps, e - 1)
                nc.gpsimd.tensor_tensor(hot_v[e % 2][:, :, 1, :], hot_b[e % 2][:], tile_no[:], ALU.mult).then_inc(hott_s, 1)

        @block.scalar
        def _(act):
            act.wait_ge(sub_s, 1)
            nc.scalar.activation(ex[:], ex[:], ACT.Exp).then_inc(ex_s, 1)
            act.wait_ge(keyT_s, 1)
            nc.scalar.activation(keys[:], ps_k[:, 0:2 * P], ACT.Copy).then_inc(key_s, 1)

        @block.vector
        def _(dve):
            V = nc.vector
            dve.wait_ge(iota_s, 6)
            V.tensor_scalar(diff_i[:], diff_i[:], E - 1, None, ALU.bitwise_and).then_inc(bit_s, 1)
            V.tensor_tensor(bit_i[:], one_i[:], shift_i[:], ALU.logical_shift_left).then_inc(bit_s, 1)
            dve.wait_ge(bit_s, 2)
            V.tensor_scalar(same[:], diff_i[:], 0.0, None, ALU.is_equal).then_inc(bit_s, 1)
            V.tensor_copy(bit_f[:], bit_i[:]).then_inc(bit_s, 1)
            V.tensor_copy(ramp[:], ramp_i[:]).then_inc(bit_s, 1)
            V.tensor_copy(tile_no[:], tile_i[:]).then_inc(bit_s, 1)
            V.tensor_copy(part_no[:], part_i[:]).then_inc(bit_s, 1)
            V.memset(thr[:], 0).then_inc(bit_s, 1)
            dve.wait_ge(lg_s, 1)
            lg = ps_l[:, 0:N].rearrange("p (t e) -> p t e", e=E)
            V.tensor_reduce(tmax[:], lg, AX.X, ALU.max).then_inc(mx_s, 1)
            dve.wait_ge(mx_s, 1)
            V.tensor_tensor(ex[:], lg, tmax[:].unsqueeze(2).broadcast_to([P, TT, E]), ALU.subtract).then_inc(sub_s, 1)
            dve.wait_ge(ex_s, 1)
            V.tensor_reduce(tsum[:], ex[:], AX.X, ALU.add).then_inc(sum_s, 1)
            dve.wait_ge(sum_s, 1)
            V.reciprocal(tsum[:], tsum[:]).then_inc(rec_s, 1)
            dve.wait_ge(rec_s, 1)
            V.tensor_tensor(score[:], ex[:], tsum[:].unsqueeze(2).broadcast_to([P, TT, E]), ALU.mult).then_inc(sc_s, 1)

            dve.wait_ge(key_s, 1)
            dve.wait_ge(bit_s, 8)
            with dve.Fori(0, KEY_BITS) as i:
                bit = bass.ds(i, 1)
                V.tensor_tensor(cand[:], thr[:], bit_i[:, bit], ALU.bitwise_or).then_inc(cand_s, 1)
                dve.wait_ge(cand_s, i + 1)
                V.tensor_scalar(junk[:], keys[:], cand[:].bitcast(F32), None, ALU.is_ge, ALU.add,
                                accum_out=count_f[:]).then_inc(cnt_s, 1)
                dve.wait_ge(cnt_s, i + 1)
                V.tensor_copy(count[:], count_f[:]).then_inc(cntb_s, 1)
                dve.wait_ge(tot_s, i + 1)
                V.tensor_scalar(step[:], ps_n[:, 0:1], CAP - 0.5, bit_f[:, bit], ALU.is_ge, ALU.mult).then_inc(step_s, 1)
                dve.wait_ge(step_s, i + 1)
                V.tensor_tensor(thr[:], thr[:], step[:], ALU.bitwise_or).then_inc(thr_s, 1)
                dve.wait_ge(thr_s, i + 1)

            V.tensor_copy(thr_row[:], thr[0:E, :].bitcast(F32).broadcast_to([E, P])).then_inc(row_s, 1)
            dve.wait_ge(thrT_s, 1)
            V.tensor_copy(thr_b[:], ps_t[:, 0:E]).then_inc(thrb_s, 1)
            dve.wait_ge(thrb_s, 1)
            thr_et = thr_b[:].unsqueeze(2).broadcast_to([P, E, TT])
            V.tensor_tensor(above[:], s_et, thr_et, ALU.is_gt).then_inc(cmp_s, 1)
            V.tensor_tensor(equal[:], s_et, thr_et, ALU.is_equal).then_inc(cmp_s, 1)

            def ranks(ps_c, done):
                tot = ps_c[:, N:]
                V.tensor_tensor_scan(scan[:].rearrange("p e t -> p (e t)"), S["keep"][:].rearrange("p e t -> p (e t)"), tot, 0.0,
                                     ALU.mult, ALU.add).then_inc(scan_s, 1)
                dve.wait_ge(scan_s, done + 1)
                V.tensor_tensor(scan[:], scan[:], tot.rearrange("p (e t) -> p e t", e=E), ALU.subtract).then_inc(off_s, 1)
                dve.wait_ge(off_s, done + 1)
                V.tensor_tensor(rank[:], scan[:], ps_c[:, 0:N].rearrange("p (e t) -> p e t", e=E), ALU.add).then_inc(rank_s, 1)
                dve.wait_ge(rank_s, done + 1)

            dve.wait_ge(cnt1_s, 1)
            dve.wait_ge(tab_s, 5)
            V.tensor_reduce(n_above[:], ps_t[:, N:2 * N].rearrange("p (e t) -> p e t", e=E), AX.X, ALU.add).then_inc(red_s, 1)
            ranks(ps_c, 0)
            dve.wait_ge(red_s, 1)
            V.tensor_tensor(rank[:], rank[:], n_above[:].unsqueeze(2).broadcast_to([P, E, TT]), ALU.add).then_inc(early_s, 1)
            dve.wait_ge(early_s, 1)
            V.scalar_tensor_tensor(early[:].rearrange("p e t -> p (e t)"), rank[:].rearrange("p e t -> p (e t)"), CAP - 0.5,
                                   equal[:].rearrange("p e t -> p (e t)"), ALU.is_lt, ALU.mult).then_inc(mix_s, 1)
            dve.wait_ge(mix_s, 1)
            V.tensor_tensor(chosen[:], early[:], above[:], ALU.add).then_inc(ch_s, 1)
            dve.wait_ge(cnt2_s, 1)
            ranks(ps_i, 1)
            V.tensor_scalar(rank[:], rank[:], 2.0 * TOKENS, None, ALU.add).then_inc(pos_s, 1)
            dve.wait_ge(pos_s, 1)
            V.scalar_tensor_tensor(pos_i[:].rearrange("p e t -> p (e t)"), chosen[:].rearrange("p e t -> p (e t)"), -2.0 * TOKENS,
                                   rank[:].rearrange("p e t -> p (e t)"), ALU.mult, ALU.add).then_inc(posi_s, 1)
            dve.wait_ge(posi_s, 1)
            V.tensor_scalar(dig_i[:, 0], pos_i[:], 4, None, ALU.logical_shift_right).then_inc(dg_s, 1)
            V.tensor_scalar(dig_i[:, 1], pos_i[:], 15, None, ALU.bitwise_and).then_inc(dg_s, 1)
            dve.wait_ge(dg_s, 2)
            V.tensor_copy(dig[:], dig_i[:]).then_inc(dgb_s, 1)
            dve.wait_ge(dgb_s, 1)
            for e in range(E):
                par = e % 2
                if e >= 2:
                    dve.wait_ge(idx_ps, e - 1)
                    dve.wait_ge(hott_s, e - 1)
                V.tensor_tensor(hot_b[par][:], ramp[:, 0:16].unsqueeze(1).broadcast_to([P, TT, 16]),
                                dig[:, 1, e, :].unsqueeze(2).broadcast_to([P, TT, 16]), ALU.is_equal).then_inc(hotb_s, 1)
                V.tensor_tensor(hot_a[par][:], ramp[:].unsqueeze(1).broadcast_to([P, TT, 32]),
                                dig[:, 0, e, :].unsqueeze(2).broadcast_to([P, TT, 32]), ALU.is_equal).then_inc(hot_s, 1)
                dve.wait_ge(hotb_s, e + 1)
                V.tensor_scalar(hot_v[par][:, :, 0, :], hot_b[par][:], part_no[:], None, ALU.mult).then_inc(hotv_s, 1)
            dve.wait_ge(idx_ps, E)
            V.tensor_copy(idx_f[:], ps_n[0:32, 0:E * 32].rearrange("a (e v b) -> a e v b", e=E, v=2)).then_inc(idxf_s, 1)
            dve.wait_ge(idxf_s, 1)
            V.scalar_tensor_tensor(idx_i[:], idx_f[:, :, 1, :], float(P), idx_f[:, :, 0, :], ALU.mult, ALU.add).then_inc(idxi_s, 1)

        @block.tensor
        def _(pe):
            for t in range(TT):
                ins = nc.tensor.transpose(ps_l[:, t * E:(t + 1) * E], S["logitsT"][:, t * P:(t + 1) * P], S["ident"][0:E, 0:E])
            ins.then_inc(lg_s, 1)
            pe.wait_ge(sc_s, 1)
            for j in range(2):
                ins = nc.tensor.transpose(ps_k[:, j * P:(j + 1) * P], score[:, j * SEG:(j + 1) * SEG, :].rearrange("p t e -> p (t e)"),
                                          S["ident"][:])
            ins.then_inc(keyT_s, 1)
            pe.wait_ge(bit_s, 8)
            with pe.Fori(0, KEY_BITS) as i:
                pe.wait_ge(cntb_s, i + 1)
                nc.tensor.matmul(ps_n[:, 0:1], same[:], count[:], start=True, stop=True).then_inc(tot_s, 1)
            pe.wait_ge(row_s, 1)
            nc.tensor.transpose(ps_t[:, 0:E], thr_row[:], S["ident"][0:E, 0:E]).then_inc(thrT_s, 1)
            pe.wait_ge(cmp_s, 2)
            pe.wait_ge(tab_s, 5)
            pe.wait_ge(thrb_s, 1)
            flat = lambda m: m[:].rearrange("p e t -> p (e t)")
            nc.tensor.matmul(ps_t[:, N:2 * N], S["ones_b"][:], flat(above), start=True, stop=True)
            running_count(nc, flat(equal), S["before"], S["ones_b"], ps_c).then_inc(cnt1_s, 1)
            pe.wait_ge(ch_s, 1)
            running_count(nc, flat(chosen), S["before"], S["ones_b"], ps_i).then_inc(cnt2_s, 1)
            for e in range(E):
                pe.wait_ge(hot_s, e + 1)
                pe.wait_ge(hotv_s, e + 1)
                pe.wait_ge(hott_s, e + 1)
                for t in range(TT):
                    ins = nc.tensor.matmul(ps_n[0:32, e * 32:(e + 1) * 32], hot_a[e % 2][:, t, :],
                                           hot_v[e % 2][:, t].rearrange("p v b -> p (v b)"), start=(t == 0), stop=(t == TT - 1))
                ins.then_inc(idx_ps, 1)


def expert_choice_ffn(nc, S, T):
    MT = -(-FFN // P)
    LAST = FFN - (MT - 1) * P
    GROUPS = EXPERTS // 2
    ST = CAP // P
    with ExitStack() as ctx:
        sb = lambda n, s, d=F32: ctx.enter_context(nc.sbuf_tensor(n, s, d))
        sem = ctx.enter_context(Semaphores(nc)).new
        ident = S["ident"]
        rows = [sb(f"rows{i}", [P, ST, ROW0]) for i in range(2)]
        gate = [sb(f"gate{i}", [P, ST]) for i in range(2)]
        gT = [sb(f"gT{i}", [P, HALVES, CAP]) for i in range(2)]
        w_up = sb("w_up", [P, HALVES, FFN])
        b_up = sb("b_up", [P, MT])
        w_dn = [sb(f"w_dn{i}", [P, MT, D]) for i in range(2)]
        mid = [[sb(f"mid{i}_{m}", [P if m < MT - 1 else 64, CAP]) for m in range(MT)] for i in range(2)]
        y = [sb(f"y{i}", [P, ST, D]) for i in range(2)]
        banks = [ctx.enter_context(nc.psum_tensor(f"pd{i}", [P, 512], F32)) for i in range(8)]
        ps_t, ps_y = banks[0:2], banks[2:4]
        ps_u = banks[4:8]
        rows_in = [sem(f"pd_rows{i}") for i in range(2)]
        dn_in = [sem(f"pd_dn{i}") for i in range(2)]
        up_in = sem("pd_up")
        added = sem("pd_added")
        one_s, t_ps, gT_s, gate_s, u_ps, mid_s, y_ps, y_s, b_in = (sem("pd_" + n) for n in (
            "one", "t_ps", "gT", "gate", "u_ps", "mid", "y_ps", "y", "b_in"))
        block = ctx.enter_context(nc.Block())

        def groups(engine, emit):
            emit(0, True, False)
            with engine.Fori(1, GROUPS - 1) as g:
                emit(g, False, False)
            emit(GROUPS - 1, False, True)

        @block.sync
        def _(sp):
            sp.wait_ge(one_s, 2)

            def emit(g, first, last):
                if not first:
                    sp.wait_ge(u_ps, g * 2 * MT)
                sp.dma_start(w_up[:], T["W_up"][bass.ds(g, 1)].rearrange("a (h p) f -> p (a h) f", p=P)).then_inc(up_in, 16)
                if not first:
                    sp.wait_ge(mid_s, g * 2 * MT)
                sp.dma_start(b_up[:, 0:MT - 1], T["b_up"][bass.ds(g, 1), 0:(MT - 1) * P].rearrange("a (m p) -> p (a m)", p=P),
                             allow_slow_non_contiguous=True).then_inc(b_in, 16)
                sp.dma_start(b_up[0:LAST, MT - 1:MT], T["b_up"][bass.ds(g, 1), (MT - 1) * P:].rearrange("a p -> p a"),
                             allow_slow_non_contiguous=True).then_inc(b_in, 16)
                for par in range(2):
                    if not first:
                        sp.wait_ge(y_ps, (g * 2 + (par - 1)) * (ST // 2))
                    e = bass.ds(g * 2 + par, 1)
                    sp.dma_start(w_dn[par][:, 0:MT - 1, :], T["W_down"][e, 0:(MT - 1) * P].rearrange("a (m p) d -> p (a m) d", p=P)
                                 ).then_inc(dn_in[par], 16)
                    sp.dma_start(w_dn[par][0:LAST, MT - 1, :], T["W_down"][e, (MT - 1) * P:].rearrange("a p d -> p (a d)")
                                 ).then_inc(dn_in[par], 16)
                    sp.dma_start(w_dn[par][LAST:LAST + 1, MT - 1, :], T["b_down"][e]).then_inc(dn_in[par], 16)

            groups(sp, emit)

        @block.gpsimd
        def _(pool):
            def gather(e, par, first):
                if not first:
                    pool.wait_ge(t_ps, e - 1)
                    pool.wait_ge(gate_s, e - 1)
                for c in range(ST):
                    pool.indirect_dma_start(
                        out=rows[par][:, c, :], out_offset=None, in_=T["rows0"],
                        in_offset=bass.IndirectOffsetOnAxis(ap=S["idx"][:, e, c:c + 1], axis=0)).then_inc(rows_in[par], 16)

            def add(e, par):
                pool.wait_ge(y_s, (e + 1) * ST)
                if e:
                    pool.wait_ge(added, e * 16 * ST)
                for c in range(ST):
                    pool.indirect_dma_start(
                        out=T["resid"], out_offset=bass.IndirectOffsetOnAxis(ap=S["idx"][:, e, c:c + 1], axis=0),
                        in_=y[par][:, c, :], in_offset=None, compute_op=ALU.add).then_inc(added, 16)

            gather(0, 0, True)
            gather(1, 1, True)
            for e in range(EXPERTS):
                add(e, e % 2)
                if e + 2 < EXPERTS:
                    gather(e + 2, e % 2, False)
            pool.wait_ge(added, EXPERTS * 16 * ST)

        @block.vector
        def _(dve):
            for i in range(2):
                nc.vector.memset(mid[i][MT - 1][:], 1.0).then_inc(one_s, 1)

            def emit(g, first, last):
                for par in range(2):
                    e = g * 2 + par
                    dve.wait_ge(t_ps, e + 1)
                    if not first:
                        dve.wait_ge(u_ps, (e - 1) * MT)
                    nc.vector.tensor_copy(gT[par][:, 1, :], ps_t[1][:]).then_inc(gT_s, 1)
                    dve.wait_ge(rows_in[par], (g + 1) * 16 * ST)
                    nc.vector.tensor_scalar(gate[par][:], rows[par][:, :, bass.ds(g * 2 + (D + par), 1)].rearrange("p c a -> p (c a)"),
                                            S["tanh_g"][:, 2:3], None, ALU.mult).then_inc(gate_s, 1)
                    dve.wait_ge(gate_s, e + 1)
                    for c in range(ST):
                        if c % 2 == 0:
                            dve.wait_ge(y_ps, e * (ST // 2) + (c // 2 + 1))
                        if not first and c == 0:
                            dve.wait_ge(added, (e - 1) * 16 * ST)
                        nc.vector.tensor_scalar(y[par][:, c, :], ps_y[c // 2][:, c % 2 * D:(c % 2 + 1) * D], gate[par][:, c:c + 1],
                                                None, ALU.mult).then_inc(y_s, 1)

            groups(dve, emit)

        @block.scalar
        def _(act):
            act.wait_ge(one_s, 2)

            def emit(g, first, last):
                for par in range(2):
                    e = g * 2 + par
                    act.wait_ge(t_ps, e + 1)
                    if not first:
                        act.wait_ge(u_ps, (e - 1) * MT)
                    nc.scalar.activation(gT[par][:, 0, :], ps_t[0][:], ACT.Copy).then_inc(gT_s, 1)
                    act.wait_ge(b_in, (g + 1) * 32)
                    for m in range(MT):
                        n = P if m < MT - 1 else LAST
                        act.wait_ge(u_ps, e * MT + (m + 1))
                        if not first:
                            act.wait_ge(y_ps, (e - 1) * (ST // 2))
                        nc.scalar.activation(mid[par][m][0:n, :], ps_u[(par * MT + m) % 4][0:n, :], ACT.Silu,
                                             bias=b_up[0:n, m:m + 1]).then_inc(mid_s, 1)

            groups(act, emit)

        @block.tensor
        def _(pe):
            def turn(e, par, n16, first):
                pe.wait_ge(rows_in[par], n16)
                if not first:
                    pe.wait_ge(gT_s, e * 2)
                for h in range(HALVES):
                    for c in range(ST):
                        ins = nc.tensor.transpose(ps_t[h][:, c * P:(c + 1) * P], rows[par][:, c, h * P:(h + 1) * P], ident[:])
                ins.then_inc(t_ps, 1)

            def up(g, e, par, first):
                pe.wait_ge(up_in, (g + 1) * 16)
                pe.wait_ge(gT_s, (e + 1) * 2)
                for m in range(MT):
                    n = P if m < MT - 1 else LAST
                    k = par * MT + m
                    if not (first and k < 4):
                        pe.wait_ge(mid_s, e * MT + (m - 3))
                    for h in range(HALVES):
                        ins = nc.tensor.matmul(ps_u[k % 4][0:n, :], w_up[:, h, m * P:m * P + n], gT[par][:, h, :],
                                               start=(h == 0), stop=(h == HALVES - 1))
                    ins.then_inc(u_ps, 1)

            def down(g, e, par, first):
                pe.wait_ge(dn_in[par], (g + 1) * 48)
                pe.wait_ge(mid_s, (e + 1) * MT)
                for c in range(ST):
                    if c == 0 and not (first and par == 0):
                        pe.wait_ge(y_s, e * ST)
                    for m in range(MT):
                        n = P if m < MT - 1 else LAST + 1
                        ins = nc.tensor.matmul(ps_y[c // 2][:, c % 2 * D:(c % 2 + 1) * D], mid[par][m][0:n, c * P:(c + 1) * P],
                                               w_dn[par][0:n, m, :], start=(m == 0), stop=(m == MT - 1))
                    if c % 2:
                        ins.then_inc(y_ps, 1)

            def emit(g, first, last):
                for par in range(2):
                    e = g * 2 + par
                    up(g, e, par, first)
                    if not (last and par == 1):
                        turn(e + 1, 1 - par, (g + (1 + par)) * 16 * ST, False)
                    down(g, e, par, first)

            turn(0, 0, 16 * ST, True)
            groups(pe, emit)


def bidirectional_attention(nc, S, T):
    with ExitStack() as ctx:
        sb = lambda n, s, d=F32: ctx.enter_context(nc.sbuf_tensor(n, s, d))
        two = lambda n, s, d=F32: [sb(f"{n}{i}", s, d) for i in range(2)]
        sem = ctx.enter_context(Semaphores(nc)).new
        ident = S["ident"]
        w_f = sb("w_f", [P, 4, HALVES, D])
        w_sim = sb("w_sim", [P, 3, HALVES])
        w1_row, b_sim = sb("w1_row", [P, D]), sb("b_sim", [P, 1])
        b_qv = sb("b_qv", [P, D])
        wg = sb("wg", [P, HALVES, EXPERTS])
        x_in, c_in, xb = two("dx_in", [P, D]), two("dc_in", [P, D]), two("dxb", [P, D])
        enc = two("enc", [P, D + 1])
        stats, moments = sb("d_stats", [P, 6]), two("d_moments", [P, 2])
        vareps, rstd = sb("d_vareps", [P, 1]), two("d_rstd", [P, 1])
        stats4, moments4 = sb("d_stats4", [P, 6]), two("d_moments4", [P, 2])
        vareps4, rstd4 = sb("d_vareps4", [P, 1]), two("d_rstd4", [P, 1])
        encT, encW, hqT, ehqT = two("encT", [P, HALVES, P]), sb("encW", [P, HALVES, P]), two("hqT", [P, HALVES, P]), two("ehqT", [P, HALVES, P])
        cT = sb("d_cT", [P, HALVES, P])
        neg_max, row_sum, inv = sb("d_neg_max", [P, 1]), sb("d_row_sum", [P, 1]), sb("d_inv", [P, 1])
        a_w = sb("a_w", [P, P])
        a_n = sb("a_n", [P, P])
        aT = sb("d_aT", [P, P])
        prod = sb("d_prod", [P, D])
        s1, v, v_max, v_exp = sb("d_s1", [P, 1]), sb("d_v", [P, 1]), sb("d_vmax", [P, 1]), sb("d_vexp", [P, 1])
        v_sub = sb("d_vsub", [P, 1])
        inv_b, hc_row, hc_col = sb("d_inv_b", [1, 1]), sb("d_hc_row", [1, D]), sb("d_hc_col", [P, HALVES])
        w_c = sb("d_w_c", [P, HALVES, D])
        x3, xn4 = two("d_x3", [P, D]), two("d_xn4", [P, D])
        x4T = sb("d_x4T", [P, HALVES, P])
        ps = [ctx.enter_context(nc.psum_tensor(f"pe{i}", [P, 512], F32)) for i in range(8)]
        ps_t, ps_sim, ps_a, ps_hq, ps_out, ps_row, ps_col, ps_x4 = ps
        ps_lg = ps_row
        w_s, one_s, thb_s = sem("pe_w"), sem("pe_one"), sem("pe_thb")
        x_in_s, c_in_s = [sem(f"pe_x{i}") for i in range(2)], [sem(f"pe_c{i}") for i in range(2)]
        (t_ps, enc_s, encT_s, cT_s, encW_s, sim_ps, max_s, exp_s, inv_s, an_s, a_ps, aT_s, hq_ps, hqT_s, ehqT_s, s1_s, v_s,
         vmax_s, vsub_s, vexp_s, row_ps, invb_s, row_s, col_ps, col_s, wc_s, out_ps, x3_s, st_s, mom_s, ve_s, rstd_s, st4_s,
         mom4_s, ve4_s, rstd4_s, xn4_s, x4_ps, x4T_s, lg_ps, lg_s, xb_s, keep_s, neg_s) = (sem("pe_" + n) for n in (
            "t_ps", "enc", "encT", "cT", "encW", "sim_ps", "max", "exp", "inv", "an", "a_ps", "aT", "hq_ps", "hqT", "ehqT",
            "s1", "v", "vmax", "vsub", "vexp", "row_ps", "invb", "row", "col_ps", "col", "wc", "out_ps", "x3", "st", "mom", "ve",
            "rstd", "st4", "mom4", "ve4", "rstd4", "xn4", "x4_ps", "x4T", "lg_ps", "lg", "xb", "keep", "neg"))
        block = ctx.enter_context(nc.Block())
        x_t = T["resid"].rearrange("(t p) d -> p t d", p=P)
        c_t = T["ctx"].rearrange("(t p) d -> p t d", p=P)
        one = lambda ap: ap.rearrange("p a d -> p (a d)")

        @block.sync
        def _(sp):
            def load(s):
                par = s.k % 2
                wait(sp, enc_s, s.count(1, -1))
                wait(sp, xb_s, s.count(1, -1))
                sp.dma_start(x_in[par][:], one(x_t[:, bass.ds(s.tile(), 1), :])).then_inc(x_in_s[par], 16)
                wait(sp, hq_ps, s.count(1, -1))
                sp.dma_start(c_in[par][:], one(c_t[:, bass.ds(s.tile(), 1), :])).then_inc(c_in_s[par], 16)

            load(Step(0, 0))
            sp.dma_start(w_f[:], T["W_qv"].rearrange("(b h p) n -> p b h n", p=P, h=HALVES)).then_inc(w_s, 16)
            sp.dma_start(w_sim[:], T["w_sim"].rearrange("(w h p) -> p w h", p=P, h=HALVES), allow_slow_non_contiguous=True).then_inc(w_s, 16)
            sp.dma_start(w1_row[:], T["w_sim"][0:D].partition_broadcast(P)).then_inc(w_s, 16)
            sp.dma_start(b_sim[:], T["b_sim"].partition_broadcast(P)).then_inc(w_s, 16)
            sp.dma_start(b_qv[:], T["b_qv"].partition_broadcast(P)).then_inc(w_s, 16)
            sp.dma_start(wg[:], T["wg"].rearrange("(h p) n -> p h n", p=P)).then_inc(w_s, 16)
            load(Step(0, 1))

            def emit(s):
                if s.plus(2).exists():
                    load(s.plus(2))

            steps(sp, emit, 0)

        @block.gpsimd
        def _(pool):
            G = nc.gpsimd
            for i in range(2):
                G.memset(enc[i][:], 1.0).then_inc(one_s, 1)
            pool.wait_ge(w_s, 96)
            G.tensor_scalar(b_qv[:], b_qv[:], S["tanh_g"][:, 1:2], None, ALU.mult).then_inc(thb_s, 1)
            pool.wait_ge(thb_s, 1)

            def power(s, mom, mom_sem, ve, ve_sem, out, out_sem, used_s, used):
                pool.wait_ge(mom_sem, s.count(1, 1))
                G.tensor_tensor(ve[:], mom[s.k % 2][:, 1:2], S["eps"][:, 0:1], ALU.add).then_inc(ve_sem, 1)
                pool.wait_ge(ve_sem, s.count(1, 1))
                wait(pool, used_s, used)
                G.tensor_tensor(out[s.k % 2][:], ve[:], S["minus_half"][:, 0:1], ALU.pow).then_inc(out_sem, 1)

            def emit(s):
                if s.exists():
                    pool.wait_ge(x_in_s[s.k % 2], s.dma(2))
                    wait(pool, x3_s, s.count(1, -1))
                    wait(pool, vsub_s, s.count(1, 0))
                    pool.wait_ge(v_s, s.count(1, 1))
                    G.tensor_tensor(xb[s.k % 2][:], x_in[s.k % 2][:], b_qv[:], ALU.add).then_inc(xb_s, 1)
                    G.partition_all_reduce(v_max[:], v[:], P, REDUCE_MAX).then_inc(vmax_s, 1)
                if s.plus(1).exists():
                    power(s.plus(1), moments, mom_s, vareps, ve_s, rstd, rstd_s, enc_s, s.count(1, 0))
                if s.plus(-1).exists():
                    power(s.plus(-1), moments4, mom4_s, vareps4, ve4_s, rstd4, rstd4_s, xn4_s, s.count(1, -2))

            power(Step(0, 0), moments, mom_s, vareps, ve_s, rstd, rstd_s, enc_s, 0)
            steps(pool, emit, 2)

        @block.vector
        def _(dve):
            V = nc.vector

            def statistics(s):
                par = s.k % 2
                dve.wait_ge(x_in_s[par], s.dma(2))
                V.bn_stats(stats[:], x_in[par][:]).then_inc(st_s, 1)
                settle(nc, S, dve, st_s, s.count(1, 1))
                V.bn_aggr(moments[par][:], stats[:]).then_inc(mom_s, 1)

            def normalise(s):
                par = s.k % 2
                dve.wait_ge(rstd_s, s.count(1, 1))
                wait(dve, row_ps, s.count(1, -1))
                V.tensor_scalar(enc[par][:, 0:D], x_in[par][:], moments[par][:, 0:1], rstd[par][:],
                                ALU.subtract, ALU.mult).then_inc(enc_s, 1)

            def weigh(s):
                dve.wait_ge(encT_s, s.count(1, 1))
                dve.wait_ge(cT_s, s.count(1, 1))
                wait(dve, sim_ps, s.count(1, 0))
                for h in range(HALVES):
                    V.tensor_scalar(encW[:, h, :], encT[s.k % 2][:, h, :], w_sim[:, 2, h:h + 1], w_sim[:, 1, h:h + 1],
                                    ALU.mult, ALU.add).then_inc(encW_s, 1)

            def row_max(s):
                par = s.k % 2
                dve.wait_ge(sim_ps, s.count(1, 1))
                wait(dve, exp_s, s.count(1, 0))
                wait(dve, v_s, s.count(1, 0))
                V.tensor_reduce(neg_max[:], ps_sim[:, 0:P], AX.X, ALU.max, negate=True).then_inc(max_s, 1)
                V.tensor_tensor(prod[:], enc[par][:, 0:D], w1_row[:], ALU.mult).then_inc(neg_s, 1)
                dve.wait_ge(neg_s, s.count(1, 1))
                V.tensor_reduce(s1[:], prod[:], AX.X, ALU.add).then_inc(s1_s, 1)
                dve.wait_ge(s1_s, s.count(1, 1))
                dve.wait_ge(max_s, s.count(1, 1))
                wait(dve, vmax_s, s.count(1, 0))
                V.tensor_scalar(v[:], s1[:], b_sim[:], neg_max[:], ALU.add, ALU.subtract).then_inc(v_s, 1)

            def sub_max(s):
                dve.wait_ge(vmax_s, s.count(1, 1))
                wait(dve, vexp_s, s.count(1, 0))
                V.tensor_tensor(v_sub[:], v[:], v_max[:], ALU.subtract).then_inc(vsub_s, 1)

            def context_row(s):
                dve.wait_ge(row_ps, s.count(1, 1))
                wait(dve, col_ps, s.count(1, 0))
                V.reciprocal(inv_b[:], ps_row[0:1, D:D + 1]).then_inc(invb_s, 1)
                dve.wait_ge(invb_s, s.count(1, 1))
                V.tensor_scalar(hc_row[:], ps_row[0:1, 0:D], inv_b[:], None, ALU.mult).then_inc(row_s, 1)

            def fold(s):
                dve.wait_ge(col_ps, s.count(1, 1))
                V.tensor_copy(hc_col[:], ps_col[:, 0:HALVES]).then_inc(col_s, 1)
                dve.wait_ge(col_s, s.count(1, 1))
                wait(dve, out_ps, s.count(1, 0))
                for h in range(HALVES):
                    V.scalar_tensor_tensor(w_c[:, h, :], w_f[:, 3, h, :], hc_col[:, h:h + 1], w_f[:, 0, h, :],
                                           ALU.mult, ALU.add).then_inc(wc_s, 1)

            def scale_a(s):
                dve.wait_ge(exp_s, s.count(1, 1))
                V.reciprocal(inv[:], row_sum[:]).then_inc(inv_s, 1)
                dve.wait_ge(inv_s, s.count(1, 1))
                wait(dve, a_ps, s.count(1, 0))
                V.tensor_scalar(a_n[:], a_w[:], inv[:], None, ALU.mult).then_inc(an_s, 1)

            def product(s):
                par = s.k % 2
                dve.wait_ge(hqT_s, s.count(1, 1))
                V.tensor_tensor(ehqT[par][:], hqT[par][:], encT[par][:], ALU.mult).then_inc(ehqT_s, 1)

            def residual(s):
                par = s.k % 2
                dve.wait_ge(out_ps, s.count(1, 1))
                dve.wait_ge(xb_s, s.count(1, 1))
                V.scalar_tensor_tensor(x3[par][:], ps_out[:, 0:D], S["tanh_g"][:, 1:2], xb[par][:], ALU.mult, ALU.add).then_inc(x3_s, 1)
                dve.wait_ge(x3_s, s.count(1, 1))
                V.bn_stats(stats4[:], x3[par][:]).then_inc(st4_s, 1)
                V.tensor_copy(one(S["x3"][:, bass.ds(s.tile(), 1), :]), x3[par][:])
                settle(nc, S, dve, st4_s, s.count(1, 1))
                V.bn_aggr(moments4[par][:], stats4[:]).then_inc(mom4_s, 1)

            def normalise4(s):
                par = s.k % 2
                dve.wait_ge(rstd4_s, s.count(1, 1))
                wait(dve, x4_ps, s.count(1, -1))
                wait(dve, keep_s, s.count(1, -1))
                V.tensor_scalar(xn4[par][:], x3[par][:], moments4[par][:, 0:1], rstd4[par][:],
                                ALU.subtract, ALU.mult).then_inc(xn4_s, 1)

            def emit(s):
                if s.plus(-2).exists():
                    normalise4(s.plus(-2))
                if s.exists():
                    weigh(s)
                if s.plus(-1).exists():
                    context_row(s.plus(-1))
                if s.exists():
                    row_max(s)
                if s.plus(-1).exists():
                    fold(s.plus(-1))
                if s.exists():
                    scale_a(s)
                if s.plus(1).exists():
                    statistics(s.plus(1))
                if s.exists():
                    sub_max(s)
                    product(s)
                if s.plus(1).exists():
                    normalise(s.plus(1))
                if s.plus(-1).exists():
                    residual(s.plus(-1))

            dve.wait_ge(one_s, 2)
            statistics(Step(0, 0))
            normalise(Step(0, 0))
            dve.wait_ge(w_s, 96)
            steps(dve, emit, 2)

        @block.scalar
        def _(act):
            def copy(dst, src, s_):
                nc.scalar.activation(dst, src, ACT.Copy).then_inc(s_, 1)

            def emit(s):
                halves = lambda p: p.rearrange("p (h t) -> p h t", h=HALVES)
                if s.exists():
                    par = s.k % 2
                    act.wait_ge(t_ps, s.count(1, 1))
                    wait(act, out_ps, s.count(1, -1))
                    copy(encT[par][:], halves(ps_t[:, 0:D]), encT_s)
                    wait(act, sim_ps, s.count(1, 0))
                    copy(cT[:], halves(ps_t[:, D:2 * D]), cT_s)
                    act.wait_ge(max_s, s.count(1, 1))
                    wait(act, an_s, s.count(1, 0))
                    nc.scalar.activation(a_w[:], ps_sim[:, 0:P], ACT.Exp, bias=neg_max[:], accum_out=row_sum[:]).then_inc(exp_s, 1)
                    act.wait_ge(a_ps, s.count(1, 1))
                    wait(act, hq_ps, s.count(1, 0))
                    copy(aT[:], ps_a[:, 0:P], aT_s)
                    act.wait_ge(vsub_s, s.count(1, 1))
                    wait(act, row_ps, s.count(1, 0))
                    nc.scalar.activation(v_exp[:], v_sub[:], ACT.Exp).then_inc(vexp_s, 1)
                    act.wait_ge(hq_ps, s.count(1, 1))
                    copy(hqT[par][:], halves(ps_hq[:, 0:D]), hqT_s)
                if s.plus(-2).exists():
                    act.wait_ge(x4_ps, s.count(1, -1))
                    wait(act, lg_ps, s.count(1, -2))
                    copy(x4T[:], halves(ps_x4[:, 0:D]), x4T_s)
                    copy(one(S["xn4"][:, bass.ds(s.plus(-2).tile(), 1), :]), xn4[s.k % 2][:], keep_s)
                    act.wait_ge(lg_ps, s.count(1, -1))
                    copy(S["logitsT"][:, bass.ds(s.plus(-2).tile() * P, P)], ps_lg[0:EXPERTS, 0:P], lg_s)

            steps(act, emit, 2)

        @block.tensor
        def _(pe):
            M = nc.tensor

            def emit(s):
                par, pre = s.k % 2, (s.k - 1) % 2
                prev = s.plus(-1).exists()
                if s.exists():
                    pe.wait_ge(enc_s, s.count(1, 1))
                    pe.wait_ge(c_in_s[par], s.dma(2))
                    wait(pe, cT_s, s.count(1, 0))
                    for h in range(HALVES):
                        M.transpose(ps_t[:, h * P:(h + 1) * P], enc[par][:, h * P:(h + 1) * P], ident[:])
                    for h in range(HALVES):
                        ins = M.transpose(ps_t[:, D + h * P:D + (h + 1) * P], c_in[par][:, h * P:(h + 1) * P], ident[:])
                    ins.then_inc(t_ps, 1)
                if prev:
                    pe.wait_ge(vexp_s, s.count(1, 0))
                    wait(pe, lg_s, s.count(1, -2))
                    wait(pe, row_s, s.count(1, -1))
                    M.matmul(ps_row[0:1, 0:D + 1], v_exp[:], enc[pre][:], start=True, stop=True).then_inc(row_ps, 1)
                    pe.wait_ge(ehqT_s, s.count(1, 0))
                    wait(pe, x3_s, s.count(1, -1))
                    for i, op in enumerate((hqT, ehqT)):
                        for h in range(HALVES):
                            M.matmul(ps_out[:, 0:D], op[pre][:, h, :], w_f[:, 1 + i, h, :], start=(i + h == 0), stop=False)
                if s.exists():
                    pe.wait_ge(encW_s, s.count(2, 2))
                    wait(pe, exp_s, s.count(1, 0))
                    for h in range(HALVES):
                        ins = M.matmul(ps_sim[:, 0:P], encW[:, h, :], cT[:, h, :], start=(h == 0), stop=(h == HALVES - 1))
                    ins.then_inc(sim_ps, 1)
                if prev:
                    pe.wait_ge(row_s, s.count(1, 0))
                    wait(pe, col_s, s.count(1, -1))
                    for h in range(HALVES):
                        ins = M.matmul(ps_col[:, h:h + 1], hc_row[:, h * P:(h + 1) * P], ident[0:1, 0:1], start=True, stop=True)
                    ins.then_inc(col_ps, 1)
                    pe.wait_ge(wc_s, s.count(2, 0))
                    for h in range(HALVES):
                        ins = M.matmul(ps_out[:, 0:D], encT[pre][:, h, :], w_c[:, h, :], start=False, stop=(h == HALVES - 1))
                    ins.then_inc(out_ps, 1)
                if s.exists():
                    pe.wait_ge(an_s, s.count(1, 1))
                    wait(pe, aT_s, s.count(1, 0))
                    M.transpose(ps_a[:, 0:P], a_n[:], ident[:]).then_inc(a_ps, 1)
                if s.plus(-2).exists():
                    pe.wait_ge(xn4_s, s.count(1, -1))
                    wait(pe, x4T_s, s.count(1, -2))
                    for h in range(HALVES):
                        ins = M.transpose(ps_x4[:, h * P:(h + 1) * P], xn4[par][:, h * P:(h + 1) * P], ident[:])
                    ins.then_inc(x4_ps, 1)
                if s.exists():
                    pe.wait_ge(aT_s, s.count(1, 1))
                    wait(pe, hqT_s, s.count(1, 0))
                    for h in range(HALVES):
                        ins = M.matmul(ps_hq[:, h * P:(h + 1) * P], c_in[par][:, h * P:(h + 1) * P], aT[:], start=True, stop=True)
                    ins.then_inc(hq_ps, 1)
                if s.plus(-2).exists():
                    pe.wait_ge(x4T_s, s.count(1, -1))
                    wait(pe, row_s, s.count(1, 0) if prev else s.count(1, -1))
                    for h in range(HALVES):
                        ins = M.matmul(ps_lg[0:EXPERTS, 0:P], wg[:, h, :], x4T[:, h, :], start=(h == 0), stop=(h == HALVES - 1))
                    ins.then_inc(lg_ps, 1)

            pe.wait_ge(w_s, 96)
            steps(pe, emit, 2)


def route_first(nc, S, T):
    E, TT, N = EXPERTS, TOK_T, EXPERTS * TOK_T
    with ExitStack() as ctx:
        sb = lambda n, s, d=F32: ctx.enter_context(nc.sbuf_tensor(n, s, d))
        sem = ctx.enter_context(Semaphores(nc)).new
        tmax, tsum = sb("f_tmax", [P, TT]), sb("f_tsum", [P, TT])
        prob = sb("f_prob", [P, TT, E])
        first = sb("f_first", [P, TT, E])
        rev_i, rev = sb("f_rev_i", [P, TT, E], I32), sb("f_rev", [P, TT, E])
        base_i, base = sb("f_base_i", [P, E, TT], I32), sb("f_base", [P, E, TT])
        own_i, own = sb("f_own_i", [P, 1], I32), sb("f_own", [P, 1])
        pick = sb("f_pick", [P, E, TT], BF16)
        scan, rank = sb("f_scan", [P, E, TT]), sb("f_rank", [P, E, TT])
        kept = sb("f_kept", [P, E, TT])
        n_kept, slot, miss = sb("f_n_kept", [P, TT]), sb("f_slot", [P, TT]), sb("f_miss", [P, TT])
        dest = sb("f_dest", [P, TT, 1], I32)
        ps_l = ctx.enter_context(nc.psum_tensor("pf0", [P, 512], F32))
        ps_c = ctx.enter_context(nc.psum_tensor("pf1", [P, 512], F32))
        lg_s, tab_s, sub_s, exp_s, pick_s, cnt_s, dest_s, sent_s, chain = (sem("pf_" + n) for n in (
            "lg", "tab", "sub", "exp", "pick", "cnt", "dest", "sent", "chain"))
        block = ctx.enter_context(nc.Block())
        flat = lambda m: m[:].rearrange("p e t -> p (e t)")
        over_e = lambda m: m[:].rearrange("p e t -> p t e")

        @block.gpsimd
        def _(pool):
            nc.gpsimd.iota(rev_i[:], [[0, TT], [-1, E]], base=E, channel_multiplier=0).then_inc(tab_s, 1)
            nc.gpsimd.iota(base_i[:], [[CAP, E], [0, TT]], base=0, channel_multiplier=0).then_inc(tab_s, 1)
            nc.gpsimd.iota(own_i[:], [[0, 1]], base=TOKENS, channel_multiplier=1).then_inc(tab_s, 1)
            pool.wait_ge(dest_s, 1)
            for t in range(TT):
                pool.indirect_dma_start(out=T["slots"], out_offset=bass.IndirectOffsetOnAxis(ap=dest[:, t, :], axis=0),
                                        in_=S["xn4"][:, t, :], in_offset=None,
                                        bounds_check=TOKENS - 1, oob_is_err=False).then_inc(sent_s, 16)
            pool.wait_ge(sent_s, 16 * TT)

        @block.scalar
        def _(act):
            act.wait_ge(sub_s, 1)
            nc.scalar.activation(prob[:], prob[:], ACT.Exp).then_inc(exp_s, 1)

        @block.tensor
        def _(pe):
            for t in range(TT):
                ins = nc.tensor.transpose(ps_l[:, t * E:(t + 1) * E], S["logitsT"][:, t * P:(t + 1) * P], S["ident"][0:E, 0:E])
            ins.then_inc(lg_s, 1)
            pe.wait_ge(pick_s, 1)
            running_count(nc, flat(pick), S["before"], S["ones_b"], ps_c).then_inc(cnt_s, 1)

        @block.vector
        def _(dve):
            V = nc.vector
            done = [0]

            def then(ins):
                done[0] += 1
                ins.then_inc(chain, 1)
                dve.wait_ge(chain, done[0])

            e_bc = lambda m: m[:].unsqueeze(2).broadcast_to([P, TT, E])
            dve.wait_ge(tab_s, 3)
            V.tensor_copy(rev[:], rev_i[:])
            V.tensor_copy(base[:], base_i[:])
            then(V.tensor_copy(own[:], own_i[:]))
            dve.wait_ge(lg_s, 1)
            lg = ps_l[:, 0:N].rearrange("p (t e) -> p t e", e=E)
            then(V.tensor_reduce(tmax[:], lg, AX.X, ALU.max))
            V.tensor_tensor(prob[:], lg, e_bc(tmax), ALU.subtract).then_inc(sub_s, 1)
            dve.wait_ge(exp_s, 1)
            then(V.tensor_reduce(tsum[:], prob[:], AX.X, ALU.add))
            then(V.reciprocal(tsum[:], tsum[:]))
            then(V.tensor_tensor(prob[:], prob[:], e_bc(tsum), ALU.mult))
            then(V.tensor_reduce(tmax[:], prob[:], AX.X, ALU.max))
            then(V.tensor_tensor(first[:], prob[:], e_bc(tmax), ALU.is_equal))
            then(V.tensor_tensor(first[:], first[:], rev[:], ALU.mult))
            then(V.tensor_reduce(tsum[:], first[:], AX.X, ALU.max))
            V.tensor_tensor(over_e(pick), first[:], e_bc(tsum), ALU.is_equal).then_inc(pick_s, 1)
            dve.wait_ge(cnt_s, 1)
            tot = ps_c[:, N:]
            then(V.tensor_tensor_scan(flat(scan), flat(S["keep"]), tot, 0.0, ALU.mult, ALU.add))
            then(V.tensor_tensor(flat(scan), flat(scan), tot, ALU.subtract))
            then(V.tensor_tensor(flat(rank), flat(scan), ps_c[:, 0:N], ALU.add))
            then(V.scalar_tensor_tensor(flat(kept), flat(rank), CAP - 0.5, flat(pick), ALU.is_lt, ALU.mult))
            then(V.tensor_tensor(flat(rank), flat(rank), flat(base), ALU.add))
            then(V.tensor_tensor(flat(rank), flat(rank), flat(kept), ALU.mult))
            V.tensor_reduce(slot[:], over_e(rank), AX.X, ALU.add)
            then(V.tensor_reduce(n_kept[:], over_e(kept), AX.X, ALU.add))
            then(V.tensor_scalar(miss[:], n_kept[:], -1.0, 1.0, ALU.mult, ALU.add))
            then(V.scalar_tensor_tensor(miss[:], miss[:], own[:], slot[:], ALU.mult, ALU.add))
            V.tensor_copy(dest[:, :, 0], miss[:]).then_inc(dest_s, 1)
            V.tensor_copy(S["slot"][:, :, 0], slot[:])
            then(V.tensor_tensor(n_kept[:], n_kept[:], tmax[:], ALU.mult))
            V.tensor_scalar(S["gate1"][:], n_kept[:], S["tanh_g"][:, 3:4], None, ALU.mult)


def first_choice_ffn(nc, S, T):
    ST = CAP // P
    with ExitStack() as ctx:
        sb = lambda n, s, d=F32: ctx.enter_context(nc.sbuf_tensor(n, s, d))
        two = lambda n, s, d=F32: [sb(f"{n}{i}", s, d) for i in range(2)]
        sem = ctx.enter_context(Semaphores(nc)).new
        rows, rT = two("g_rows", [P, ST, D]), two("g_rT", [P, HALVES, CAP])
        w, bias, y = two("g_w", [P, HALVES, D]), two("g_b", [P, D]), two("g_y", [P, ST, D])
        ps = [ctx.enter_context(nc.psum_tensor(f"pg{i}", [P, 512], F32)) for i in range(8)]
        in_s, w_in, out_s = ([sem(f"pg_{n}{i}") for i in range(2)] for n in ("in", "w", "out"))
        t_ps, rT_s, y_ps, y_s = (sem("pg_" + n) for n in ("t_ps", "rT", "y_ps", "y"))
        block = ctx.enter_context(nc.Block())
        slots_t = T["slots"].rearrange("(c p) d -> p c d", p=P)
        y_t = T["expert_out"].rearrange("(c p) d -> p c d", p=P)

        def pairs(engine, emit):
            for par in range(2):
                emit(par, par, 16, True)
            with engine.Fori(1, EXPERTS // 2) as g:
                for par in range(2):
                    emit(g * 2 + par, par, g * 16 + 16, False)

        @block.sync
        def _(sp):
            def load(e, par, first):
                if not first:
                    sp.wait_ge(t_ps, e - 1)
                sp.dma_start(rows[par][:], slots_t[:, bass.ds(e * ST, ST), :]).then_inc(in_s[par], 16)
                if not first:
                    sp.wait_ge(y_ps, (e - 1) * 2)
                    sp.wait_ge(y_s, (e - 1) * 2)
                sp.dma_start(w[par][:], T["W1"][bass.ds(e, 1)].rearrange("a (h p) n -> p (a h) n", p=P)).then_inc(w_in[par], 16)
                sp.dma_start(bias[par][:], T["b1"][bass.ds(e, 1), :].rearrange("a n -> (a n)").partition_broadcast(P)).then_inc(w_in[par], 16)

            def store(e, par):
                sp.wait_ge(y_s, e * 2 + 2)
                sp.dma_start(y_t[:, bass.ds(e * ST, ST), :], y[par][:]).then_inc(out_s[par], 16)

            for par in range(2):
                load(par, par, True)
            with sp.Fori(0, EXPERTS // 2 - 1) as g:
                for par in range(2):
                    store(g * 2 + par, par)
                    load(g * 2 + (par + 2), par, False)
            for par in range(2):
                store(EXPERTS - 2 + par, par)
            for par in range(2):
                sp.wait_ge(out_s[par], 16 * EXPERTS // 2)

        @block.scalar
        def _(act):
            def emit(e, par, n16, first):
                for h in range(HALVES):
                    act.wait_ge(t_ps, e + 1)
                    if not first:
                        act.wait_ge(y_ps, (e - 1) * 2)
                    nc.scalar.activation(rT[par][:, h, :], ps[par * 2 + h][:], ACT.Copy).then_inc(rT_s, 1)

            pairs(act, emit)

        @block.vector
        def _(dve):
            def emit(e, par, n16, first):
                dve.wait_ge(w_in[par], n16 * 2)
                if not first:
                    dve.wait_ge(out_s[par], n16 - 16)
                for j in range(2):
                    dve.wait_ge(y_ps, e * 2 + (j + 1))
                    nc.vector.tensor_tensor(y[par][:, 2 * j:2 * j + 2, :], ps[4 + par * 2 + j][:].rearrange("p (c d) -> p c d", c=2),
                                            bias[par][:].unsqueeze(1).broadcast_to([P, 2, D]), ALU.add).then_inc(y_s, 1)

            pairs(dve, emit)

        @block.tensor
        def _(pe):
            def emit(e, par, n16, first):
                pe.wait_ge(in_s[par], n16)
                if not first:
                    pe.wait_ge(rT_s, (e - 1) * 2)
                for h in range(HALVES):
                    for c in range(ST):
                        ins = nc.tensor.transpose(ps[par * 2 + h][:, c * P:(c + 1) * P], rows[par][:, c, h * P:(h + 1) * P], S["ident"][:])
                ins.then_inc(t_ps, 1)
                pe.wait_ge(rT_s, (e + 1) * 2)
                pe.wait_ge(w_in[par], n16 * 2)
                if not first:
                    pe.wait_ge(y_s, (e - 1) * 2)
                for c in range(ST):
                    for h in range(HALVES):
                        ins = nc.tensor.matmul(ps[4 + par * 2 + c // 2][:, c % 2 * D:(c % 2 + 1) * D], rT[par][:, h, c * P:(c + 1) * P],
                                               w[par][:, h, :], start=(h == 0), stop=(h == HALVES - 1))
                    if c % 2:
                        ins.then_inc(y_ps, 1)

            pairs(pe, emit)


def combine(nc, S, T):
    SLOTS = 4
    with ExitStack() as ctx:
        sb = lambda n, s, d=F32: ctx.enter_context(nc.sbuf_tensor(n, s, d))
        sem = ctx.enter_context(Semaphores(nc)).new
        row, res = [sb(f"h_row{i}", [P, D]) for i in range(SLOTS)], [sb(f"h_res{i}", [P, D]) for i in range(SLOTS)]
        in_s, out_s = [sem(f"ph_in{i}") for i in range(SLOTS)], [sem(f"ph_out{i}") for i in range(SLOTS)]
        res_s = sem("ph_res")
        block = ctx.enter_context(nc.Block())
        out_t = T["out"].rearrange("(t p) d -> t p d", p=P)

        @block.gpsimd
        def _(pool):
            for t in range(TOK_T):
                if t >= SLOTS:
                    pool.wait_ge(res_s, t - SLOTS + 1)
                pool.indirect_dma_start(out=row[t % SLOTS][:], out_offset=None, in_=T["expert_out"],
                                        in_offset=bass.IndirectOffsetOnAxis(ap=S["slot"][:, t, :], axis=0)).then_inc(in_s[t % SLOTS], 16)

        @block.vector
        def _(dve):
            for t in range(TOK_T):
                k = t % SLOTS
                dve.wait_ge(in_s[k], 16 * (t // SLOTS + 1))
                if t >= SLOTS:
                    dve.wait_ge(out_s[k], 16 * (t // SLOTS))
                nc.vector.scalar_tensor_tensor(res[k][:], row[k][:], S["gate1"][:, t:t + 1], S["x3"][:, t, :],
                                               ALU.mult, ALU.add).then_inc(res_s, 1)

        @block.sync
        def _(sp):
            for t in range(TOK_T):
                sp.wait_ge(res_s, t + 1)
                sp.dma_start(out_t[t], res[t % SLOTS][:]).then_inc(out_s[t % SLOTS], 16)
            for k in range(SLOTS):
                sp.wait_ge(out_s[k], 16 * TOK_T // SLOTS)


def program(nc, T):
    with ExitStack() as ctx:
        def keep(name, shape, dtype=F32):
            return ctx.enter_context(nc.sbuf_tensor("s_" + name, shape, dtype))

        S = {name: keep(name, shape, dtype) for name, shape, dtype in (
            ("ident", [P, P], F32), ("ident_b", [P, P], BF16), ("minus_half", [P, QUAD], F32), ("eps", [P, QUAD], F32), ("spare", [P, 1], F32), ("tanh_g", [P, 4], F32),
            ("zero", [P, D], F32), ("logitsT", [EXPERTS, TOKENS], F32), ("ones_b", [P, P], BF16), ("before", [P, P], BF16),
            ("keep", [P, EXPERTS, TILES], F32), ("slot", [P, TILES, 1], I32), ("gate1", [P, TILES], F32))}
        setup(nc, S, T)
        project_qkv(nc, S, T)
        attention(nc, S, T)
        with ExitStack() as routed:
            S["score"] = routed.enter_context(nc.sbuf_tensor("s_score", [P, TILES, EXPERTS], F32))
            S["idx"] = routed.enter_context(nc.sbuf_tensor("s_idx", [P, EXPERTS, CAP // P], I32))
            route_top_k(nc, S, T)
            expert_choice_ffn(nc, S, T)
        S["x3"], S["xn4"] = keep("x3", [P, TILES, D]), keep("xn4", [P, TILES, D])
        bidirectional_attention(nc, S, T)
        route_first(nc, S, T)
        first_choice_ffn(nc, S, T)
        combine(nc, S, T)


def kernel(**inputs):
    import concourse.bacc as bacc
    from concourse.bass_utils import run_bass_kernel_spmd

    laid = {
        "x": inputs["x"].reshape(TOKENS, D), "ctx": inputs["ctx_1024"].reshape(TOKENS, D), "mask": inputs["mask_BxS2_ik0"],
        "g_xattn": inputs["g_xattn"], "g_ffn": inputs["g_ffn"],
    }
    for name in ("Wq", "bq", "Wk", "bk", "Wv", "bv", "Wo", "bo"):
        laid[name] = inputs["L0_xattn_" + name]
    for name in ("Wr", "br", "W_up", "b_up", "W_down", "b_down"):
        laid[name] = inputs["L0_ffn_" + name]
    for name in ("w_sim", "b_sim", "W_qv", "b_qv"):
        laid[name] = inputs["L1_xattn_" + name]
    laid["wg"] = inputs["L1_ffn_wg"]
    laid["W1"] = inputs["L1_ffn_W"].transpose(0, 2, 1)
    laid["b1"] = inputs["L1_ffn_b"]

    nc = bacc.Bacc("TRN2", target_bir_lowering=False, num_devices=1)
    arrays, T = {}, {}
    for name, a in laid.items():
        a = np.ascontiguousarray(a)
        arrays["in_" + name] = a
        T[name] = nc.dram_tensor("in_" + name, a.shape, mybir.dt.from_np(a.dtype), kind="ExternalInput").ap()
    for name, shape, dtype in (
            ("mask_row", (TOKENS,), BF16), ("qparts", (2, D, TOKENS), BF16), ("kparts", (2, D, TOKENS), BF16), ("v", (TOKENS, D), F32),
            ("resid", (TOKENS, D), F32), ("rows0", (TOKENS, ROW0), F32), ("idx", (TOKENS,), I32),
            ("slots", (TOKENS, D), F32), ("expert_out", (TOKENS, D), F32)):
        T[name] = nc.dram_tensor("scratch_" + name, shape, dtype, kind="Internal").ap()
    T["out"] = nc.dram_tensor("result", (TOKENS, D), F32, kind="ExternalOutput").ap()
    program(nc, T)
    r = run_bass_kernel_spmd(nc, [arrays], core_ids=[0])
    return r.results[0]["result"].reshape(BATCHES, SEQ, D)
```

```python
import numpy as np
import concourse.bass as bass
from concourse import mybir
from contextlib import ExitStack

F32 = mybir.dt.float32
BF16 = mybir.dt.bfloat16
I32 = mybir.dt.int32
ALU = mybir.AluOpType
ACT = mybir.ActivationFunctionType
AX = mybir.AxisListType
REDUCE_MAX = bass.bass_isa.ReduceOp.max

P = 128
BATCHES, SEQ, D = 32, 128, 256
TOKENS = BATCHES * SEQ
QUAD = 4
QT = QUAD * P
QUADS = TOKENS // QT
HALVES = D // P
HEADS, HD = 16, 16
EXPERTS = 8
CAP = TOKENS // EXPERTS
FFN = 682
LN_EPS = 1e-5
MASKED = -4e20


class Semaphores:

    def __init__(self, nc):
        self.nc, self.made = nc, []

    def __enter__(self):
        return self

    def new(self, name):
        self.made.append(self.nc.alloc_semaphore(name))
        return self.made[-1]

    def __exit__(self, *exc):
        if exc[0] is None:
            self.nc.clear_and_free_semaphores(self.made)
            self.nc.all_engine_barrier()


def settle(nc, S, dve, semaphore, value):
    dve.wait_ge(semaphore, value)
    nc.vector.memset(S["spare"][:], 0.0)


def setup(nc, S, T):
    with ExitStack() as ctx:
        sem = ctx.enter_context(Semaphores(nc)).new
        mask_i = ctx.enter_context(nc.sbuf_tensor("mask_i", [BATCHES, SEQ], I32))
        mask_add = ctx.enter_context(nc.sbuf_tensor("mask_add", [BATCHES, SEQ], BF16))
        gates = ctx.enter_context(nc.sbuf_tensor("gates", [P, 4], F32))
        loaded, made, masked, stored, tanhed = (sem(n) for n in
            ("su_loaded", "su_made", "su_masked", "su_stored", "su_tanhed"))
        zeroed, cleared = sem("su_zeroed"), sem("su_cleared")
        block = ctx.enter_context(nc.Block())

        @block.sync
        def _(sp):
            sp.dma_start(mask_i[:], T["mask"]).then_inc(loaded, 16)
            sp.dma_start(gates[:, 0:2], T["g_xattn"].partition_broadcast(P)).then_inc(loaded, 16)
            sp.dma_start(gates[:, 2:4], T["g_ffn"].partition_broadcast(P)).then_inc(loaded, 16)
            sp.wait_ge(masked, 1)
            sp.dma_start(T["mask_row"].rearrange("(b s) -> b s", s=SEQ), mask_add[:]).then_inc(stored, 16)
            sp.wait_ge(zeroed, 1)
            sp.dma_start(T["slots"].rearrange("(t p) d -> p t d", p=P),
                         S["zero"][:].unsqueeze(1).broadcast_to([P, TOKENS // P, ROW1])).then_inc(cleared, 16)
            sp.wait_ge(stored, 16)
            sp.wait_ge(cleared, 16)

        @block.gpsimd
        def _(pool):
            nc.gpsimd.memset(S["zero"][:], 0.0).then_inc(zeroed, 1)
            nc.gpsimd.memset(S["ident"][:], 0.0).then_inc(made, 1)
            nc.gpsimd.memset(S["ident_b"][:], 0.0).then_inc(made, 1)
            nc.gpsimd.memset(S["minus_half"][:], -0.5).then_inc(made, 1)
            nc.gpsimd.memset(S["eps"][:], LN_EPS).then_inc(made, 1)
            pool.wait_ge(made, 4)
            for m in (S["ident"], S["ident_b"]):
                nc.gpsimd.affine_select(out=m[:], in_=m[:], compare_op=ALU.not_equal, fill=1.0, base=0,
                                        pattern=[[-1, P]], channel_multiplier=1).then_inc(made, 1)

        @block.vector
        def _(dve):
            dve.wait_ge(loaded, 48)
            nc.vector.tensor_scalar(mask_add[:], mask_i[:], 0.0, MASKED, ALU.is_equal, ALU.mult).then_inc(masked, 1)

        @block.scalar
        def _(act):
            act.wait_ge(loaded, 48)
            nc.scalar.activation(S["tanh_g"][:], gates[:], ACT.Tanh).then_inc(tanhed, 1)


def project_qkv(nc, S, T):
    with ExitStack() as ctx:
        sb = lambda n, s, d=F32: ctx.enter_context(nc.sbuf_tensor(n, s, d))
        sem = ctx.enter_context(Semaphores(nc)).new
        ident = S["ident"]
        wq, wk, wv = (sb(n, [P, HALVES, D]) for n in ("wq", "wk", "wv"))
        bias_qk = sb("bias_qk", [P, 2, HALVES])
        bias_v = sb("bias_v", [P, 2, D])
        x_in = [sb(f"x_in{i}", [P, QUAD, D]) for i in range(2)]
        c_in = [sb(f"c_in{i}", [P, QUAD, D]) for i in range(2)]
        xn = [sb(f"xn{i}", [P, QUAD, D]) for i in range(2)]
        stats = sb("stats", [P, QUAD, 6])
        moments = sb("moments", [P, QUAD, 2])
        vareps = sb("vareps", [P, QUAD])
        rstd = sb("rstd", [P, QUAD])
        xT = [sb(f"xT{i}", [P, HALVES, QT]) for i in range(2)]
        cT = [sb(f"cT{i}", [P, HALVES, QT]) for i in range(2)]
        parts = [sb(f"parts{i}", [P, 2, HALVES, 2, QT], BF16) for i in range(2)]
        v_out = [sb(f"v_out{i}", [P, QUAD, D]) for i in range(2)]
        banks = [ctx.enter_context(nc.psum_tensor(f"pa{i}", [P, 512], F32)) for i in range(8)]
        ps_x, ps_c, ps_q, ps_k = banks[0:2], banks[2:4], banks[4:6], banks[6:8]
        ps_v = ps_x
        weights = sem("pa_weights")
        x_in_s = [sem(f"pa_x{i}") for i in range(2)]
        c_in_s = [sem(f"pa_c{i}") for i in range(2)]
        stats_s, moments_s, rstd_s, xn_s = (sem(n) for n in ("pa_stats", "pa_moments", "pa_rstd", "pa_xn"))
        vareps_s = sem("pa_vareps")
        xt_ps, ct_ps, q_ps, k_ps, v_ps = (sem(n) for n in ("pa_xt_ps", "pa_ct_ps", "pa_q_ps", "pa_k_ps", "pa_v_ps"))
        xt_s, ct_s, hi_s, lo_s, v_s = (sem(n) for n in ("pa_xt", "pa_ct", "pa_hi", "pa_lo", "pa_v"))
        qk_out = [sem(f"pa_qk_out{i}") for i in range(2)]
        v_outs = [sem(f"pa_v_out{i}") for i in range(2)]
        block = ctx.enter_context(nc.Block())
        x_t = T["x"].rearrange("(t p) d -> p t d", p=P)
        c_t = T["ctx"].rearrange("(t p) d -> p t d", p=P)
        v_t = T["v"].rearrange("(t p) d -> p t d", p=P)

        @block.sync
        def _(sp):
            for i, w in enumerate(("Wq", "Wk", "Wv")):
                sp.dma_start((wq, wk, wv)[i][:], T[w].rearrange("(h p) n -> p h n", p=P)).then_inc(weights, 16)
            for j in range(2):
                sp.dma_start(bias_v[:, j, :], T["bv"].partition_broadcast(P)).then_inc(weights, 16)
                sp.dma_start(bias_qk[:, j, :], T[("bq", "bk")[j]].rearrange("(h p) -> p h", p=P), allow_slow_non_contiguous=True).then_inc(weights, 16)

            def load(q, par, first):
                if not first:
                    sp.wait_ge(ct_ps, q - 1)
                    sp.wait_ge(xt_ps, q - 1)
                sp.dma_start(x_in[par][:], x_t[:, bass.ds(q * QUAD, QUAD), :]).then_inc(x_in_s[par], 16)
                sp.dma_start(c_in[par][:], c_t[:, bass.ds(q * QUAD, QUAD), :]).then_inc(c_in_s[par], 16)

            def store(q, par):
                sp.wait_ge(lo_s, 4 * q + 4)
                for j, name in enumerate(("qparts", "kparts")):
                    for h in range(HALVES):
                        sp.dma_start(T[name][:, h * P:(h + 1) * P, bass.ds(q * QT, QT)].rearrange("s p t -> p s t"),
                                     parts[par][:, j, h]).then_inc(qk_out[par], 16)
                sp.wait_ge(v_s, 2 * q + 2)
                sp.dma_start(v_t[:, bass.ds(q * QUAD, QUAD), :], v_out[par][:]).then_inc(v_outs[par], 16)

            for par in range(2):
                load(par, par, True)
            with sp.Fori(0, QUADS // 2 - 1) as pair:
                for par in range(2):
                    load(pair * 2 + (par + 2), par, False)
                    store(pair * 2 + par, par)
            for par in range(2):
                store(QUADS - 2 + par, par)
            for par in range(2):
                sp.wait_ge(qk_out[par], 64 * QUADS // 2)
                sp.wait_ge(v_outs[par], 16 * QUADS // 2)

        @block.gpsimd
        def _(pool):
            with pool.Fori(0, QUADS) as q:
                pool.wait_ge(moments_s, q + 1)
                nc.gpsimd.tensor_tensor(vareps[:], moments[:, :, 1], S["eps"][:], ALU.add).then_inc(vareps_s, 1)
                pool.wait_ge(vareps_s, q + 1)
                nc.gpsimd.tensor_tensor(rstd[:], vareps[:], S["minus_half"][:, 0:QUAD], ALU.pow).then_inc(rstd_s, 1)

        @block.vector
        def _(dve):
            def norm(q, par, n16, first):
                dve.wait_ge(x_in_s[par], n16)
                if not first:
                    dve.wait_ge(xt_ps, q - 1)
                for t in range(QUAD):
                    nc.vector.bn_stats(stats[:, t, :], x_in[par][:, t, :]).then_inc(stats_s, 1)
                settle(nc, S, dve, stats_s, q * QUAD + QUAD)
                for t in range(QUAD):
                    ins = nc.vector.bn_aggr(moments[:, t, :], stats[:, t, :])
                ins.then_inc(moments_s, 1)
                dve.wait_ge(rstd_s, q + 1)
                dve.wait_ge(moments_s, q + 1)
                for t in range(QUAD):
                    ins = nc.vector.tensor_scalar(xn[par][:, t, :], x_in[par][:, t, :], moments[:, t, 0:1], rstd[:, t:t + 1],
                                                  ALU.subtract, ALU.mult)
                ins.then_inc(xn_s, 1)

            def quad(q, par, first, fresh):
                for h in range(HALVES):
                    dve.wait_ge(ct_ps, q + 1)
                    if not first:
                        dve.wait_ge(k_ps, q)
                    nc.vector.tensor_copy(cT[par][:, h, :], ps_c[h][:]).then_inc(ct_s, 1)
                for h in range(HALVES):
                    dve.wait_ge(hi_s, 4 * q + (h + 1))
                    nc.vector.scalar_tensor_tensor(parts[par][:, 0, h, 1, :], ps_q[h][:], bias_qk[:, 0, h:h + 1],
                                                   parts[par][:, 0, h, 0, :], ALU.add, ALU.subtract).then_inc(lo_s, 1)
                for j in range(2):
                    dve.wait_ge(v_ps, 2 * q + (j + 1))
                    if not fresh:
                        dve.wait_ge(v_outs[par], out16(q, par))
                    nc.vector.tensor_tensor(v_out[par][:, 2 * j:2 * j + 2, :], ps_v[j][:].rearrange("p (a d) -> p a d", a=2),
                                            bias_v[:], ALU.add).then_inc(v_s, 1)
                for h in range(HALVES):
                    dve.wait_ge(hi_s, 4 * q + (h + 3))
                    nc.vector.scalar_tensor_tensor(parts[par][:, 1, h, 1, :], ps_k[h][:], bias_qk[:, 1, h:h + 1],
                                                   parts[par][:, 1, h, 0, :], ALU.add, ALU.subtract).then_inc(lo_s, 1)

            def out16(q, par):
                return (q - par) * 8

            dve.wait_ge(weights, 16 * 7)
            norm(0, 0, 16, True)
            norm(1, 1, 16, True)
            quad(0, 0, True, True)
            norm(2, 0, 32, False)
            quad(1, 1, False, True)
            with dve.Fori(1, QUADS // 2 - 1) as pair:
                norm(pair * 2 + 1, 1, pair * 16 + 16, False)
                quad(pair * 2, 0, False, False)
                norm(pair * 2 + 2, 0, pair * 16 + 32, False)
                quad(pair * 2 + 1, 1, False, False)
            norm(QUADS - 1, 1, 8 * QUADS, False)
            quad(QUADS - 2, 0, False, False)
            quad(QUADS - 1, 1, False, False)

        @block.scalar
        def _(act):
            def quad(q, par, first):
                for h in range(HALVES):
                    act.wait_ge(xt_ps, q + 1)
                    if not first:
                        act.wait_ge(q_ps, q - 1)
                    nc.scalar.activation(xT[par][:, h, :], ps_x[h][:], ACT.Copy).then_inc(xt_s, 1)
                for h in range(HALVES):
                    act.wait_ge(q_ps, q + 1)
                    if not first:
                        act.wait_ge(qk_out[par], (q - par) * 32)
                    nc.scalar.activation(parts[par][:, 0, h, 0, :], ps_q[h][:], ACT.Identity,
                                         bias=bias_qk[:, 0, h:h + 1]).then_inc(hi_s, 1)
                for h in range(HALVES):
                    act.wait_ge(k_ps, q + 1)
                    nc.scalar.activation(parts[par][:, 1, h, 0, :], ps_k[h][:], ACT.Identity,
                                         bias=bias_qk[:, 1, h:h + 1]).then_inc(hi_s, 1)

            act.wait_ge(weights, 16 * 7)
            for par in range(2):
                quad(par, par, True)
            with act.Fori(1, QUADS // 2) as pair:
                for par in range(2):
                    quad(pair * 2 + par, par, False)

        @block.tensor
        def _(pe):
            def quad(q, par, n16, first):
                pe.wait_ge(xn_s, q + 1)
                if not first:
                    pe.wait_ge(v_s, 2 * q)
                for h in range(HALVES):
                    for t in range(QUAD):
                        ins = nc.tensor.transpose(ps_x[h][:, t * P:(t + 1) * P], xn[par][:, t, h * P:(h + 1) * P], ident[:])
                ins.then_inc(xt_ps, 1)
                pe.wait_ge(c_in_s[par], n16)
                if not first:
                    pe.wait_ge(ct_s, 2 * q)
                for h in range(HALVES):
                    for t in range(QUAD):
                        ins = nc.tensor.transpose(ps_c[h][:, t * P:(t + 1) * P], c_in[par][:, t, h * P:(h + 1) * P], ident[:])
                ins.then_inc(ct_ps, 1)
                pe.wait_ge(xt_s, 2 * q + 2)
                if not first:
                    pe.wait_ge(lo_s, 4 * q)
                for m in range(HALVES):
                    for h in range(HALVES):
                        ins = nc.tensor.matmul(ps_q[m][:], wq[:, h, m * P:(m + 1) * P], xT[par][:, h, :],
                                               start=(h == 0), stop=(h == HALVES - 1))
                ins.then_inc(q_ps, 1)
                pe.wait_ge(ct_s, 2 * q + 2)
                for t in range(QUAD):
                    for h in range(HALVES):
                        ins = nc.tensor.matmul(ps_v[t // 2][:, (t % 2) * D:(t % 2 + 1) * D], cT[par][:, h, t * P:(t + 1) * P],
                                               wv[:, h, :], start=(h == 0), stop=(h == HALVES - 1))
                    if t % 2:
                        ins.then_inc(v_ps, 1)
                for m in range(HALVES):
                    for h in range(HALVES):
                        ins = nc.tensor.matmul(ps_k[m][:], wk[:, h, m * P:(m + 1) * P], cT[par][:, h, :],
                                               start=(h == 0), stop=(h == HALVES - 1))
                ins.then_inc(k_ps, 1)

            pe.wait_ge(weights, 16 * 7)
            for par in range(2):
                quad(par, par, 16, par == 0)
            with pe.Fori(1, QUADS // 2) as pair:
                for par in range(2):
                    quad(pair * 2 + par, par, pair * 16 + 16, False)


TILES = TOKENS // P
STACK = 3 * HD + 1
SLOTW = 32


class Step:

    def __init__(self, base, k):
        self.base, self.k = base, k

    def plus(self, d):
        return Step(self.base, self.k + d)

    def count(self, per, extra):
        return self.base * (4 * per) + (self.k * per + extra)

    def dma(self, slots, per=1):
        return self.base * (4 // slots * 16 * per) + 16 * per * (self.k // slots + 1)

    def exists(self):
        return not isinstance(self.base, int) or 0 <= self.base * 4 + self.k < TILES

    def tile(self):
        return self.base * 4 + self.k


def wait(engine, semaphore, value):
    if not isinstance(value, int) or value > 0:
        engine.wait_ge(semaphore, value)


def steps(engine, emit, tail):
    for k in range(4):
        emit(Step(0, k))
    with engine.Fori(1, TILES // 4 - 1) as base:
        for k in range(4):
            emit(Step(base, k))
    for k in range(4 + tail):
        emit(Step(TILES // 4 - 1, k))


def attention(nc, S, T):
    with ExitStack() as ctx:
        sb = lambda n, s, d=F32: ctx.enter_context(nc.sbuf_tensor(n, s, d))
        sem = ctx.enter_context(Semaphores(nc)).new
        ident, ident_b = S["ident"], S["ident_b"]
        wo, wr = sb("wo", [P, HALVES, D]), sb("wr", [P, HALVES, EXPERTS])
        bo = sb("bo", [P, D])
        br = sb("br", [EXPERTS, 1])
        pick = sb("pick", [2 * HEADS, HEADS, P], BF16)
        qs = [sb(f"qs{i}", [64, HEADS, 2 * P], BF16) for i in range(2)]
        ks = [sb(f"ks{i}", [64, HEADS, 2 * P], BF16) for i in range(2)]
        v_in = [sb(f"v_in{i}", [P, D]) for i in range(2)]
        v_wide = [sb(f"v_wide{i}", [P, HEADS, SLOTW]) for i in range(2)]
        x_res = [sb(f"x_res{i}", [P, D]) for i in range(2)]
        neg_max = sb("neg_max", [P, HEADS])
        nm_parts = sb("nm_parts", [P, 2, HEADS], BF16)
        nmT = sb("nmT", [2 * HEADS, P], BF16)
        probs = [sb(f"probs{i}", [P, 4, P]) for i in range(2)]
        ctxT = sb("ctxT", [P, 4 * P])
        inv_sum = sb("inv_sum", [P, HEADS])
        attn = sb("attn", [P, D])
        attnT = sb("attnT", [P, HALVES, P])
        x1 = [sb(f"x1_{i}", [P, D]) for i in range(2)]
        stats, moments = sb("b_stats", [P, 6]), [sb(f"b_moments{i}", [P, 2]) for i in range(2)]
        vareps, rstd = sb("b_vareps", [P, 1]), sb("b_rstd", [P, 1])
        xn = [sb(f"b_xn{i}", [P, D]) for i in range(2)]
        xnT = sb("b_xnT", [P, HALVES, P])
        ps = [ctx.enter_context(nc.psum_tensor(f"pb{i}", [P, 512], F32)) for i in range(6)]
        ps_s, ps_st, ps_ctx, ps_ctxT = ps[0:2], ps[2:4], ps[4], ps[5]
        ps6 = ctx.enter_context(nc.psum_tensor("pb6", [P, 512], F32))
        ps7 = ctx.enter_context(nc.psum_tensor("pb7", [P, 512], F32))
        ps_aT, ps_nmT = ps6[:, 0:D], ps6[0:2 * HEADS, D:D + P // 2].bitcast(BF16)
        ps_o, ps_xnT = ps7[:, 0:D], ps7[:, D:2 * D]
        ps_lg = ps_ctxT[0:EXPERTS, 0:P]
        w_s, thbo_s, pick_s, ones_s = sem("pb_w"), sem("pb_thbo"), sem("pb_pick"), sem("pb_ones")
        q_in = [sem(f"pb_q{i}") for i in range(2)]
        k_in = [sem(f"pb_k{i}") for i in range(2)]
        v_in_s = [sem(f"pb_vin{i}") for i in range(2)]
        x_in_s = [sem(f"pb_xin{i}") for i in range(2)]
        x1_out = [sem(f"pb_x1out{i}") for i in range(2)]
        xn_out = [sem(f"pb_xnout{i}") for i in range(2)]
        (s_ps, max_s, nm_hi_s, nm_s, nmT_ps, nmT_s, st_ps, exp_s, ctx_ps, ctxT_s, ctxT_ps, inv_s, attn_s, aT_ps, aT_s,
         o_ps, x1_s, stats_s, mom_s, ve_s, rstd_s, xn_s, xnT_ps, xnT_s, lg_ps, lg_s, vw_s, xb_s) = (
            sem("pb_" + n) for n in (
                "s_ps", "max", "nm_hi", "nm", "nmT_ps", "nmT", "st_ps", "exp", "ctx_ps", "ctxT", "ctxT_ps", "inv",
                "attn", "aT_ps", "aT", "o_ps", "x1", "stats", "mom", "ve", "rstd", "xn", "xnT_ps", "xnT", "lg_ps", "lg",
                "vw", "xb"))
        av_s = sem("pb_av")
        block = ctx.enter_context(nc.Block())
        v_t = T["v"].rearrange("(t p) d -> p t d", p=P)
        x_t = T["x"].rearrange("(t p) d -> p t d", p=P)
        x1_t = T["resid"].rearrange("(t p) d -> p t d", p=P)
        xn_t = T["rows0"].rearrange("(t p) d -> p t d", p=P)

        @block.sync
        def _(sp):
            sp.dma_start(wo[:], T["Wo"].rearrange("(h p) n -> p h n", p=P)).then_inc(w_s, 16)
            sp.dma_start(wr[:], T["Wr"].rearrange("(h p) n -> p h n", p=P)).then_inc(w_s, 16)
            sp.dma_start(bo[:], T["bo"].partition_broadcast(P)).then_inc(w_s, 16)
            sp.dma_start(br[:], T["br"].rearrange("(e a) -> e a", a=1)).then_inc(w_s, 16)
            sp.wait_ge(ones_s, 2)

            def load_stacks(s):
                slot = s.k // 2 % 2
                wait(sp, st_ps, s.count(4, -8))
                toks = bass.ds(s.tile() * P, 2 * P)
                for i, part in enumerate((0, 1, 0)):
                    sp.dma_start(qs[slot][i * HD:(i + 1) * HD, :, :],
                                 T["qparts"][part, :, toks].rearrange("(h r) t -> r h t", r=HD)).then_inc(q_in[slot], 16)
                for i, part in enumerate((0, 0, 1)):
                    sp.dma_start(ks[slot][i * HD:(i + 1) * HD, :, :],
                                 T["kparts"][part, :, toks].rearrange("(h r) t -> r h t", r=HD)).then_inc(k_in[slot], 16)
                sp.dma_start(ks[slot][3 * HD:STACK, :, :],
                             T["mask_row"][toks].unsqueeze(0).unsqueeze(0).broadcast_to([1, HEADS, 2 * P])
                             ).then_inc(k_in[slot], 16)

            def load_tiles(s):
                slot = s.k % 2
                wait(sp, vw_s, s.count(1, -1))
                sp.dma_start(v_in[slot][:], v_t[:, bass.ds(s.tile(), 1), :].rearrange("p a d -> p (a d)")).then_inc(v_in_s[slot], 16)
                wait(sp, x1_s, s.count(1, -1))
                sp.dma_start(x_res[slot][:], x_t[:, bass.ds(s.tile(), 1), :].rearrange("p a d -> p (a d)")).then_inc(x_in_s[slot], 16)

            def emit(s):
                if s.k % 2 == 0 and s.plus(2).exists():
                    load_stacks(s.plus(2))
                if s.plus(1).exists():
                    load_tiles(s.plus(1))
                if s.plus(-1).exists():
                    sp.wait_ge(x1_s, s.count(1, 0))
                    sp.dma_start(x1_t[:, bass.ds(s.plus(-1).tile(), 1), :].rearrange("p a d -> p (a d)"),
                                 x1[(s.k - 1) % 2][:]).then_inc(x1_out[(s.k - 1) % 2], 16)
                if s.plus(-2).exists():
                    sp.wait_ge(xn_s, s.count(1, -1))
                    sp.dma_start(xn_t[:, bass.ds(s.plus(-2).tile(), 1), 0:D].rearrange("p a d -> p (a d)"),
                                 xn[s.k % 2][:]).then_inc(xn_out[s.k % 2], 16)

            load_stacks(Step(0, 0))
            load_tiles(Step(0, 0))
            steps(sp, emit, 2)
            for i in range(2):
                sp.wait_ge(x1_out[i], 16 * TILES // 2)
                sp.wait_ge(xn_out[i], 16 * TILES // 2)

        @block.gpsimd
        def _(pool):
            nc.gpsimd.memset(pick[:], 0.0).then_inc(pick_s, 1)
            for t in range(2):
                nc.gpsimd.memset(v_wide[t][:], 1.0).then_inc(pick_s, 1)
            pool.wait_ge(w_s, 64)
            nc.gpsimd.tensor_scalar(bo[:], bo[:], S["tanh_g"][:, 0:1], None, ALU.mult).then_inc(thbo_s, 1)
            for r in range(2):
                pool.wait_ge(pick_s, 3 + r)
                nc.gpsimd.affine_select(out=pick[:], in_=pick[:], compare_op=ALU.not_equal, fill=1.0, base=-HEADS * r,
                                        pattern=[[-1, HEADS], [0, P]], channel_multiplier=1).then_inc(pick_s, 1)
            pool.wait_ge(thbo_s, 1)

            def widen(s):
                slot = s.k % 2
                pool.wait_ge(v_in_s[slot], s.dma(2))
                wait(pool, ctx_ps, s.count(1, -1))
                nc.gpsimd.tensor_tensor(v_wide[slot][:, :, 0:HD], v_in[slot][:].rearrange("p (h d) -> p h d", h=HEADS),
                                        S["zero"][:, 0:D].rearrange("p (h d) -> p h d", h=HEADS), ALU.add).then_inc(vw_s, 1)

            def emit(s):
                if s.plus(1).exists():
                    widen(s.plus(1))
                if s.exists():
                    slot = s.k % 2
                    pool.wait_ge(x_in_s[slot], s.dma(2))
                    nc.gpsimd.tensor_tensor(x_res[slot][:], x_res[slot][:], bo[:], ALU.add).then_inc(xb_s, 1)
                if s.plus(-1).exists():
                    pool.wait_ge(mom_s, s.count(1, 0))
                    nc.gpsimd.tensor_tensor(vareps[:], moments[(s.k - 1) % 2][:, 1:2], S["eps"][:, 0:1], ALU.add).then_inc(ve_s, 1)
                    pool.wait_ge(ve_s, s.count(1, 0))
                    wait(pool, xn_s, s.count(1, -1))
                    nc.gpsimd.tensor_tensor(rstd[:], vareps[:], S["minus_half"][:, 0:1], ALU.pow).then_inc(rstd_s, 1)

            widen(Step(0, 0))
            steps(pool, emit, 1)

        @block.vector
        def _(dve):
            def row_max(s, g):
                dve.wait_ge(s_ps, s.count(4, g + 1))
                wait(dve, nm_s, s.count(1, 0))
                nc.vector.tensor_reduce(neg_max[:, 4 * g:4 * g + 4], ps_s[g % 2][:].rearrange("p (h k) -> p h k", h=4),
                                        AX.X, ALU.max, negate=True).then_inc(max_s, 1)

            def split_max(s):
                dve.wait_ge(max_s, s.count(4, 4))
                wait(dve, nmT_ps, s.count(1, 0))
                nc.vector.tensor_copy(nm_parts[:, 0, :], neg_max[:]).then_inc(nm_hi_s, 1)
                dve.wait_ge(nm_hi_s, s.count(1, 1))
                nc.vector.tensor_tensor(nm_parts[:, 1, :], neg_max[:], nm_parts[:, 0, :], ALU.subtract).then_inc(nm_s, 1)

            def max_out(s):
                dve.wait_ge(nmT_ps, s.count(1, 1))
                wait(dve, st_ps, s.count(4, 0))
                nc.vector.tensor_copy(nmT[:], ps_nmT).then_inc(nmT_s, 1)

            def normalise(s):
                heads = ps_ctxT[:].rearrange("p (h c) -> p h c", h=HEADS)
                dve.wait_ge(ctxT_ps, s.count(1, 1))
                nc.vector.reciprocal(inv_sum[:], heads[:, :, HD]).then_inc(inv_s, 1)
                dve.wait_ge(inv_s, s.count(1, 1))
                wait(dve, aT_ps, s.count(1, 0))
                nc.vector.tensor_tensor(attn[:].rearrange("p (h d) -> p h d", h=HEADS), heads[:, :, 0:HD],
                                        inv_sum[:].unsqueeze(2).broadcast_to([P, HEADS, HD]), ALU.mult).then_inc(attn_s, 1)

            def residual(s):
                slot = s.k % 2
                dve.wait_ge(o_ps, s.count(1, 1))
                dve.wait_ge(xb_s, s.count(1, 1))
                if s.plus(-2).exists():
                    dve.wait_ge(x1_out[slot], s.plus(-2).dma(2))
                nc.vector.scalar_tensor_tensor(x1[slot][:], ps_o, S["tanh_g"][:, 0:1], x_res[slot][:],
                                               ALU.mult, ALU.add).then_inc(x1_s, 1)
                dve.wait_ge(x1_s, s.count(1, 1))
                nc.vector.bn_stats(stats[:], x1[slot][:]).then_inc(stats_s, 1)
                settle(nc, S, dve, stats_s, s.count(1, 1))
                nc.vector.bn_aggr(moments[slot][:], stats[:]).then_inc(mom_s, 1)

            def norm(s):
                slot = s.k % 2
                dve.wait_ge(rstd_s, s.count(1, 1))
                wait(dve, xnT_ps, s.count(1, -1))
                if s.plus(-2).exists():
                    dve.wait_ge(xn_out[slot], s.plus(-2).dma(2))
                nc.vector.tensor_scalar(xn[slot][:], x1[slot][:], moments[slot][:, 0:1], rstd[:],
                                        ALU.subtract, ALU.mult).then_inc(xn_s, 1)

            def emit(s):
                if s.plus(1).exists():
                    row_max(s.plus(1), 0)
                    row_max(s.plus(1), 1)
                if s.plus(-2).exists():
                    norm(s.plus(-2))
                if s.plus(1).exists():
                    row_max(s.plus(1), 2)
                    row_max(s.plus(1), 3)
                    split_max(s.plus(1))
                if s.plus(-1).exists():
                    normalise(s.plus(-1))
                    residual(s.plus(-1))
                if s.plus(1).exists():
                    max_out(s.plus(1))

            for t in qs:
                nc.vector.memset(t[32:64, :, :], 1.0).then_inc(ones_s, 1)
            for g in range(4):
                row_max(Step(0, 0), g)
            split_max(Step(0, 0))
            max_out(Step(0, 0))
            steps(dve, emit, 2)

        @block.scalar
        def _(act):
            act.wait_ge(w_s, 64)

            def emit(s):
                if s.plus(-1).exists():
                    act.wait_ge(ctx_ps, s.count(1, 0))
                    wait(act, ctxT_ps, s.count(1, -1))
                    nc.scalar.activation(ctxT[:], ps_ctx[:], ACT.Copy).then_inc(ctxT_s, 1)
                if s.exists():
                    for g in range(4):
                        act.wait_ge(st_ps, s.count(4, g + 1))
                        if g < 2:
                            wait(act, ctx_ps, s.count(1, 0))
                        else:
                            act.wait_ge(av_s, s.count(3, g - 1))
                        nc.scalar.activation(probs[g % 2][:], ps_st[g % 2][:].rearrange("p (h q) -> p h q", h=4),
                                             ACT.Exp, scale=1.0 / HD ** 0.5).then_inc(exp_s, 1)
                if s.plus(-2).exists():
                    act.wait_ge(xnT_ps, s.count(1, -1))
                    wait(act, lg_ps, s.count(1, -2))
                    nc.scalar.activation(xnT[:], ps_xnT.rearrange("p (h t) -> p h t", h=HALVES), ACT.Copy).then_inc(xnT_s, 1)
                if s.plus(-1).exists():
                    act.wait_ge(aT_ps, s.count(1, 0))
                    wait(act, o_ps, s.count(1, -1))
                    nc.scalar.activation(attnT[:], ps_aT.rearrange("p (h t) -> p h t", h=HALVES), ACT.Copy).then_inc(aT_s, 1)
                if s.plus(-2).exists():
                    act.wait_ge(lg_ps, s.count(1, -1))
                    nc.scalar.activation(S["logitsT"][:, bass.ds(s.plus(-2).tile() * P, P)], ps_lg, ACT.Identity,
                                         bias=br[:]).then_inc(lg_s, 1)

            steps(act, emit, 2)

        @block.tensor
        def _(pe):
            pe.wait_ge(w_s, 64)
            pe.wait_ge(pick_s, 5)

            def operand(t, s, h, rows):
                return t[s.k // 2 % 2][0:rows, h, s.k % 2 * P:(s.k % 2 + 1) * P]

            def scores(s, g):
                if g == 0 and s.k % 2 == 0:
                    pe.wait_ge(q_in[s.k // 2 % 2], s.dma(4, 3))
                    pe.wait_ge(k_in[s.k // 2 % 2], s.dma(4, 4))
                wait(pe, max_s, s.count(4, g - 1))
                for j in range(4):
                    ins = nc.tensor.matmul(ps_s[g % 2][:, j * P:(j + 1) * P], operand(qs, s, 4 * g + j, STACK),
                                           operand(ks, s, 4 * g + j, STACK), start=True, stop=True)
                ins.then_inc(s_ps, 1)

            def shifted(s, g):
                if g == 0:
                    pe.wait_ge(nmT_s, s.count(1, 1))
                wait(pe, exp_s, s.count(4, g - 1))
                for j in range(4):
                    out = ps_st[g % 2][:, j * P:(j + 1) * P]
                    nc.tensor.matmul(out, operand(ks, s, 4 * g + j, STACK), operand(qs, s, 4 * g + j, STACK), start=True, stop=False)
                    ins = nc.tensor.matmul(out, pick[:, 4 * g + j, :], nmT[:], start=False, stop=True)
                ins.then_inc(st_ps, 1)

            def context(s, g):
                pe.wait_ge(exp_s, s.count(4, g + 1))
                if g == 0:
                    pe.wait_ge(vw_s, s.count(1, 1))
                    wait(pe, ctxT_s, s.count(1, 0))
                for j in range(4):
                    ins = nc.tensor.matmul(ps_ctx[32 * j:32 * j + SLOTW, g * P:(g + 1) * P], v_wide[s.k % 2][:, 4 * g + j, :],
                                           probs[g % 2][:, j, :], start=True, stop=True)
                ins.then_inc(av_s if g < 3 else ctx_ps, 1)

            def emit(s):
                one = s.plus(1).exists()
                if s.exists():
                    shifted(s, 0)
                    if one:
                        scores(s.plus(1), 0)
                        scores(s.plus(1), 1)
                    shifted(s, 1)
                    context(s, 0)
                    shifted(s, 2)
                    if one:
                        scores(s.plus(1), 2)
                    context(s, 1)
                    shifted(s, 3)
                    if one:
                        scores(s.plus(1), 3)
                    context(s, 2)
                if s.plus(-1).exists():
                    pe.wait_ge(ctxT_s, s.count(1, 0))
                    wait(pe, lg_s, s.count(1, -2))
                    for g in range(4):
                        ins = nc.tensor.transpose(ps_ctxT[:, g * P:(g + 1) * P], ctxT[:, g * P:(g + 1) * P], ident[:])
                    ins.then_inc(ctxT_ps, 1)
                if s.plus(-2).exists():
                    pe.wait_ge(xn_s, s.count(1, -1))
                    wait(pe, x1_s, s.count(1, -1))
                    for h in range(HALVES):
                        ins = nc.tensor.transpose(ps_xnT[:, h * P:(h + 1) * P], xn[s.k % 2][:, h * P:(h + 1) * P], ident[:])
                    ins.then_inc(xnT_ps, 1)
                if s.exists():
                    context(s, 3)
                if s.plus(-1).exists():
                    pe.wait_ge(attn_s, s.count(1, 0))
                    wait(pe, nmT_s, min_tile(s.count(1, 1)))
                    for h in range(HALVES):
                        ins = nc.tensor.transpose(ps_aT[:, h * P:(h + 1) * P], attn[:, h * P:(h + 1) * P], ident[:])
                    ins.then_inc(aT_ps, 1)
                if s.plus(-2).exists():
                    pe.wait_ge(xnT_s, s.count(1, -1))
                    for h in range(HALVES):
                        ins = nc.tensor.matmul(ps_lg, wr[:, h, :], xnT[:, h, :], start=(h == 0), stop=(h == HALVES - 1))
                    ins.then_inc(lg_ps, 1)
                if s.plus(-1).exists():
                    pe.wait_ge(aT_s, s.count(1, 0))
                    if s.plus(-2).exists():
                        pe.wait_ge(xnT_s, s.count(1, -1))
                    for h in range(HALVES):
                        ins = nc.tensor.matmul(ps_o, attnT[:, h, :], wo[:, h, :], start=(h == 0), stop=(h == HALVES - 1))
                    ins.then_inc(o_ps, 1)
                if one:
                    max_T(s.plus(1))

            def min_tile(v):
                return min(v, TILES) if isinstance(v, int) else v

            def max_T(s):
                pe.wait_ge(nm_s, s.count(1, 1))
                wait(pe, aT_s, s.count(1, -1))
                nc.tensor.transpose(ps_nmT, nm_parts[:].rearrange("p a h -> p (a h)"), ident_b[:]).then_inc(nmT_ps, 1)

            for g in range(4):
                scores(Step(0, 0), g)
            max_T(Step(0, 0))
            steps(pe, emit, 2)


ROW0 = D + EXPERTS
KEY_BITS = 30
SEG = P // EXPERTS
TOK_T = TOKENS // P


def running_count(nc, mask, tri, ones, ps):
    nc.tensor.matmul(ps[:, 0:EXPERTS * TOK_T], tri[:], mask, start=True, stop=True)
    return nc.tensor.matmul(ps[:, EXPERTS * TOK_T:], ones[:], mask, start=True, stop=True)


def route_top_k(nc, S, T):
    E, TT, N = EXPERTS, TOK_T, EXPERTS * TOK_T
    with ExitStack() as ctx:
        sb = lambda n, s, d=F32: ctx.enter_context(nc.sbuf_tensor(n, s, d))
        sem = ctx.enter_context(Semaphores(nc)).new
        score = S["score"]
        s_et = score[:].rearrange("p t e -> p e t")
        tmax, tsum = sb("tmax", [P, TT]), sb("tsum", [P, TT])
        ex = sb("ex", [P, TT, E])
        keys = sb("keys", [P, 2 * P])
        junk = sb("junk", [P, 2 * P], BF16)
        diff_i = sb("diff_i", [P, P], I32)
        same = sb("same", [P, P], BF16)
        shift_i, one_i, bit_i = (sb(n, [P, KEY_BITS], I32) for n in ("shift_i", "one_i", "bit_i"))
        bit_f = sb("bit_f", [P, KEY_BITS])
        thr, cand, step = (sb(n, [P, 1], I32) for n in ("thr", "cand", "step"))
        count = sb("count", [P, 1], BF16)
        count_f = sb("count_f", [P, 1])
        thr_row = sb("thr_row", [E, P])
        thr_b = sb("thr_b", [P, E])
        above, equal, chosen, early = (sb(n, [P, E, TT], BF16) for n in ("above", "equal", "chosen", "early"))
        scan = sb("scan", [P, E, TT])
        rank = sb("rank", [P, E, TT])
        n_above = sb("n_above", [P, E])
        pos_i, dig_i = sb("pos_i", [P, E, TT], I32), sb("dig_i", [P, 2, E, TT], I32)
        dig = sb("dig", [P, 2, E, TT], BF16)
        ramp_i, ramp = sb("ramp_i", [P, 32], I32), sb("ramp", [P, 32], BF16)
        tile_i, tile_no = sb("tile_i", [P, TT, 16], I32), sb("tile_no", [P, TT, 16], BF16)
        part_i, part_no = sb("part_i", [P, 1], I32), sb("part_no", [P, 1])
        hot_a = [sb(f"hot_a{i}", [P, TT, 32], BF16) for i in range(2)]
        hot_b = [sb(f"hot_b{i}", [P, TT, 16], BF16) for i in range(2)]
        hot_v = [sb(f"hot_v{i}", [P, TT, 2, 16], BF16) for i in range(2)]
        idx_f = sb("idx_f", [32, E, 2, 16])
        idx_i = sb("idx_i", [32, E, 16], I32)
        ps = [ctx.enter_context(nc.psum_tensor(f"pc{i}", [P, 512], F32)) for i in range(6)]
        ps_l, ps_k, ps_n, ps_t, ps_c, ps_i = ps
        (lg_s, mx_s, sub_s, ex_s, sum_s, rec_s, sc_s, keyT_s, key_s, iota_s, tab_s, bit_s, thr0_s, cand_s, cnt_s, cntb_s, tot_s,
         step_s, thr_s, row_s, thrT_s, thrb_s, cmp_s, cnt1_s, red_s, scan_s, off_s, rank_s, early_s, mix_s, ch_s, cnt2_s, pos_s,
         posi_s, dg_s, dgb_s, hot_s, hotb_s, hotv_s, hott_s, idx_ps, idxf_s, idxi_s, out_s, in_s) = (
            sem("pc_" + n) for n in (
                "lg", "mx", "sub", "ex", "sum", "rec", "sc", "keyT", "key", "iota", "tab", "bit", "thr0", "cand", "cnt", "cntb",
                "tot", "step", "thr", "row", "thrT", "thrb", "cmp", "cnt1", "red", "scan", "off", "rank", "early", "mix",
                "ch", "cnt2", "pos", "posi", "dg", "dgb", "hot", "hotb", "hotv", "hott", "idx_ps", "idxf", "idxi", "out", "in"))
        block = ctx.enter_context(nc.Block())

        @block.sync
        def _(sp):
            sp.wait_ge(sc_s, 1)
            sp.dma_start(T["rows0"].rearrange("(t p) d -> p t d", p=P)[:, :, D:ROW0], score[:]).then_inc(out_s, 16)
            sp.wait_ge(out_s, 16)
            sp.wait_ge(idxi_s, 1)
            sp.dma_start(T["idx"].rearrange("(e a b) -> a e b", e=E, a=32), idx_i[:]).then_inc(in_s, 16)
            sp.wait_ge(in_s, 16)
            sp.dma_start(S["idx"][:], T["idx"].rearrange("(e p c) -> p e c", e=E, p=P)).then_inc(in_s, 16)
            sp.wait_ge(in_s, 32)

        @block.gpsimd
        def _(pool):
            nc.gpsimd.iota(diff_i[:], [[-1, P]], base=P, channel_multiplier=1).then_inc(iota_s, 1)
            nc.gpsimd.iota(shift_i[:], [[-1, KEY_BITS]], base=KEY_BITS - 1, channel_multiplier=0).then_inc(iota_s, 1)
            nc.gpsimd.iota(one_i[:], [[0, KEY_BITS]], base=1, channel_multiplier=0).then_inc(iota_s, 1)
            nc.gpsimd.iota(ramp_i[:], [[1, 32]], base=0, channel_multiplier=0).then_inc(iota_s, 1)
            nc.gpsimd.iota(tile_i[:], [[1, TT], [0, 16]], base=0, channel_multiplier=0).then_inc(iota_s, 1)
            nc.gpsimd.iota(part_i[:], [[0, 1]], base=0, channel_multiplier=1).then_inc(iota_s, 1)
            nc.gpsimd.memset(S["ones_b"][:], 1.0).then_inc(tab_s, 1)
            nc.gpsimd.memset(S["before"][:], 1.0).then_inc(tab_s, 1)
            nc.gpsimd.memset(S["keep"][:], 1.0).then_inc(tab_s, 1)
            pool.wait_ge(tab_s, 3)
            nc.gpsimd.affine_select(out=S["before"][:], in_=S["before"][:], compare_op=ALU.is_gt, fill=0.0, base=0,
                                    pattern=[[1, P]], channel_multiplier=-1).then_inc(tab_s, 1)
            nc.gpsimd.affine_select(out=S["keep"][:], in_=S["keep"][:], compare_op=ALU.is_gt, fill=0.0, base=0,
                                    pattern=[[0, E], [1, TT]], channel_multiplier=0).then_inc(tab_s, 1)
            for e in range(E):
                pool.wait_ge(hotb_s, e + 1)
                if e >= 2:
                    pool.wait_ge(idx_ps, e - 1)
                nc.gpsimd.tensor_tensor(hot_v[e % 2][:, :, 1, :], hot_b[e % 2][:], tile_no[:], ALU.mult).then_inc(hott_s, 1)

        @block.scalar
        def _(act):
            act.wait_ge(sub_s, 1)
            nc.scalar.activation(ex[:], ex[:], ACT.Exp).then_inc(ex_s, 1)
            act.wait_ge(keyT_s, 1)
            nc.scalar.activation(keys[:], ps_k[:, 0:2 * P], ACT.Copy).then_inc(key_s, 1)

        @block.vector
        def _(dve):
            V = nc.vector
            dve.wait_ge(iota_s, 6)
            V.tensor_scalar(diff_i[:], diff_i[:], E - 1, None, ALU.bitwise_and).then_inc(bit_s, 1)
            V.tensor_tensor(bit_i[:], one_i[:], shift_i[:], ALU.logical_shift_left).then_inc(bit_s, 1)
            dve.wait_ge(bit_s, 2)
            V.tensor_scalar(same[:], diff_i[:], 0.0, None, ALU.is_equal).then_inc(bit_s, 1)
            V.tensor_copy(bit_f[:], bit_i[:]).then_inc(bit_s, 1)
            V.tensor_copy(ramp[:], ramp_i[:]).then_inc(bit_s, 1)
            V.tensor_copy(tile_no[:], tile_i[:]).then_inc(bit_s, 1)
            V.tensor_copy(part_no[:], part_i[:]).then_inc(bit_s, 1)
            V.memset(thr[:], 0).then_inc(bit_s, 1)
            dve.wait_ge(lg_s, 1)
            lg = ps_l[:, 0:N].rearrange("p (t e) -> p t e", e=E)
            V.tensor_reduce(tmax[:], lg, AX.X, ALU.max).then_inc(mx_s, 1)
            dve.wait_ge(mx_s, 1)
            V.tensor_tensor(ex[:], lg, tmax[:].unsqueeze(2).broadcast_to([P, TT, E]), ALU.subtract).then_inc(sub_s, 1)
            dve.wait_ge(ex_s, 1)
            V.tensor_reduce(tsum[:], ex[:], AX.X, ALU.add).then_inc(sum_s, 1)
            dve.wait_ge(sum_s, 1)
            V.reciprocal(tsum[:], tsum[:]).then_inc(rec_s, 1)
            dve.wait_ge(rec_s, 1)
            V.tensor_tensor(score[:], ex[:], tsum[:].unsqueeze(2).broadcast_to([P, TT, E]), ALU.mult).then_inc(sc_s, 1)

            dve.wait_ge(key_s, 1)
            dve.wait_ge(bit_s, 8)
            with dve.Fori(0, KEY_BITS) as i:
                bit = bass.ds(i, 1)
                V.tensor_tensor(cand[:], thr[:], bit_i[:, bit], ALU.bitwise_or).then_inc(cand_s, 1)
                dve.wait_ge(cand_s, i + 1)
                V.tensor_scalar(junk[:], keys[:], cand[:].bitcast(F32), None, ALU.is_ge, ALU.add,
                                accum_out=count_f[:]).then_inc(cnt_s, 1)
                dve.wait_ge(cnt_s, i + 1)
                V.tensor_copy(count[:], count_f[:]).then_inc(cntb_s, 1)
                dve.wait_ge(tot_s, i + 1)
                V.tensor_scalar(step[:], ps_n[:, 0:1], CAP - 0.5, bit_f[:, bit], ALU.is_ge, ALU.mult).then_inc(step_s, 1)
                dve.wait_ge(step_s, i + 1)
                V.tensor_tensor(thr[:], thr[:], step[:], ALU.bitwise_or).then_inc(thr_s, 1)
                dve.wait_ge(thr_s, i + 1)

            V.tensor_copy(thr_row[:], thr[0:E, :].bitcast(F32).broadcast_to([E, P])).then_inc(row_s, 1)
            dve.wait_ge(thrT_s, 1)
            V.tensor_copy(thr_b[:], ps_t[:, 0:E]).then_inc(thrb_s, 1)
            dve.wait_ge(thrb_s, 1)
            thr_et = thr_b[:].unsqueeze(2).broadcast_to([P, E, TT])
            V.tensor_tensor(above[:], s_et, thr_et, ALU.is_gt).then_inc(cmp_s, 1)
            V.tensor_tensor(equal[:], s_et, thr_et, ALU.is_equal).then_inc(cmp_s, 1)

            def ranks(ps_c, done):
                tot = ps_c[:, N:]
                V.tensor_tensor_scan(scan[:].rearrange("p e t -> p (e t)"), S["keep"][:].rearrange("p e t -> p (e t)"), tot, 0.0,
                                     ALU.mult, ALU.add).then_inc(scan_s, 1)
                dve.wait_ge(scan_s, done + 1)
                V.tensor_tensor(scan[:], scan[:], tot.rearrange("p (e t) -> p e t", e=E), ALU.subtract).then_inc(off_s, 1)
                dve.wait_ge(off_s, done + 1)
                V.tensor_tensor(rank[:], scan[:], ps_c[:, 0:N].rearrange("p (e t) -> p e t", e=E), ALU.add).then_inc(rank_s, 1)
                dve.wait_ge(rank_s, done + 1)

            dve.wait_ge(cnt1_s, 1)
            dve.wait_ge(tab_s, 5)
            V.tensor_reduce(n_above[:], ps_t[:, N:2 * N].rearrange("p (e t) -> p e t", e=E), AX.X, ALU.add).then_inc(red_s, 1)
            ranks(ps_c, 0)
            dve.wait_ge(red_s, 1)
            V.tensor_tensor(rank[:], rank[:], n_above[:].unsqueeze(2).broadcast_to([P, E, TT]), ALU.add).then_inc(early_s, 1)
            dve.wait_ge(early_s, 1)
            V.scalar_tensor_tensor(early[:].rearrange("p e t -> p (e t)"), rank[:].rearrange("p e t -> p (e t)"), CAP - 0.5,
                                   equal[:].rearrange("p e t -> p (e t)"), ALU.is_lt, ALU.mult).then_inc(mix_s, 1)
            dve.wait_ge(mix_s, 1)
            V.tensor_tensor(chosen[:], early[:], above[:], ALU.add).then_inc(ch_s, 1)
            dve.wait_ge(cnt2_s, 1)
            ranks(ps_i, 1)
            V.tensor_scalar(rank[:], rank[:], 2.0 * TOKENS, None, ALU.add).then_inc(pos_s, 1)
            dve.wait_ge(pos_s, 1)
            V.scalar_tensor_tensor(pos_i[:].rearrange("p e t -> p (e t)"), chosen[:].rearrange("p e t -> p (e t)"), -2.0 * TOKENS,
                                   rank[:].rearrange("p e t -> p (e t)"), ALU.mult, ALU.add).then_inc(posi_s, 1)
            dve.wait_ge(posi_s, 1)
            V.tensor_scalar(dig_i[:, 0], pos_i[:], 4, None, ALU.logical_shift_right).then_inc(dg_s, 1)
            V.tensor_scalar(dig_i[:, 1], pos_i[:], 15, None, ALU.bitwise_and).then_inc(dg_s, 1)
            dve.wait_ge(dg_s, 2)
            V.tensor_copy(dig[:], dig_i[:]).then_inc(dgb_s, 1)
            dve.wait_ge(dgb_s, 1)
            for e in range(E):
                par = e % 2
                if e >= 2:
                    dve.wait_ge(idx_ps, e - 1)
                    dve.wait_ge(hott_s, e - 1)
                V.tensor_tensor(hot_b[par][:], ramp[:, 0:16].unsqueeze(1).broadcast_to([P, TT, 16]),
                                dig[:, 1, e, :].unsqueeze(2).broadcast_to([P, TT, 16]), ALU.is_equal).then_inc(hotb_s, 1)
                V.tensor_tensor(hot_a[par][:], ramp[:].unsqueeze(1).broadcast_to([P, TT, 32]),
                                dig[:, 0, e, :].unsqueeze(2).broadcast_to([P, TT, 32]), ALU.is_equal).then_inc(hot_s, 1)
                dve.wait_ge(hotb_s, e + 1)
                V.tensor_scalar(hot_v[par][:, :, 0, :], hot_b[par][:], part_no[:], None, ALU.mult).then_inc(hotv_s, 1)
            dve.wait_ge(idx_ps, E)
            V.tensor_copy(idx_f[:], ps_n[0:32, 0:E * 32].rearrange("a (e v b) -> a e v b", e=E, v=2)).then_inc(idxf_s, 1)
            dve.wait_ge(idxf_s, 1)
            V.scalar_tensor_tensor(idx_i[:], idx_f[:, :, 1, :], float(P), idx_f[:, :, 0, :], ALU.mult, ALU.add).then_inc(idxi_s, 1)

        @block.tensor
        def _(pe):
            for t in range(TT):
                ins = nc.tensor.transpose(ps_l[:, t * E:(t + 1) * E], S["logitsT"][:, t * P:(t + 1) * P], S["ident"][0:E, 0:E])
            ins.then_inc(lg_s, 1)
            pe.wait_ge(sc_s, 1)
            for j in range(2):
                ins = nc.tensor.transpose(ps_k[:, j * P:(j + 1) * P], score[:, j * SEG:(j + 1) * SEG, :].rearrange("p t e -> p (t e)"),
                                          S["ident"][:])
            ins.then_inc(keyT_s, 1)
            pe.wait_ge(bit_s, 8)
            with pe.Fori(0, KEY_BITS) as i:
                pe.wait_ge(cntb_s, i + 1)
                nc.tensor.matmul(ps_n[:, 0:1], same[:], count[:], start=True, stop=True).then_inc(tot_s, 1)
            pe.wait_ge(row_s, 1)
            nc.tensor.transpose(ps_t[:, 0:E], thr_row[:], S["ident"][0:E, 0:E]).then_inc(thrT_s, 1)
            pe.wait_ge(cmp_s, 2)
            pe.wait_ge(tab_s, 5)
            pe.wait_ge(thrb_s, 1)
            flat = lambda m: m[:].rearrange("p e t -> p (e t)")
            nc.tensor.matmul(ps_t[:, N:2 * N], S["ones_b"][:], flat(above), start=True, stop=True)
            running_count(nc, flat(equal), S["before"], S["ones_b"], ps_c).then_inc(cnt1_s, 1)
            pe.wait_ge(ch_s, 1)
            running_count(nc, flat(chosen), S["before"], S["ones_b"], ps_i).then_inc(cnt2_s, 1)
            for e in range(E):
                pe.wait_ge(hot_s, e + 1)
                pe.wait_ge(hotv_s, e + 1)
                pe.wait_ge(hott_s, e + 1)
                for t in range(TT):
                    ins = nc.tensor.matmul(ps_n[0:32, e * 32:(e + 1) * 32], hot_a[e % 2][:, t, :],
                                           hot_v[e % 2][:, t].rearrange("p v b -> p (v b)"), start=(t == 0), stop=(t == TT - 1))
                ins.then_inc(idx_ps, 1)


def expert_choice_ffn(nc, S, T):
    MT = -(-FFN // P)
    LAST = FFN - (MT - 1) * P
    GROUPS = EXPERTS // 2
    ST = CAP // P
    with ExitStack() as ctx:
        sb = lambda n, s, d=F32: ctx.enter_context(nc.sbuf_tensor(n, s, d))
        sem = ctx.enter_context(Semaphores(nc)).new
        ident = S["ident"]
        rows = [sb(f"rows{i}", [P, ST, ROW0]) for i in range(2)]
        gate = [sb(f"gate{i}", [P, ST]) for i in range(2)]
        gT = [sb(f"gT{i}", [P, HALVES, CAP]) for i in range(2)]
        w_up = sb("w_up", [P, HALVES, FFN])
        b_up = sb("b_up", [P, MT])
        w_dn = [sb(f"w_dn{i}", [P, MT, D]) for i in range(2)]
        mid = [[sb(f"mid{i}_{m}", [P if m < MT - 1 else 64, CAP]) for m in range(MT)] for i in range(2)]
        y = [sb(f"y{i}", [P, ST, D]) for i in range(2)]
        banks = [ctx.enter_context(nc.psum_tensor(f"pd{i}", [P, 512], F32)) for i in range(8)]
        ps_t, ps_y = banks[0:2], banks[2:4]
        ps_u = banks[4:8]
        rows_in = [sem(f"pd_rows{i}") for i in range(2)]
        dn_in = [sem(f"pd_dn{i}") for i in range(2)]
        up_in = sem("pd_up")
        added = sem("pd_added")
        one_s, t_ps, gT_s, gate_s, u_ps, mid_s, y_ps, y_s, b_in = (sem("pd_" + n) for n in (
            "one", "t_ps", "gT", "gate", "u_ps", "mid", "y_ps", "y", "b_in"))
        block = ctx.enter_context(nc.Block())

        def groups(engine, emit):
            emit(0, True, False)
            with engine.Fori(1, GROUPS - 1) as g:
                emit(g, False, False)
            emit(GROUPS - 1, False, True)

        @block.sync
        def _(sp):
            sp.wait_ge(one_s, 2)

            def emit(g, first, last):
                if not first:
                    sp.wait_ge(u_ps, g * 2 * MT)
                sp.dma_start(w_up[:], T["W_up"][bass.ds(g, 1)].rearrange("a (h p) f -> p (a h) f", p=P)).then_inc(up_in, 16)
                if not first:
                    sp.wait_ge(mid_s, g * 2 * MT)
                sp.dma_start(b_up[:, 0:MT - 1], T["b_up"][bass.ds(g, 1), 0:(MT - 1) * P].rearrange("a (m p) -> p (a m)", p=P),
                             allow_slow_non_contiguous=True).then_inc(b_in, 16)
                sp.dma_start(b_up[0:LAST, MT - 1:MT], T["b_up"][bass.ds(g, 1), (MT - 1) * P:].rearrange("a p -> p a"),
                             allow_slow_non_contiguous=True).then_inc(b_in, 16)
                for par in range(2):
                    if not first:
                        sp.wait_ge(y_ps, (g * 2 + (par - 1)) * (ST // 2))
                    e = bass.ds(g * 2 + par, 1)
                    sp.dma_start(w_dn[par][:, 0:MT - 1, :], T["W_down"][e, 0:(MT - 1) * P].rearrange("a (m p) d -> p (a m) d", p=P)
                                 ).then_inc(dn_in[par], 16)
                    sp.dma_start(w_dn[par][0:LAST, MT - 1, :], T["W_down"][e, (MT - 1) * P:].rearrange("a p d -> p (a d)")
                                 ).then_inc(dn_in[par], 16)
                    sp.dma_start(w_dn[par][LAST:LAST + 1, MT - 1, :], T["b_down"][e]).then_inc(dn_in[par], 16)

            groups(sp, emit)

        @block.gpsimd
        def _(pool):
            def gather(e, par, first):
                if not first:
                    pool.wait_ge(t_ps, e - 1)
                    pool.wait_ge(gate_s, e - 1)
                for c in range(ST):
                    pool.indirect_dma_start(
                        out=rows[par][:, c, :], out_offset=None, in_=T["rows0"],
                        in_offset=bass.IndirectOffsetOnAxis(ap=S["idx"][:, e, c:c + 1], axis=0)).then_inc(rows_in[par], 16)

            def add(e, par):
                pool.wait_ge(y_s, (e + 1) * ST)
                if e:
                    pool.wait_ge(added, e * 16 * ST)
                for c in range(ST):
                    pool.indirect_dma_start(
                        out=T["resid"], out_offset=bass.IndirectOffsetOnAxis(ap=S["idx"][:, e, c:c + 1], axis=0),
                        in_=y[par][:, c, :], in_offset=None, compute_op=ALU.add).then_inc(added, 16)

            gather(0, 0, True)
            gather(1, 1, True)
            for e in range(EXPERTS):
                add(e, e % 2)
                if e + 2 < EXPERTS:
                    gather(e + 2, e % 2, False)
            pool.wait_ge(added, EXPERTS * 16 * ST)

        @block.vector
        def _(dve):
            for i in range(2):
                nc.vector.memset(mid[i][MT - 1][:], 1.0).then_inc(one_s, 1)

            def emit(g, first, last):
                for par in range(2):
                    e = g * 2 + par
                    dve.wait_ge(t_ps, e + 1)
                    if not first:
                        dve.wait_ge(u_ps, (e - 1) * MT)
                    nc.vector.tensor_copy(gT[par][:, 1, :], ps_t[1][:]).then_inc(gT_s, 1)
                    dve.wait_ge(rows_in[par], (g + 1) * 16 * ST)
                    nc.vector.tensor_scalar(gate[par][:], rows[par][:, :, bass.ds(g * 2 + (D + par), 1)].rearrange("p c a -> p (c a)"),
                                            S["tanh_g"][:, 2:3], None, ALU.mult).then_inc(gate_s, 1)
                    dve.wait_ge(gate_s, e + 1)
                    for c in range(ST):
                        if c % 2 == 0:
                            dve.wait_ge(y_ps, e * (ST // 2) + (c // 2 + 1))
                        if not first and c == 0:
                            dve.wait_ge(added, (e - 1) * 16 * ST)
                        nc.vector.tensor_scalar(y[par][:, c, :], ps_y[c // 2][:, c % 2 * D:(c % 2 + 1) * D], gate[par][:, c:c + 1],
                                                None, ALU.mult).then_inc(y_s, 1)

            groups(dve, emit)

        @block.scalar
        def _(act):
            act.wait_ge(one_s, 2)

            def emit(g, first, last):
                for par in range(2):
                    e = g * 2 + par
                    act.wait_ge(t_ps, e + 1)
                    if not first:
                        act.wait_ge(u_ps, (e - 1) * MT)
                    nc.scalar.activation(gT[par][:, 0, :], ps_t[0][:], ACT.Copy).then_inc(gT_s, 1)
                    act.wait_ge(b_in, (g + 1) * 32)
                    for m in range(MT):
                        n = P if m < MT - 1 else LAST
                        act.wait_ge(u_ps, e * MT + (m + 1))
                        if not first:
                            act.wait_ge(y_ps, (e - 1) * (ST // 2))
                        nc.scalar.activation(mid[par][m][0:n, :], ps_u[(par * MT + m) % 4][0:n, :], ACT.Silu,
                                             bias=b_up[0:n, m:m + 1]).then_inc(mid_s, 1)

            groups(act, emit)

        @block.tensor
        def _(pe):
            def turn(e, par, n16, first):
                pe.wait_ge(rows_in[par], n16)
                if not first:
                    pe.wait_ge(gT_s, e * 2)
                for h in range(HALVES):
                    for c in range(ST):
                        ins = nc.tensor.transpose(ps_t[h][:, c * P:(c + 1) * P], rows[par][:, c, h * P:(h + 1) * P], ident[:])
                ins.then_inc(t_ps, 1)

            def up(g, e, par, first):
                pe.wait_ge(up_in, (g + 1) * 16)
                pe.wait_ge(gT_s, (e + 1) * 2)
                for m in range(MT):
                    n = P if m < MT - 1 else LAST
                    k = par * MT + m
                    if not (first and k < 4):
                        pe.wait_ge(mid_s, e * MT + (m - 3))
                    for h in range(HALVES):
                        ins = nc.tensor.matmul(ps_u[k % 4][0:n, :], w_up[:, h, m * P:m * P + n], gT[par][:, h, :],
                                               start=(h == 0), stop=(h == HALVES - 1))
                    ins.then_inc(u_ps, 1)

            def down(g, e, par, first):
                pe.wait_ge(dn_in[par], (g + 1) * 48)
                pe.wait_ge(mid_s, (e + 1) * MT)
                for c in range(ST):
                    if c == 0 and not (first and par == 0):
                        pe.wait_ge(y_s, e * ST)
                    for m in range(MT):
                        n = P if m < MT - 1 else LAST + 1
                        ins = nc.tensor.matmul(ps_y[c // 2][:, c % 2 * D:(c % 2 + 1) * D], mid[par][m][0:n, c * P:(c + 1) * P],
                                               w_dn[par][0:n, m, :], start=(m == 0), stop=(m == MT - 1))
                    if c % 2:
                        ins.then_inc(y_ps, 1)

            def emit(g, first, last):
                for par in range(2):
                    e = g * 2 + par
                    up(g, e, par, first)
                    if not (last and par == 1):
                        turn(e + 1, 1 - par, (g + (1 + par)) * 16 * ST, False)
                    down(g, e, par, first)

            turn(0, 0, 16 * ST, True)
            groups(pe, emit)


ROW1 = D + 4
DROPPED = 2 * TOKENS


def deep_steps(engine, emit, head, tail):
    for k in range(-head, 8):
        emit(Step(0, k))
    with engine.Fori(2, TILES // 4 - 1) as base:
        for k in range(4):
            emit(Step(base, k))
    for k in range(4 + tail):
        emit(Step(TILES // 4 - 1, k))


def bidirectional_attention(nc, S, T):
    E, HEAD, TAIL = EXPERTS, 3, 8
    with ExitStack() as ctx:
        sb = lambda n, s, d=F32: ctx.enter_context(nc.sbuf_tensor(n, s, d))
        four = lambda n, s, d=F32: [sb(f"{n}{i}", s, d) for i in range(4)]
        sem = ctx.enter_context(Semaphores(nc)).new
        ident = S["ident"]
        w_f = sb("w_f", [P, 4, HALVES, D])
        w_sim = sb("w_sim", [P, 3, HALVES])
        w1_row, b_sim = sb("w1_row", [P, D]), sb("b_sim", [P, 1])
        b_qv = sb("b_qv", [P, D])
        wg = sb("wg", [P, HALVES, EXPERTS])
        x_in, c_in, xb = four("dx_in", [P, D]), four("dc_in", [P, D]), four("dxb", [P, D])
        enc = four("enc", [P, D + 1])
        stats, moments = four("d_stats", [P, 6]), four("d_moments", [P, 2])
        vareps, rstd = four("d_vareps", [P, 1]), four("d_rstd", [P, 1])
        stats4, moments4 = four("d_stats4", [P, 6]), four("d_moments4", [P, 2])
        vareps4 = four("d_vareps4", [P, 1])
        encT, encW, hqT, ehqT = (four(n, [P, HALVES, P]) for n in ("encT", "encW", "hqT", "ehqT"))
        cT = four("d_cT", [P, HALVES, P])
        neg_max, row_sum, inv = four("d_neg_max", [P, 1]), four("d_row_sum", [P, 1]), four("d_inv", [P, 1])
        a_w, a_n, aT = four("a_w", [P, P]), four("a_n", [P, P]), four("d_aT", [P, P])
        prod = four("d_prod", [P, D])
        s1, v, v_max, v_sub, v_exp = (four("d_" + n, [P, 1]) for n in ("s1", "v", "vmax", "vsub", "vexp"))
        inv_b, hc_row, hc_col = four("d_inv_b", [1, 1]), four("d_hc_row", [1, D]), four("d_hc_col", [P, HALVES])
        w_c = four("d_w_c", [P, HALVES, D])
        row4 = four("d_row4", [P, D + 2])
        xn4, x4T = four("d_xn4", [P, D]), four("d_x4T", [P, HALVES, P])
        rows = sb("d_rows", [P, TILES, ROW1])
        lgT = sb("r_lgT", [EXPERTS, QUAD, P])
        prob, first = sb("r_prob", [P, QUAD, E]), sb("r_first", [P, QUAD, E])
        rev_i, rev = sb("r_rev_i", [P, QUAD, E], I32), sb("r_rev", [P, QUAD, E])
        base_i, base = sb("r_base_i", [P, QUAD, E], I32), sb("r_base", [P, QUAD, E])
        tok_i = sb("r_tok_i", [P, TILES], I32)
        tmax, tsum, inv_e, pmax, best = (sb("r_" + n, [P, QUAD]) for n in ("tmax", "tsum", "inv", "pmax", "best"))
        chosen = sb("r_chosen", [P, QUAD, E], BF16)
        seen = sb("r_seen", [P, E])
        rank, kept, place = sb("r_rank", [P, QUAD, E]), sb("r_kept", [P, QUAD, E]), sb("r_place", [P, QUAD, E])
        slot = sb("r_slot", [P, QUAD])
        dest = sb("r_dest", [P, QUAD, 1], I32)
        pool_spare = sb("r_pool_spare", [P, 1])
        ps = [ctx.enter_context(nc.psum_tensor(f"pe{i}", [P, 512], F32)) for i in range(8)]
        ps_t, ps_sim, ps_route, ps_hq, ps_out, ps_row, ps_col, ps_x4 = ps
        ps_a, ps_lg = ps_sim, ps_x4
        w_s, one_s, thb_s, tab_s = sem("pe_w"), sem("pe_one"), sem("pe_thb"), sem("pe_tab")
        x_in_s, c_in_s = [sem(f"pe_xin{i}") for i in range(4)], [sem(f"pe_cin{i}") for i in range(4)]
        (t_ps, enc_s, encT_s, cT_s, encW_s, sim_ps, max_s, exp_s, inv_s, an_s, a_ps, aT_s, hq_ps, hqT_s, ehqT_s, prod_s, s1_s, v_s,
         vmax_s, vsub_s, vexp_s, row_ps, invb_s, row_s, col_ps, col_s, wc_s, out_ps, x3_s, st_s, mom_s, ve_s, rstd_s, st4_s,
         mom4_s, ve4_s, rstd4_s, xn4_s, x4_ps, x4T_s, lg_ps, lg_s, xb_s, keep_s, stored_s) = (sem("pe_" + n) for n in (
            "t_ps", "enc", "encT", "cT", "encW", "sim_ps", "max", "exp", "inv", "an", "a_ps", "aT", "hq_ps", "hqT", "ehqT",
            "prod", "s1", "v", "vmax", "vsub", "vexp", "row_ps", "invb", "row", "col_ps", "col", "wc", "out_ps", "x3", "st", "mom", "ve",
            "rstd", "st4", "mom4", "ve4", "rstd4", "xn4", "x4_ps", "x4T", "lg_ps", "lg", "xb", "keep", "stored"))
        lt_ps, sub_s, pexp_s, chosen_s, cnt_ps, dest_s, sent_s, free_s, chain = (sem("pr_" + n) for n in (
            "lt_ps", "sub", "exp", "chosen", "cnt_ps", "dest", "sent", "free", "chain"))
        block = ctx.enter_context(nc.Block())
        x_t = T["resid"].rearrange("(t p) d -> p t d", p=P)
        c_t = T["ctx"].rearrange("(t p) d -> p t d", p=P)
        out_t = T["out"].rearrange("(t p) d -> p t d", p=P)
        one = lambda ap: ap.rearrange("p a d -> p (a d)")

        def quad_of(s, k):
            return s.plus(-k)

        def at(u, per, extra):
            return u.base * per + (u.k // 4 * per + extra)

        @block.sync
        def _(sp):
            def load(s):
                slot4 = s.k % 4
                wait(sp, enc_s, s.count(1, -3))
                wait(sp, xb_s, s.count(1, -3))
                sp.dma_start(x_in[slot4][:], one(x_t[:, bass.ds(s.tile(), 1), :])).then_inc(x_in_s[slot4], 16)
                wait(sp, hq_ps, s.count(1, -3))
                sp.dma_start(c_in[slot4][:], one(c_t[:, bass.ds(s.tile(), 1), :])).then_inc(c_in_s[slot4], 16)

            load(Step(0, 0))
            load(Step(0, 1))
            sp.dma_start(w1_row[:], T["w_sim"][0:D].partition_broadcast(P)).then_inc(w_s, 16)
            sp.dma_start(w_sim[:], T["w_sim"].rearrange("(w h p) -> p w h", p=P, h=HALVES), allow_slow_non_contiguous=True).then_inc(w_s, 16)
            sp.dma_start(b_sim[:], T["b_sim"].partition_broadcast(P)).then_inc(w_s, 16)
            sp.dma_start(b_qv[:], T["b_qv"].partition_broadcast(P)).then_inc(w_s, 16)
            sp.dma_start(wg[:], T["wg"].rearrange("(h p) n -> p h n", p=P)).then_inc(w_s, 16)
            sp.dma_start(w_f[:], T["W_qv"].rearrange("(b h p) n -> p b h n", p=P, h=HALVES)).then_inc(w_s, 16)
            load(Step(0, 2))
            load(Step(0, 3))

            def emit(s):
                if s.exists() and s.plus(4).exists():
                    load(s.plus(4))
                u = quad_of(s, 7)
                if s.k % 4 == 3 and u.exists():
                    sp.wait_ge(keep_s, u.count(1, 4))
                    sp.dma_start(out_t[:, bass.ds(u.tile(), QUAD), :], rows[:, bass.ds(u.tile(), QUAD), 0:D]).then_inc(stored_s, 16)

            deep_steps(sp, emit, 0, TAIL)
            sp.wait_ge(stored_s, 16 * TILES // QUAD)

        @block.gpsimd
        def _(pool):
            G = nc.gpsimd
            for i in range(4):
                G.memset(enc[i][:, D:D + 1], 1.0).then_inc(one_s, 1)
            G.iota(rev_i[:], [[0, QUAD], [-1, E]], base=E, channel_multiplier=0).then_inc(tab_s, 1)
            G.iota(base_i[:], [[0, QUAD], [CAP, E]], base=-DROPPED, channel_multiplier=0).then_inc(tab_s, 1)
            G.iota(tok_i[:], [[-P, TILES]], base=TOKENS, channel_multiplier=-1).then_inc(tab_s, 1)

            def power(u, mom, mom_sem, ve, ve_sem, out, out_sem):
                pool.wait_ge(mom_sem, u.count(1, 1))
                G.tensor_tensor(ve[u.k % 4][:], mom[u.k % 4][:, 1:2], S["eps"][:, 0:1], ALU.add).then_inc(ve_sem, 1)
                pool.wait_ge(ve_sem, u.count(1, 1))
                G.tensor_tensor(out[u.k % 4], ve[u.k % 4][:], S["minus_half"][:, 0:1], ALU.pow).then_inc(out_sem, 1)

            rstd_out = [t[:] for t in rstd]
            rstd4_out = [t[:, D + 1:D + 2] for t in row4]

            def emit(s):
                slot4 = s.k % 4
                if s.exists():
                    pool.wait_ge(v_s, s.count(1, 1))
                    pool.wait_ge(x_in_s[slot4], s.dma(4))
                    wait(pool, x3_s, s.count(1, -3))
                    G.tensor_tensor(xb[slot4][:], x_in[slot4][:], b_qv[:], ALU.add).then_inc(xb_s, 1)
                    G.partition_all_reduce(v_max[slot4][:], v[slot4][:], P, REDUCE_MAX).then_inc(vmax_s, 1)
                u = s.plus(3)
                if u.exists():
                    power(u, moments, mom_s, vareps, ve_s, rstd_out, rstd_s)
                u = s.plus(2)
                if u.exists():
                    pool.wait_ge(enc_s, u.count(1, 1))
                    wait(pool, s1_s, u.count(1, -3))
                    G.tensor_tensor(prod[u.k % 4][:], enc[u.k % 4][:, 0:D], w1_row[:], ALU.mult).then_inc(prod_s, 1)
                u = s.plus(-2)
                if u.exists():
                    power(u, moments4, mom4_s, vareps4, ve4_s, rstd4_out, rstd4_s)
                u = quad_of(s, 12)
                if s.k % 4 == 0 and u.exists():
                    pool.wait_ge(sent_s, at(u, 16 * QUAD, 16 * QUAD))
                    G.memset(pool_spare[:], 0.0).then_inc(free_s, 1)
                for k in (2, 3):
                    u = quad_of(s, 8 + k)
                    if s.k % 4 == k and u.exists():
                        pool.wait_ge(dest_s, at(u, 1, 1))
                        for j in (2 * k - 4, 2 * k - 3):
                            pool.indirect_dma_start(out=T["slots"], out_offset=bass.IndirectOffsetOnAxis(ap=dest[:, j, :], axis=0),
                                                    in_=rows[:, u.tile() + j, :], in_offset=None,
                                                    bounds_check=TOKENS - 1, oob_is_err=False).then_inc(sent_s, 16)

            G.memset(pool_spare[:], 0.0).then_inc(free_s, 1)
            pool.wait_ge(w_s, 96)
            G.tensor_scalar(b_qv[:], b_qv[:], S["tanh_g"][:, 1:2], None, ALU.mult).then_inc(thb_s, 1)
            pool.wait_ge(thb_s, 1)
            for tile in range(-HEAD, TILES + TAIL):
                emit(Step(0, tile))
            pool.wait_ge(sent_s, 16 * TILES)

        @block.vector
        def _(dve):
            V = nc.vector

            def statistics(u):
                i = u.k % 4
                dve.wait_ge(x_in_s[i], u.dma(4))
                V.bn_stats(stats[i][:], x_in[i][:]).then_inc(st_s, 1)
                settle(nc, S, dve, st_s, u.count(1, 1))
                V.bn_aggr(moments[i][:], stats[i][:]).then_inc(mom_s, 1)

            def normalise(u):
                i = u.k % 4
                dve.wait_ge(mom_s, u.count(1, 1))
                dve.wait_ge(rstd_s, u.count(1, 1))
                V.tensor_scalar(enc[i][:, 0:D], x_in[i][:], moments[i][:, 0:1], rstd[i][:],
                                ALU.subtract, ALU.mult).then_inc(enc_s, 1)

            def dot_w1(u):
                dve.wait_ge(prod_s, u.count(1, 1))
                V.tensor_reduce(s1[u.k % 4][:], prod[u.k % 4][:], AX.X, ALU.add).then_inc(s1_s, 1)

            def weigh(u):
                dve.wait_ge(encT_s, u.count(1, 1))
                for h in range(HALVES):
                    V.tensor_scalar(encW[u.k % 4][:, h, :], encT[u.k % 4][:, h, :], w_sim[:, 2, h:h + 1], w_sim[:, 1, h:h + 1],
                                    ALU.mult, ALU.add).then_inc(encW_s, 1)

            def row_max(u):
                i = u.k % 4
                dve.wait_ge(sim_ps, u.count(1, 1))
                V.tensor_reduce(neg_max[i][:], ps_sim[:, 0:P], AX.X, ALU.max, negate=True).then_inc(max_s, 1)
                dve.wait_ge(s1_s, u.count(1, 1))
                dve.wait_ge(max_s, u.count(1, 1))
                V.tensor_scalar(v[i][:], s1[i][:], b_sim[:], neg_max[i][:], ALU.add, ALU.subtract).then_inc(v_s, 1)

            def sub_max(u):
                i = u.k % 4
                dve.wait_ge(vmax_s, u.count(1, 1))
                V.tensor_tensor(v_sub[i][:], v[i][:], v_max[i][:], ALU.subtract).then_inc(vsub_s, 1)

            def context_row(u):
                i = u.k % 4
                dve.wait_ge(row_ps, u.count(1, 1))
                V.reciprocal(inv_b[i][:], ps_row[0:1, D:D + 1]).then_inc(invb_s, 1)
                dve.wait_ge(invb_s, u.count(1, 1))
                V.tensor_scalar(hc_row[i][:], ps_row[0:1, 0:D], inv_b[i][:], None, ALU.mult).then_inc(row_s, 1)

            def fold(u):
                i = u.k % 4
                dve.wait_ge(col_ps, u.count(1, 1))
                V.tensor_copy(hc_col[i][:], ps_col[:, 0:HALVES]).then_inc(col_s, 1)
                dve.wait_ge(col_s, u.count(1, 1))
                for h in range(HALVES):
                    V.scalar_tensor_tensor(w_c[i][:, h, :], w_f[:, 3, h, :], hc_col[i][:, h:h + 1], w_f[:, 0, h, :],
                                           ALU.mult, ALU.add).then_inc(wc_s, 1)

            def scale_a(u):
                i = u.k % 4
                dve.wait_ge(exp_s, u.count(1, 1))
                V.reciprocal(inv[i][:], row_sum[i][:]).then_inc(inv_s, 1)
                dve.wait_ge(inv_s, u.count(1, 1))
                V.tensor_scalar(a_n[i][:], a_w[i][:], inv[i][:], None, ALU.mult).then_inc(an_s, 1)

            def product(u):
                i = u.k % 4
                dve.wait_ge(hqT_s, u.count(1, 1))
                V.tensor_tensor(ehqT[i][:], hqT[i][:], encT[i][:], ALU.mult).then_inc(ehqT_s, 1)

            def residual(u):
                i = u.k % 4
                dve.wait_ge(out_ps, u.count(1, 1))
                dve.wait_ge(xb_s, u.count(1, 1))
                wait(dve, keep_s, u.count(1, -3))
                V.scalar_tensor_tensor(row4[i][:, 0:D], ps_out[:, 0:D], S["tanh_g"][:, 1:2], xb[i][:], ALU.mult, ALU.add).then_inc(x3_s, 1)
                dve.wait_ge(x3_s, u.count(1, 1))
                V.bn_stats(stats4[i][:], row4[i][:, 0:D]).then_inc(st4_s, 1)

            def aggregate(u):
                i = u.k % 4
                settle(nc, S, dve, st4_s, u.count(1, 1))
                V.bn_aggr(moments4[i][:], stats4[i][:]).then_inc(mom4_s, 1)

            def normalise4(u):
                i = u.k % 4
                dve.wait_ge(mom4_s, u.count(1, 1))
                dve.wait_ge(rstd4_s, u.count(1, 1))
                V.tensor_copy(row4[i][:, D:D + 1], moments4[i][:, 0:1])
                V.tensor_scalar(xn4[i][:], row4[i][:, 0:D], moments4[i][:, 0:1], row4[i][:, D + 1:D + 2],
                                ALU.subtract, ALU.mult).then_inc(xn4_s, 1)

            LINKS = 14
            over_e = lambda m: m[:].unsqueeze(2).broadcast_to([P, QUAD, E])
            flat = lambda m: m[:].rearrange("p t e -> p (t e)")
            route = lambda i: ps_route[:, i * QUAD * E:(i + 1) * QUAD * E].rearrange("p (t e) -> p t e", e=E)

            def link(u, i, ins):
                ins.then_inc(chain, 1)
                dve.wait_ge(chain, at(u, LINKS, i))

            def route_shift(u):
                dve.wait_ge(lt_ps, at(u, 1, 1))
                link(u, 1, V.tensor_reduce(tmax[:], route(0), AX.X, ALU.max))
                V.tensor_tensor(prob[:], route(0), over_e(tmax), ALU.subtract).then_inc(sub_s, 1)

            def route_choose(u):
                dve.wait_ge(pexp_s, at(u, 1, 1))
                link(u, 2, V.tensor_reduce(tsum[:], prob[:], AX.X, ALU.add))
                link(u, 3, V.reciprocal(inv_e[:], tsum[:]))
                link(u, 4, V.tensor_tensor(prob[:], prob[:], over_e(inv_e), ALU.mult))
                link(u, 5, V.tensor_reduce(pmax[:], prob[:], AX.X, ALU.max))
                link(u, 6, V.tensor_tensor(first[:], prob[:], over_e(pmax), ALU.is_equal))
                link(u, 7, V.tensor_tensor(first[:], first[:], rev[:], ALU.mult))
                link(u, 8, V.tensor_reduce(best[:], first[:], AX.X, ALU.max))
                V.tensor_tensor(chosen[:], first[:], over_e(best), ALU.is_equal).then_inc(chosen_s, 1)

            def route_place(u):
                dve.wait_ge(cnt_ps, at(u, 1, 1))
                link(u, 9, V.tensor_tensor(rank[:], route(1), seen[:].unsqueeze(1).broadcast_to([P, QUAD, E]), ALU.add))
                V.tensor_tensor(seen[:], seen[:], ps_route[:, 2 * QUAD * E:2 * QUAD * E + E], ALU.add)
                V.tensor_tensor(place[:], rank[:], base[:], ALU.add)
                link(u, 10, V.scalar_tensor_tensor(flat(kept), flat(rank), CAP - 0.5, flat(chosen), ALU.is_lt, ALU.mult))
                link(u, 11, V.tensor_tensor(place[:], place[:], kept[:], ALU.mult))
                V.tensor_scalar(rows[:, bass.ds(u.tile(), QUAD), D + 2], pmax[:], S["tanh_g"][:, 3:4], None, ALU.mult)
                link(u, 12, V.tensor_reduce(slot[:], place[:], AX.X, ALU.add))
                dve.wait_ge(free_s, at(u, 1, 1))
                link(u, 13, V.tensor_scalar(dest[:, :, 0], slot[:], float(DROPPED), None, ALU.add))
                dve.wait_ge(keep_s, u.count(1, 4))
                V.memset(S["spare"][:], 0.0).then_inc(chain, 1)
                dve.wait_ge(chain, at(u, LINKS, 14))
                V.memset(S["spare"][:], 0.0).then_inc(dest_s, 1)

            def emit(s):
                now = s.exists()
                if now:
                    dot_w1(s)
                    row_max(s)
                if s.plus(-1).exists():
                    context_row(s.plus(-1))
                if s.plus(-3).exists():
                    normalise4(s.plus(-3))
                if now:
                    scale_a(s)
                if s.plus(3).exists():
                    statistics(s.plus(3))
                if now:
                    sub_max(s)
                if s.plus(-2).exists():
                    residual(s.plus(-2))
                if s.plus(3).exists():
                    normalise(s.plus(3))
                if s.plus(-2).exists():
                    aggregate(s.plus(-2))
                if s.plus(1).exists():
                    weigh(s.plus(1))
                if s.plus(-1).exists():
                    fold(s.plus(-1))
                if now:
                    product(s)
                if s.k % 4 == 3 and quad_of(s, 7).exists():
                    route_shift(quad_of(s, 7))
                if s.k % 4 == 0 and quad_of(s, 8).exists():
                    route_choose(quad_of(s, 8))
                if s.k % 4 == 1 and quad_of(s, 9).exists():
                    route_place(quad_of(s, 9))

            dve.wait_ge(one_s, 4)
            dve.wait_ge(tab_s, 3)
            V.tensor_copy(rev[:], rev_i[:])
            V.tensor_copy(base[:], base_i[:])
            V.memset(seen[:], 0.0)
            V.tensor_copy(rows[:, :, D + 3], tok_i[:]).then_inc(tab_s, 1)
            dve.wait_ge(tab_s, 4)
            dve.wait_ge(w_s, 96)
            deep_steps(dve, emit, HEAD, TAIL)

        @block.scalar
        def _(act):
            def copy(dst, src, s_):
                nc.scalar.activation(dst, src, ACT.Copy).then_inc(s_, 1)

            def emit(s):
                halves = lambda p: p.rearrange("p (h t) -> p h t", h=HALVES)
                i = s.k % 4
                u4 = s.plus(-3)
                j = u4.k % 4
                if s.exists():
                    act.wait_ge(max_s, s.count(1, 1))
                    nc.scalar.activation(a_w[i][:], ps_sim[:, 0:P], ACT.Exp, bias=neg_max[i][:], accum_out=row_sum[i][:]).then_inc(exp_s, 1)
                    act.wait_ge(vsub_s, s.count(1, 1))
                    nc.scalar.activation(v_exp[i][:], v_sub[i][:], ACT.Exp).then_inc(vexp_s, 1)
                if u4.exists():
                    act.wait_ge(xn4_s, u4.count(1, 1))
                    copy(one(rows[:, bass.ds(u4.tile(), 1), 0:D + 2]), row4[j][:], keep_s)
                if s.exists():
                    act.wait_ge(a_ps, s.count(1, 1))
                    copy(aT[i][:], ps_a[:, P:2 * P], aT_s)
                u = s.plus(1)
                if u.exists():
                    act.wait_ge(t_ps, u.count(1, 1))
                    copy(encT[u.k % 4][:], halves(ps_t[:, 0:D]), encT_s)
                    copy(cT[u.k % 4][:], halves(ps_t[:, D:2 * D]), cT_s)
                if u4.exists():
                    act.wait_ge(x4_ps, u4.count(1, 1))
                    copy(x4T[j][:], halves(ps_x4[:, 0:D]), x4T_s)
                if s.exists():
                    act.wait_ge(hq_ps, s.count(1, 1))
                    copy(hqT[i][:], halves(ps_hq[:, 0:D]), hqT_s)
                if u4.exists():
                    act.wait_ge(lg_ps, u4.count(1, 1))
                    wait(act, lt_ps, at(u4.plus(-j), 1, 0))
                    copy(lgT[:, j, :], ps_lg[0:EXPERTS, D:D + P], lg_s)
                u = quad_of(s, 7)
                if s.k % 4 == 3 and u.exists():
                    act.wait_ge(sub_s, at(u, 1, 1))
                    nc.scalar.activation(prob[:], prob[:], ACT.Exp).then_inc(pexp_s, 1)

            deep_steps(act, emit, HEAD, TAIL)

        @block.tensor
        def _(pe):
            M = nc.tensor

            def emit(s):
                i = s.k % 4
                if s.exists():
                    pe.wait_ge(encW_s, s.count(2, 2))
                    pe.wait_ge(cT_s, s.count(1, 1))
                    wait(pe, aT_s, s.count(1, 0))
                    for h in range(HALVES):
                        ins = M.matmul(ps_sim[:, 0:P], encW[i][:, h, :], cT[i][:, h, :], start=(h == 0), stop=(h == HALVES - 1))
                    ins.then_inc(sim_ps, 1)
                u = s.plus(-1)
                if u.exists():
                    pe.wait_ge(vexp_s, u.count(1, 1))
                    wait(pe, row_s, u.count(1, 0))
                    M.matmul(ps_row[0:1, 0:D + 1], v_exp[u.k % 4][:], enc[u.k % 4][:], start=True, stop=True).then_inc(row_ps, 1)
                u = s.plus(-2)
                if u.exists():
                    pe.wait_ge(ehqT_s, u.count(1, 1))
                    pe.wait_ge(wc_s, u.count(2, 2))
                    wait(pe, x3_s, u.count(1, 0))
                    n, j = 0, u.k % 4
                    for op, w in ((hqT[j], w_f[:, 1]), (ehqT[j], w_f[:, 2]), (encT[j], w_c[j][:])):
                        for h in range(HALVES):
                            ins = M.matmul(ps_out[:, 0:D], op[:, h, :], w[:, h, :], start=(n == 0), stop=(n == 5))
                            n += 1
                    ins.then_inc(out_ps, 1)
                if s.exists():
                    pe.wait_ge(an_s, s.count(1, 1))
                    M.transpose(ps_a[:, P:2 * P], a_n[i][:], ident[:]).then_inc(a_ps, 1)
                u = s.plus(1)
                if u.exists():
                    j = u.k % 4
                    pe.wait_ge(enc_s, u.count(1, 1))
                    pe.wait_ge(c_in_s[j], u.dma(4))
                    wait(pe, cT_s, u.count(1, 0))
                    for h in range(HALVES):
                        M.transpose(ps_t[:, h * P:(h + 1) * P], enc[j][:, h * P:(h + 1) * P], ident[:])
                    for h in range(HALVES):
                        ins = M.transpose(ps_t[:, D + h * P:D + (h + 1) * P], c_in[j][:, h * P:(h + 1) * P], ident[:])
                    ins.then_inc(t_ps, 1)
                u = s.plus(-3)
                if u.exists():
                    pe.wait_ge(xn4_s, u.count(1, 1))
                    wait(pe, lg_s, u.count(1, 0))
                    for h in range(HALVES):
                        ins = M.transpose(ps_x4[:, h * P:(h + 1) * P], xn4[u.k % 4][:, h * P:(h + 1) * P], ident[:])
                    ins.then_inc(x4_ps, 1)
                if s.plus(-1).exists():
                    u = s.plus(-1)
                    pe.wait_ge(row_s, u.count(1, 1))
                    wait(pe, col_s, u.count(1, 0))
                    for h in range(HALVES):
                        ins = M.matmul(ps_col[:, h:h + 1], hc_row[u.k % 4][:, h * P:(h + 1) * P], ident[0:1, 0:1], start=True, stop=True)
                    ins.then_inc(col_ps, 1)
                if s.exists():
                    pe.wait_ge(aT_s, s.count(1, 1))
                    wait(pe, hqT_s, s.count(1, 0))
                    for h in range(HALVES):
                        ins = M.matmul(ps_hq[:, h * P:(h + 1) * P], c_in[i][:, h * P:(h + 1) * P], aT[i][:], start=True, stop=True)
                    ins.then_inc(hq_ps, 1)
                u = s.plus(-3)
                if u.exists():
                    pe.wait_ge(x4T_s, u.count(1, 1))
                    for h in range(HALVES):
                        ins = M.matmul(ps_lg[0:EXPERTS, D:D + P], wg[:, h, :], x4T[u.k % 4][:, h, :], start=(h == 0), stop=(h == HALVES - 1))
                    ins.then_inc(lg_ps, 1)
                u = quad_of(s, 7)
                if s.k % 4 == 3 and u.exists():
                    pe.wait_ge(lg_s, u.count(1, 4))
                    wait(pe, chain, at(u, 14, -4))
                    M.matmul(ps_route[:, 0:E], lgT[:, 0, :], ident[0:E, 0:E], start=True, stop=True)
                    for t in range(1, QUAD):
                        ins = M.transpose(ps_route[:, t * E:(t + 1) * E], lgT[:, t, :], ident[0:E, 0:E])
                    ins.then_inc(lt_ps, 1)
                u = quad_of(s, 9)
                if s.k % 4 == 1 and u.exists():
                    pe.wait_ge(chosen_s, at(u, 1, 1))
                    C = QUAD * E
                    for t in range(QUAD):
                        M.matmul(ps_route[:, C + t * E:C + (t + 1) * E], S["before"][:], chosen[:, t, :], start=True, stop=(t == 0))
                        for r in range(t):
                            M.matmul(ps_route[:, C + t * E:C + (t + 1) * E], S["ones_b"][:], chosen[:, r, :], start=False, stop=(r == t - 1))
                    for t in range(QUAD):
                        ins = M.matmul(ps_route[:, 2 * C:2 * C + E], S["ones_b"][:], chosen[:, t, :], start=(t == 0), stop=(t == QUAD - 1))
                    ins.then_inc(cnt_ps, 1)

            pe.wait_ge(w_s, 96)
            deep_steps(pe, emit, HEAD, TAIL)


def first_choice_ffn(nc, S, T):
    ST = CAP // P
    with ExitStack() as ctx:
        sb = lambda n, s, d=F32: ctx.enter_context(nc.sbuf_tensor(n, s, d))
        two = lambda n, s, d=F32: [sb(f"{n}{i}", s, d) for i in range(2)]
        sem = ctx.enter_context(Semaphores(nc)).new
        rows, xn, rT = [sb(f"g_rows{i}", [P, ST, ROW1]) for i in range(4)], two("g_xn", [P, ST, D]), two("g_rT", [P, HALVES, CAP])
        w, bias = two("g_w", [P, HALVES, D]), two("g_b", [P, D])
        yb, y, idx = two("g_yb", [P, ST, D]), two("g_y", [P, ST, D]), two("g_idx", [P, ST], I32)
        ps = [ctx.enter_context(nc.psum_tensor(f"pg{i}", [P, 512], F32)) for i in range(8)]
        w_in, sent = ([sem(f"pg_{n}{i}") for i in range(2)] for n in ("w", "sent"))
        in_s = [sem(f"pg_in{i}") for i in range(4)]
        xn_s, t_ps, rT_s, y_ps, yb_s, y_s, idx_s = (sem("pg_" + n) for n in ("xn", "t_ps", "rT", "y_ps", "yb", "y", "idx"))
        block = ctx.enter_context(nc.Block())
        slots_t = T["slots"].rearrange("(c p) d -> p c d", p=P)

        @block.sync
        def _(sp):
            def emit(e, par, n16, first, last):
                if e >= 4:
                    sp.wait_ge(y_s, (e - 3) * ST)
                sp.dma_start(rows[e % 4][:], slots_t[:, bass.ds(e * ST, ST), :]).then_inc(in_s[e % 4], 16)
                if not first:
                    sp.wait_ge(y_ps, (e - 1) * 2)
                    sp.wait_ge(yb_s, (e - 1) * 2)
                sp.dma_start(w[par][:], T["W1"][bass.ds(e, 1)].rearrange("a (h p) n -> p (a h) n", p=P)).then_inc(w_in[par], 16)
                sp.dma_start(bias[par][:], T["b1"][bass.ds(e, 1), :].rearrange("a n -> (a n)").partition_broadcast(P)).then_inc(w_in[par], 16)

            for e in range(EXPERTS):
                emit(e, e % 2, 16 * (e // 2 + 1), e < 2, e == EXPERTS - 1)

        @block.gpsimd
        def _(pool):
            for e in range(EXPERTS):
                pool.wait_ge(idx_s, e + 1)
                for c in range(ST):
                    pool.wait_ge(y_s, e * ST + c + 1)
                    pool.indirect_dma_start(out=T["out"], out_offset=bass.IndirectOffsetOnAxis(ap=idx[e % 2][:, c:c + 1], axis=0),
                                            in_=y[e % 2][:, c, :], in_offset=None,
                                            bounds_check=TOKENS - 1, oob_is_err=False).then_inc(sent[e % 2], 16)
            for par in range(2):
                pool.wait_ge(sent[par], 16 * ST * EXPERTS // 2)

        @block.scalar
        def _(act):
            def emit(e, par, n16, first, last):
                for h in range(HALVES):
                    act.wait_ge(t_ps, e + 1)
                    if not first:
                        act.wait_ge(y_ps, (e - 1) * 2)
                    nc.scalar.activation(rT[par][:, h, :], ps[par * 2 + h][:], ACT.Copy).then_inc(rT_s, 1)

            for e in range(EXPERTS):
                emit(e, e % 2, 16 * (e // 2 + 1), e < 2, e == EXPERTS - 1)

        @block.vector
        def _(dve):
            def norm(e, par, n16, first):
                dve.wait_ge(in_s[e % 4], 16 * (e // 4 + 1))
                if not first:
                    dve.wait_ge(t_ps, e - 1)
                for c in range(ST):
                    nc.vector.tensor_scalar(xn[par][:, c, :], rows[e % 4][:, c, 0:D], rows[e % 4][:, c, D:D + 1], rows[e % 4][:, c, D + 1:D + 2],
                                            ALU.subtract, ALU.mult).then_inc(xn_s, 1)

            def emit(e, par, n16, first, last):
                if not last:
                    other = 1 - par
                    norm(e + 1, other, n16 + 16 * par, first and par == 0)
                if not first:
                    dve.wait_ge(sent[par], (n16 - 16) * ST)
                nc.vector.tensor_scalar(idx[par][:], rows[e % 4][:, :, D + 3], -1.0, float(TOKENS), ALU.mult, ALU.add).then_inc(idx_s, 1)
                dve.wait_ge(w_in[par], n16 * 2)
                for j in range(2):
                    dve.wait_ge(y_ps, e * 2 + (j + 1))
                    nc.vector.tensor_tensor(yb[par][:, 2 * j:2 * j + 2, :], ps[4 + par * 2 + j][:].rearrange("p (c d) -> p c d", c=2),
                                            bias[par][:].unsqueeze(1).broadcast_to([P, 2, D]), ALU.add).then_inc(yb_s, 1)
                    dve.wait_ge(yb_s, e * 2 + (j + 1))
                    for c in (2 * j, 2 * j + 1):
                        nc.vector.scalar_tensor_tensor(y[par][:, c, :], yb[par][:, c, :], rows[e % 4][:, c, D + 2:D + 3],
                                                       rows[e % 4][:, c, 0:D], ALU.mult, ALU.add).then_inc(y_s, 1)

            norm(0, 0, 16, True)
            for e in range(EXPERTS):
                emit(e, e % 2, 16 * (e // 2 + 1), e < 2, e == EXPERTS - 1)

        @block.tensor
        def _(pe):
            def turn(e, par, first):
                pe.wait_ge(xn_s, (e + 1) * ST)
                if not first:
                    pe.wait_ge(rT_s, (e - 1) * 2)
                for h in range(HALVES):
                    for c in range(ST):
                        ins = nc.tensor.transpose(ps[par * 2 + h][:, c * P:(c + 1) * P], xn[par][:, c, h * P:(h + 1) * P], S["ident"][:])
                ins.then_inc(t_ps, 1)

            def emit(e, par, n16, first, last):
                if not last:
                    turn(e + 1, 1 - par, first and par == 0)
                pe.wait_ge(rT_s, (e + 1) * 2)
                pe.wait_ge(w_in[par], n16 * 2)
                if not first:
                    pe.wait_ge(yb_s, (e - 1) * 2)
                for c in range(ST):
                    for h in range(HALVES):
                        ins = nc.tensor.matmul(ps[4 + par * 2 + c // 2][:, c % 2 * D:(c % 2 + 1) * D], rT[par][:, h, c * P:(c + 1) * P],
                                               w[par][:, h, :], start=(h == 0), stop=(h == HALVES - 1))
                    if c % 2:
                        ins.then_inc(y_ps, 1)

            turn(0, 0, True)
            for e in range(EXPERTS):
                emit(e, e % 2, 16 * (e // 2 + 1), e < 2, e == EXPERTS - 1)


def program(nc, T):
    with ExitStack() as ctx:
        def keep(name, shape, dtype=F32):
            return ctx.enter_context(nc.sbuf_tensor("s_" + name, shape, dtype))

        S = {name: keep(name, shape, dtype) for name, shape, dtype in (
            ("ident", [P, P], F32), ("ident_b", [P, P], BF16), ("minus_half", [P, QUAD], F32), ("eps", [P, QUAD], F32), ("spare", [P, 1], F32), ("tanh_g", [P, 4], F32),
            ("zero", [P, ROW1], F32), ("logitsT", [EXPERTS, TOKENS], F32), ("ones_b", [P, P], BF16), ("before", [P, P], BF16),
            ("keep", [P, EXPERTS, TILES], F32))}
        setup(nc, S, T)
        project_qkv(nc, S, T)
        attention(nc, S, T)
        with ExitStack() as routed:
            S["score"] = routed.enter_context(nc.sbuf_tensor("s_score", [P, TILES, EXPERTS], F32))
            S["idx"] = routed.enter_context(nc.sbuf_tensor("s_idx", [P, EXPERTS, CAP // P], I32))
            route_top_k(nc, S, T)
            expert_choice_ffn(nc, S, T)
        bidirectional_attention(nc, S, T)
        first_choice_ffn(nc, S, T)


def kernel(**inputs):
    import concourse.bacc as bacc
    from concourse.bass_utils import run_bass_kernel_spmd

    laid = {
        "x": inputs["x"].reshape(TOKENS, D), "ctx": inputs["ctx_1024"].reshape(TOKENS, D), "mask": inputs["mask_BxS2_ik0"],
        "g_xattn": inputs["g_xattn"], "g_ffn": inputs["g_ffn"],
    }
    for name in ("Wq", "bq", "Wk", "bk", "Wv", "bv", "Wo", "bo"):
        laid[name] = inputs["L0_xattn_" + name]
    for name in ("Wr", "br", "W_up", "b_up", "W_down", "b_down"):
        laid[name] = inputs["L0_ffn_" + name]
    for name in ("w_sim", "b_sim", "W_qv", "b_qv"):
        laid[name] = inputs["L1_xattn_" + name]
    laid["wg"] = inputs["L1_ffn_wg"]
    laid["W1"] = inputs["L1_ffn_W"].transpose(0, 2, 1)
    laid["b1"] = inputs["L1_ffn_b"]

    nc = bacc.Bacc("TRN2", target_bir_lowering=False, num_devices=1)
    arrays, T = {}, {}
    for name, a in laid.items():
        a = np.ascontiguousarray(a)
        arrays["in_" + name] = a
        T[name] = nc.dram_tensor("in_" + name, a.shape, mybir.dt.from_np(a.dtype), kind="ExternalInput").ap()
    for name, shape, dtype in (
            ("mask_row", (TOKENS,), BF16), ("qparts", (2, D, TOKENS), BF16), ("kparts", (2, D, TOKENS), BF16), ("v", (TOKENS, D), F32),
            ("resid", (TOKENS, D), F32), ("rows0", (TOKENS, ROW0), F32), ("idx", (TOKENS,), I32),
            ("slots", (TOKENS, ROW1), F32)):
        T[name] = nc.dram_tensor("scratch_" + name, shape, dtype, kind="Internal").ap()
    T["out"] = nc.dram_tensor("result", (TOKENS, D), F32, kind="ExternalOutput").ap()
    program(nc, T)
    r = run_bass_kernel_spmd(nc, [arrays], core_ids=[0])
    return r.results[0]["result"].reshape(BATCHES, SEQ, D)
```

```python
import numpy as np
import concourse.bass as bass
from concourse import mybir
from contextlib import ExitStack

F32 = mybir.dt.float32
BF16 = mybir.dt.bfloat16
I32 = mybir.dt.int32
ALU = mybir.AluOpType
ACT = mybir.ActivationFunctionType
AX = mybir.AxisListType
REDUCE_MAX = bass.bass_isa.ReduceOp.max

P = 128
BATCHES, SEQ, D = 32, 128, 256
TOKENS = BATCHES * SEQ
QUAD = 4
QT = QUAD * P
QUADS = TOKENS // QT
HALVES = D // P
HEADS, HD = 16, 16
EXPERTS = 8
CAP = TOKENS // EXPERTS
FFN = 682
LN_EPS = 1e-5
MASKED = -4e20


class Semaphores:

    def __init__(self, nc):
        self.nc, self.made = nc, []

    def __enter__(self):
        return self

    def new(self, name):
        self.made.append(self.nc.alloc_semaphore(name))
        return self.made[-1]

    def __exit__(self, *exc):
        if exc[0] is None:
            self.nc.clear_and_free_semaphores(self.made)
            self.nc.all_engine_barrier()


def settle(nc, S, dve, semaphore, value):
    dve.wait_ge(semaphore, value)
    nc.vector.memset(S["spare"][:], 0.0)


def setup(nc, S, T):
    with ExitStack() as ctx:
        sem = ctx.enter_context(Semaphores(nc)).new
        mask_i = ctx.enter_context(nc.sbuf_tensor("mask_i", [BATCHES, SEQ], I32))
        mask_add = ctx.enter_context(nc.sbuf_tensor("mask_add", [BATCHES, SEQ], BF16))
        ones_row = ctx.enter_context(nc.sbuf_tensor("ones_row", [BATCHES, SEQ], BF16))
        gates = ctx.enter_context(nc.sbuf_tensor("gates", [P, 4], F32))
        loaded, made, masked, stored, tanhed = (sem(n) for n in
            ("su_loaded", "su_made", "su_masked", "su_stored", "su_tanhed"))
        block = ctx.enter_context(nc.Block())

        @block.sync
        def _(sp):
            sp.dma_start(mask_i[:], T["mask"]).then_inc(loaded, 16)
            sp.dma_start(gates[:, 0:2], T["g_xattn"].partition_broadcast(P)).then_inc(loaded, 16)
            sp.dma_start(gates[:, 2:4], T["g_ffn"].partition_broadcast(P)).then_inc(loaded, 16)
            sp.wait_ge(masked, 1)
            sp.dma_start(T["mask_row"].rearrange("(b s) -> b s", s=SEQ), mask_add[:]).then_inc(stored, 16)
            sp.wait_ge(made, 7)
            sp.dma_start(T["ones_row"].rearrange("(b s) -> b s", s=SEQ), ones_row[:]).then_inc(stored, 16)
            sp.wait_ge(stored, 32)

        @block.gpsimd
        def _(pool):
            nc.gpsimd.memset(S["zero"][:], 0.0)
            nc.gpsimd.memset(ones_row[:], 1.0).then_inc(made, 1)
            nc.gpsimd.memset(S["ident"][:], 0.0).then_inc(made, 1)
            nc.gpsimd.memset(S["ident_b"][:], 0.0).then_inc(made, 1)
            nc.gpsimd.memset(S["minus_half"][:], -0.5).then_inc(made, 1)
            nc.gpsimd.memset(S["eps"][:], LN_EPS).then_inc(made, 1)
            pool.wait_ge(made, 5)
            for m in (S["ident"], S["ident_b"]):
                nc.gpsimd.affine_select(out=m[:], in_=m[:], compare_op=ALU.not_equal, fill=1.0, base=0,
                                        pattern=[[-1, P]], channel_multiplier=1).then_inc(made, 1)

        @block.vector
        def _(dve):
            dve.wait_ge(loaded, 48)
            nc.vector.tensor_scalar(mask_add[:], mask_i[:], 0.0, MASKED, ALU.is_equal, ALU.mult).then_inc(masked, 1)

        @block.scalar
        def _(act):
            act.wait_ge(loaded, 48)
            nc.scalar.activation(S["tanh_g"][:], gates[:], ACT.Tanh).then_inc(tanhed, 1)


def project_qkv(nc, S, T):
    with ExitStack() as ctx:
        sb = lambda n, s, d=F32: ctx.enter_context(nc.sbuf_tensor(n, s, d))
        sem = ctx.enter_context(Semaphores(nc)).new
        ident = S["ident"]
        wq, wk, wv = (sb(n, [P, HALVES, D]) for n in ("wq", "wk", "wv"))
        bias_qk = sb("bias_qk", [P, 2, HALVES])
        bias_v = sb("bias_v", [P, 2, D])
        x_in = [sb(f"x_in{i}", [P, QUAD, D]) for i in range(2)]
        c_in = [sb(f"c_in{i}", [P, QUAD, D]) for i in range(2)]
        xn = [sb(f"xn{i}", [P, QUAD, D]) for i in range(2)]
        stats = sb("stats", [P, QUAD, 6])
        moments = sb("moments", [P, QUAD, 2])
        vareps = sb("vareps", [P, QUAD])
        rstd = sb("rstd", [P, QUAD])
        xT = [sb(f"xT{i}", [P, HALVES, QT]) for i in range(2)]
        cT = [sb(f"cT{i}", [P, HALVES, QT]) for i in range(2)]
        parts = [sb(f"parts{i}", [P, 2, HALVES, 2, QT], BF16) for i in range(2)]
        v_out = [sb(f"v_out{i}", [P, QUAD, D]) for i in range(2)]
        banks = [ctx.enter_context(nc.psum_tensor(f"pa{i}", [P, 512], F32)) for i in range(8)]
        ps_x, ps_c, ps_q, ps_k = banks[0:2], banks[2:4], banks[4:6], banks[6:8]
        ps_v = ps_x
        weights = sem("pa_weights")
        x_in_s = [sem(f"pa_x{i}") for i in range(2)]
        c_in_s = [sem(f"pa_c{i}") for i in range(2)]
        stats_s, moments_s, rstd_s, xn_s = (sem(n) for n in ("pa_stats", "pa_moments", "pa_rstd", "pa_xn"))
        vareps_s = sem("pa_vareps")
        xt_ps, ct_ps, q_ps, k_ps, v_ps = (sem(n) for n in ("pa_xt_ps", "pa_ct_ps", "pa_q_ps", "pa_k_ps", "pa_v_ps"))
        xt_s, ct_s, hi_s, lo_s, v_s = (sem(n) for n in ("pa_xt", "pa_ct", "pa_hi", "pa_lo", "pa_v"))
        qk_out = [sem(f"pa_qk_out{i}") for i in range(2)]
        v_outs = [sem(f"pa_v_out{i}") for i in range(2)]
        block = ctx.enter_context(nc.Block())
        x_t = T["x"].rearrange("(t p) d -> p t d", p=P)
        c_t = T["ctx"].rearrange("(t p) d -> p t d", p=P)
        v_t = T["v"].rearrange("(t p) d -> p t d", p=P)

        @block.sync
        def _(sp):
            def load(q, par, first):
                if not first:
                    sp.wait_ge(ct_ps, q - 1)
                    sp.wait_ge(xt_ps, q - 1)
                sp.dma_start(x_in[par][:], x_t[:, bass.ds(q * QUAD, QUAD), :]).then_inc(x_in_s[par], 16)
                sp.dma_start(c_in[par][:], c_t[:, bass.ds(q * QUAD, QUAD), :]).then_inc(c_in_s[par], 16)

            def store(q, par):
                sp.wait_ge(lo_s, 4 * q + 4)
                for j, name in enumerate(("qparts", "kparts")):
                    for h in range(HALVES):
                        sp.dma_start(T[name][:, h * P:(h + 1) * P, bass.ds(q * QT, QT)].rearrange("s p t -> p s t"),
                                     parts[par][:, j, h]).then_inc(qk_out[par], 16)
                sp.wait_ge(v_s, 2 * q + 2)
                sp.dma_start(v_t[:, bass.ds(q * QUAD, QUAD), :], v_out[par][:]).then_inc(v_outs[par], 16)

            load(0, 0, True)
            for i, w in enumerate(("Wq", "Wk", "Wv")):
                sp.dma_start((wq, wk, wv)[i][:], T[w].rearrange("(h p) n -> p h n", p=P)).then_inc(weights, 16)
            for j in range(2):
                sp.dma_start(bias_v[:, j, :], T["bv"].partition_broadcast(P)).then_inc(weights, 16)
                sp.dma_start(bias_qk[:, j, :], T[("bq", "bk")[j]].rearrange("(h p) -> p h", p=P), allow_slow_non_contiguous=True).then_inc(weights, 16)
            load(1, 1, True)
            with sp.Fori(0, QUADS // 2 - 1) as pair:
                for par in range(2):
                    load(pair * 2 + (par + 2), par, False)
                    store(pair * 2 + par, par)
            for par in range(2):
                store(QUADS - 2 + par, par)
            for par in range(2):
                sp.wait_ge(qk_out[par], 64 * QUADS // 2)
                sp.wait_ge(v_outs[par], 16 * QUADS // 2)

        @block.gpsimd
        def _(pool):
            with pool.Fori(0, QUADS) as q:
                pool.wait_ge(moments_s, q + 1)
                nc.gpsimd.tensor_tensor(vareps[:], moments[:, :, 1], S["eps"][:], ALU.add).then_inc(vareps_s, 1)
                pool.wait_ge(vareps_s, q + 1)
                nc.gpsimd.tensor_tensor(rstd[:], vareps[:], S["minus_half"][:, 0:QUAD], ALU.pow).then_inc(rstd_s, 1)

        @block.vector
        def _(dve):
            def statistics(q, par, n16):
                dve.wait_ge(x_in_s[par], n16)
                for t in range(QUAD):
                    nc.vector.bn_stats(stats[:, t, :], x_in[par][:, t, :]).then_inc(stats_s, 1)
                settle(nc, S, dve, stats_s, q * QUAD + QUAD)
                for t in range(QUAD):
                    ins = nc.vector.bn_aggr(moments[:, t, :], stats[:, t, :])
                ins.then_inc(moments_s, 1)

            def norm(q, par, first):
                dve.wait_ge(rstd_s, q + 1)
                if not first:
                    dve.wait_ge(xt_ps, q - 1)
                dve.wait_ge(moments_s, q + 1)
                for t in range(QUAD):
                    ins = nc.vector.tensor_scalar(xn[par][:, t, :], x_in[par][:, t, :], moments[:, t, 0:1], rstd[:, t:t + 1],
                                                  ALU.subtract, ALU.mult)
                ins.then_inc(xn_s, 1)

            def quad(q, par, first, fresh, last=False):
                for h in range(HALVES):
                    dve.wait_ge(ct_ps, q + 1)
                    if not first:
                        dve.wait_ge(k_ps, q)
                    nc.vector.tensor_copy(cT[par][:, h, :], ps_c[h][:]).then_inc(ct_s, 1)
                if not last:
                    norm(q + 1, 1 - par, first)
                for h in range(HALVES):
                    dve.wait_ge(hi_s, 4 * q + (h + 1))
                    nc.vector.scalar_tensor_tensor(parts[par][:, 0, h, 1, :], ps_q[h][:], bias_qk[:, 0, h:h + 1],
                                                   parts[par][:, 0, h, 0, :], ALU.add, ALU.subtract).then_inc(lo_s, 1)
                for j in range(2):
                    dve.wait_ge(v_ps, 2 * q + (j + 1))
                    if not fresh:
                        dve.wait_ge(v_outs[par], out16(q, par))
                    nc.vector.tensor_tensor(v_out[par][:, 2 * j:2 * j + 2, :], ps_v[j][:].rearrange("p (a d) -> p a d", a=2),
                                            bias_v[:], ALU.add).then_inc(v_s, 1)
                for h in range(HALVES):
                    dve.wait_ge(hi_s, 4 * q + (h + 3))
                    nc.vector.scalar_tensor_tensor(parts[par][:, 1, h, 1, :], ps_k[h][:], bias_qk[:, 1, h:h + 1],
                                                   parts[par][:, 1, h, 0, :], ALU.add, ALU.subtract).then_inc(lo_s, 1)

            def out16(q, par):
                return (q - par) * 8

            statistics(0, 0, 16)
            norm(0, 0, True)
            statistics(1, 1, 16)
            dve.wait_ge(weights, 16 * 7)
            quad(0, 0, True, True)
            statistics(2, 0, 32)
            quad(1, 1, False, True)
            statistics(3, 1, 32)
            with dve.Fori(1, QUADS // 2 - 1) as pair:
                for par in range(2):
                    quad(pair * 2 + par, par, False, False)
                    statistics(pair * 2 + (par + 2), par, pair * 16 + 32)
            quad(QUADS - 2, 0, False, False)
            quad(QUADS - 1, 1, False, False, last=True)

        @block.scalar
        def _(act):
            def quad(q, par, first):
                for h in range(HALVES):
                    act.wait_ge(xt_ps, q + 1)
                    if not first:
                        act.wait_ge(q_ps, q - 1)
                    nc.scalar.activation(xT[par][:, h, :], ps_x[h][:], ACT.Copy).then_inc(xt_s, 1)
                for h in range(HALVES):
                    act.wait_ge(q_ps, q + 1)
                    if not first:
                        act.wait_ge(qk_out[par], (q - par) * 32)
                    nc.scalar.activation(parts[par][:, 0, h, 0, :], ps_q[h][:], ACT.Identity,
                                         bias=bias_qk[:, 0, h:h + 1]).then_inc(hi_s, 1)
                for h in range(HALVES):
                    act.wait_ge(k_ps, q + 1)
                    nc.scalar.activation(parts[par][:, 1, h, 0, :], ps_k[h][:], ACT.Identity,
                                         bias=bias_qk[:, 1, h:h + 1]).then_inc(hi_s, 1)

            act.wait_ge(weights, 16 * 7)
            for par in range(2):
                quad(par, par, True)
            with act.Fori(1, QUADS // 2) as pair:
                for par in range(2):
                    quad(pair * 2 + par, par, False)

        @block.tensor
        def _(pe):
            def quad(q, par, n16, first):
                pe.wait_ge(xn_s, q + 1)
                if not first:
                    pe.wait_ge(v_s, 2 * q)
                for h in range(HALVES):
                    for t in range(QUAD):
                        ins = nc.tensor.transpose(ps_x[h][:, t * P:(t + 1) * P], xn[par][:, t, h * P:(h + 1) * P], ident[:])
                ins.then_inc(xt_ps, 1)
                pe.wait_ge(c_in_s[par], n16)
                if not first:
                    pe.wait_ge(ct_s, 2 * q)
                for h in range(HALVES):
                    for t in range(QUAD):
                        ins = nc.tensor.transpose(ps_c[h][:, t * P:(t + 1) * P], c_in[par][:, t, h * P:(h + 1) * P], ident[:])
                ins.then_inc(ct_ps, 1)
                pe.wait_ge(xt_s, 2 * q + 2)
                if not first:
                    pe.wait_ge(lo_s, 4 * q)
                for m in range(HALVES):
                    for h in range(HALVES):
                        ins = nc.tensor.matmul(ps_q[m][:], wq[:, h, m * P:(m + 1) * P], xT[par][:, h, :],
                                               start=(h == 0), stop=(h == HALVES - 1))
                ins.then_inc(q_ps, 1)
                pe.wait_ge(ct_s, 2 * q + 2)
                for t in range(QUAD):
                    for h in range(HALVES):
                        ins = nc.tensor.matmul(ps_v[t // 2][:, (t % 2) * D:(t % 2 + 1) * D], cT[par][:, h, t * P:(t + 1) * P],
                                               wv[:, h, :], start=(h == 0), stop=(h == HALVES - 1))
                    if t % 2:
                        ins.then_inc(v_ps, 1)
                for m in range(HALVES):
                    for h in range(HALVES):
                        ins = nc.tensor.matmul(ps_k[m][:], wk[:, h, m * P:(m + 1) * P], cT[par][:, h, :],
                                               start=(h == 0), stop=(h == HALVES - 1))
                ins.then_inc(k_ps, 1)

            pe.wait_ge(weights, 16 * 7)
            for par in range(2):
                quad(par, par, 16, par == 0)
            with pe.Fori(1, QUADS // 2) as pair:
                for par in range(2):
                    quad(pair * 2 + par, par, pair * 16 + 16, False)


TILES = TOKENS // P
STACK = 3 * HD + 1
SLOTW = 32


class Step:

    def __init__(self, base, k):
        self.base, self.k = base, k

    def plus(self, d):
        return Step(self.base, self.k + d)

    def count(self, per, extra):
        return self.base * (4 * per) + (self.k * per + extra)

    def dma(self, slots, per=1):
        return self.base * (4 // slots * 16 * per) + 16 * per * (self.k // slots + 1)

    def exists(self):
        return not isinstance(self.base, int) or 0 <= self.base * 4 + self.k < TILES

    def tile(self):
        return self.base * 4 + self.k


def wait(engine, semaphore, value):
    if not isinstance(value, int) or value > 0:
        engine.wait_ge(semaphore, value)


def steps(engine, emit, tail):
    for k in range(4):
        emit(Step(0, k))
    with engine.Fori(1, TILES // 4 - 1) as base:
        for k in range(4):
            emit(Step(base, k))
    for k in range(4 + tail):
        emit(Step(TILES // 4 - 1, k))


def attention(nc, S, T):
    with ExitStack() as ctx:
        sb = lambda n, s, d=F32: ctx.enter_context(nc.sbuf_tensor(n, s, d))
        sem = ctx.enter_context(Semaphores(nc)).new
        ident, ident_b = S["ident"], S["ident_b"]
        wo, wr = sb("wo", [P, HALVES, D]), sb("wr", [P, HALVES, EXPERTS])
        bo = sb("bo", [P, D])
        br = sb("br", [EXPERTS, 1])
        pick = sb("pick", [2 * HEADS, HEADS, P], BF16)
        qs = [sb(f"qs{i}", [64, HEADS, 2 * P], BF16) for i in range(2)]
        ks = [sb(f"ks{i}", [64, HEADS, 2 * P], BF16) for i in range(2)]
        v_in = [sb(f"v_in{i}", [P, D]) for i in range(2)]
        v_wide = [sb(f"v_wide{i}", [P, HEADS, SLOTW]) for i in range(2)]
        x_res = [sb(f"x_res{i}", [P, D]) for i in range(4)]
        neg_max = sb("neg_max", [P, HEADS])
        nm_parts = sb("nm_parts", [P, 2, HEADS], BF16)
        nmT = sb("nmT", [2 * HEADS, P], BF16)
        probs = [sb(f"probs{i}", [P, 4, P]) for i in range(2)]
        ctxT = sb("ctxT", [P, 4 * P])
        inv_sum = sb("inv_sum", [P, HEADS])
        attn = sb("attn", [P, D])
        attnT = sb("attnT", [P, HALVES, P])
        x1 = [sb(f"x1_{i}", [P, D]) for i in range(2)]
        stats, moments = sb("b_stats", [P, 6]), [sb(f"b_moments{i}", [P, 2]) for i in range(2)]
        vareps, rstd = sb("b_vareps", [P, 1]), sb("b_rstd", [P, 1])
        xn = [sb(f"b_xn{i}", [P, D]) for i in range(2)]
        xnT = sb("b_xnT", [P, HALVES, P])
        ps = [ctx.enter_context(nc.psum_tensor(f"pb{i}", [P, 512], F32)) for i in range(6)]
        ps_s, ps_st, ps_ctx, ps_ctxT = ps[0:2], ps[2:4], ps[4], ps[5]
        ps6 = ctx.enter_context(nc.psum_tensor("pb6", [P, 512], F32))
        ps7 = ctx.enter_context(nc.psum_tensor("pb7", [P, 512], F32))
        ps_aT, ps_nmT = ps6[:, 0:D], ps6[0:2 * HEADS, D:D + P // 2].bitcast(BF16)
        ps_o, ps_xnT = ps7[:, 0:D], ps7[:, D:2 * D]
        ps_lg = ps_ctxT[0:EXPERTS, 0:P]
        w_s, thbo_s, pick_s, ones_s = sem("pb_w"), sem("pb_thbo"), sem("pb_pick"), sem("pb_ones")
        q_in = [sem(f"pb_q{i}") for i in range(2)]
        k_in = [sem(f"pb_k{i}") for i in range(2)]
        v_in_s = [sem(f"pb_vin{i}") for i in range(2)]
        x_in_s = [sem(f"pb_xin{i}") for i in range(4)]
        x1_out = [sem(f"pb_x1out{i}") for i in range(2)]
        xn_out = [sem(f"pb_xnout{i}") for i in range(2)]
        (s_ps, max_s, nm_hi_s, nm_s, nmT_ps, nmT_s, st_ps, exp_s, ctx_ps, ctxT_s, ctxT_ps, inv_s, attn_s, aT_ps, aT_s,
         o_ps, x1_s, stats_s, mom_s, ve_s, rstd_s, xn_s, xnT_ps, xnT_s, lg_ps, lg_s, vw_s, xb_s) = (
            sem("pb_" + n) for n in (
                "s_ps", "max", "nm_hi", "nm", "nmT_ps", "nmT", "st_ps", "exp", "ctx_ps", "ctxT", "ctxT_ps", "inv",
                "attn", "aT_ps", "aT", "o_ps", "x1", "stats", "mom", "ve", "rstd", "xn", "xnT_ps", "xnT", "lg_ps", "lg",
                "vw", "xb"))
        av_s = sem("pb_av")
        block = ctx.enter_context(nc.Block())
        v_t = T["v"].rearrange("(t p) d -> p t d", p=P)
        x_t = T["x"].rearrange("(t p) d -> p t d", p=P)
        x1_t = T["resid"].rearrange("(t p) d -> p t d", p=P)
        xn_t = T["rows0"].rearrange("(t p) d -> p t d", p=P)

        @block.sync
        def _(sp):
            for t in qs:
                sp.dma_start(t[3 * HD:STACK, :, :], T["ones_row"].rearrange("(a h t) -> a h t", a=1, h=HEADS)).then_inc(ones_s, 16)

            def load_stacks(s):
                slot = s.k // 2 % 2
                wait(sp, st_ps, s.count(4, -8))
                toks = bass.ds(s.tile() * P, 2 * P)
                for i, part in enumerate((0, 1, 0)):
                    sp.dma_start(qs[slot][i * HD:(i + 1) * HD, :, :],
                                 T["qparts"][part, :, toks].rearrange("(h r) t -> r h t", r=HD)).then_inc(q_in[slot], 16)
                for i, part in enumerate((0, 0, 1)):
                    sp.dma_start(ks[slot][i * HD:(i + 1) * HD, :, :],
                                 T["kparts"][part, :, toks].rearrange("(h r) t -> r h t", r=HD)).then_inc(k_in[slot], 16)
                sp.dma_start(ks[slot][3 * HD:STACK, :, :],
                             T["mask_row"][toks].unsqueeze(0).unsqueeze(0).broadcast_to([1, HEADS, 2 * P])
                             ).then_inc(k_in[slot], 16)

            def load_tiles(s):
                slot = s.k % 2
                wait(sp, vw_s, s.count(1, -1))
                sp.dma_start(v_in[slot][:], v_t[:, bass.ds(s.tile(), 1), :].rearrange("p a d -> p (a d)")).then_inc(v_in_s[slot], 16)
                wait(sp, x1_s, s.count(1, -3))
                sp.dma_start(x_res[s.k % 4][:], x_t[:, bass.ds(s.tile(), 1), :].rearrange("p a d -> p (a d)")).then_inc(x_in_s[s.k % 4], 16)

            def emit(s):
                if s.k % 2 == 0 and s.plus(2).exists():
                    load_stacks(s.plus(2))
                if s.plus(1).exists():
                    load_tiles(s.plus(1))
                if s.plus(-2).exists():
                    sp.wait_ge(x1_s, s.count(1, -1))
                    sp.dma_start(x1_t[:, bass.ds(s.plus(-2).tile(), 1), :].rearrange("p a d -> p (a d)"),
                                 x1[s.k % 2][:]).then_inc(x1_out[s.k % 2], 16)
                    sp.wait_ge(xn_s, s.count(1, -1))
                    sp.dma_start(xn_t[:, bass.ds(s.plus(-2).tile(), 1), 0:D].rearrange("p a d -> p (a d)"),
                                 xn[s.k % 2][:]).then_inc(xn_out[s.k % 2], 16)

            load_stacks(Step(0, 0))
            load_tiles(Step(0, 0))
            sp.dma_start(wo[:], T["Wo"].rearrange("(h p) n -> p h n", p=P)).then_inc(w_s, 16)
            sp.dma_start(wr[:], T["Wr"].rearrange("(h p) n -> p h n", p=P)).then_inc(w_s, 16)
            sp.dma_start(bo[:], T["bo"].partition_broadcast(P)).then_inc(w_s, 16)
            sp.dma_start(br[:], T["br"].rearrange("(e a) -> e a", a=1)).then_inc(w_s, 16)
            steps(sp, emit, 2)
            for i in range(2):
                sp.wait_ge(x1_out[i], 16 * TILES // 2)
                sp.wait_ge(xn_out[i], 16 * TILES // 2)

        @block.gpsimd
        def _(pool):
            nc.gpsimd.memset(pick[:], 0.0).then_inc(pick_s, 1)
            for t in range(2):
                nc.gpsimd.memset(v_wide[t][:], 1.0).then_inc(pick_s, 1)
            for r in range(2):
                pool.wait_ge(pick_s, 3 + r)
                nc.gpsimd.affine_select(out=pick[:], in_=pick[:], compare_op=ALU.not_equal, fill=1.0, base=-HEADS * r,
                                        pattern=[[-1, HEADS], [0, P]], channel_multiplier=1).then_inc(pick_s, 1)
            pool.wait_ge(w_s, 64)
            nc.gpsimd.tensor_scalar(bo[:], bo[:], S["tanh_g"][:, 0:1], None, ALU.mult).then_inc(thbo_s, 1)
            pool.wait_ge(thbo_s, 1)

            def widen(s):
                slot = s.k % 2
                pool.wait_ge(v_in_s[slot], s.dma(2))
                wait(pool, ctx_ps, s.count(1, -1))
                nc.gpsimd.tensor_tensor(v_wide[slot][:, :, 0:HD], v_in[slot][:].rearrange("p (h d) -> p h d", h=HEADS),
                                        S["zero"][:, 0:D].rearrange("p (h d) -> p h d", h=HEADS), ALU.add).then_inc(vw_s, 1)

            def emit(s):
                if s.plus(-2).exists():
                    pool.wait_ge(mom_s, s.count(1, -1))
                    nc.gpsimd.tensor_tensor(vareps[:], moments[s.k % 2][:, 1:2], S["eps"][:, 0:1], ALU.add).then_inc(ve_s, 1)
                    pool.wait_ge(ve_s, s.count(1, -1))
                    wait(pool, xn_s, s.count(1, -2))
                    nc.gpsimd.tensor_tensor(rstd[:], vareps[:], S["minus_half"][:, 0:1], ALU.pow).then_inc(rstd_s, 1)
                if s.plus(1).exists():
                    widen(s.plus(1))
                if s.exists():
                    slot = s.k % 4
                    pool.wait_ge(x_in_s[slot], s.dma(4))
                    nc.gpsimd.tensor_tensor(x_res[slot][:], x_res[slot][:], bo[:], ALU.add).then_inc(xb_s, 1)

            widen(Step(0, 0))
            steps(pool, emit, 2)

        @block.vector
        def _(dve):
            def row_max(s, g):
                dve.wait_ge(s_ps, s.count(4, g + 1))
                wait(dve, nm_s, s.count(1, 0))
                nc.vector.tensor_reduce(neg_max[:, 4 * g:4 * g + 4], ps_s[g % 2][:].rearrange("p (h k) -> p h k", h=4),
                                        AX.X, ALU.max, negate=True).then_inc(max_s, 1)

            def split_max(s):
                dve.wait_ge(max_s, s.count(4, 4))
                wait(dve, nmT_ps, s.count(1, 0))
                nc.vector.tensor_copy(nm_parts[:, 0, :], neg_max[:]).then_inc(nm_hi_s, 1)
                dve.wait_ge(nm_hi_s, s.count(1, 1))
                nc.vector.tensor_tensor(nm_parts[:, 1, :], neg_max[:], nm_parts[:, 0, :], ALU.subtract).then_inc(nm_s, 1)

            def max_out(s):
                dve.wait_ge(nmT_ps, s.count(1, 1))
                wait(dve, st_ps, s.count(4, 0))
                nc.vector.tensor_copy(nmT[:], ps_nmT).then_inc(nmT_s, 1)

            def normalise(s):
                heads = ps_ctxT[:].rearrange("p (h c) -> p h c", h=HEADS)
                dve.wait_ge(ctxT_ps, s.count(1, 1))
                nc.vector.reciprocal(inv_sum[:], heads[:, :, HD]).then_inc(inv_s, 1)
                dve.wait_ge(inv_s, s.count(1, 1))
                wait(dve, aT_ps, s.count(1, 0))
                nc.vector.tensor_tensor(attn[:].rearrange("p (h d) -> p h d", h=HEADS), heads[:, :, 0:HD],
                                        inv_sum[:].unsqueeze(2).broadcast_to([P, HEADS, HD]), ALU.mult).then_inc(attn_s, 1)

            def residual(s):
                slot = s.k % 2
                dve.wait_ge(o_ps, s.count(1, 1))
                dve.wait_ge(xb_s, s.count(1, 1))
                if s.plus(-2).exists():
                    dve.wait_ge(x1_out[slot], s.plus(-2).dma(2))
                nc.vector.scalar_tensor_tensor(x1[slot][:], ps_o, S["tanh_g"][:, 0:1], x_res[s.k % 4][:],
                                               ALU.mult, ALU.add).then_inc(x1_s, 1)
                dve.wait_ge(x1_s, s.count(1, 1))
                nc.vector.bn_stats(stats[:], x1[slot][:]).then_inc(stats_s, 1)
                settle(nc, S, dve, stats_s, s.count(1, 1))
                nc.vector.bn_aggr(moments[slot][:], stats[:]).then_inc(mom_s, 1)

            def norm(s):
                slot = s.k % 2
                dve.wait_ge(rstd_s, s.count(1, 1))
                wait(dve, xnT_ps, s.count(1, -1))
                if s.plus(-2).exists():
                    dve.wait_ge(xn_out[slot], s.plus(-2).dma(2))
                nc.vector.tensor_scalar(xn[slot][:], x1[slot][:], moments[slot][:, 0:1], rstd[:],
                                        ALU.subtract, ALU.mult).then_inc(xn_s, 1)

            def emit(s):
                one = s.plus(1).exists()
                if one:
                    row_max(s.plus(1), 0)
                if s.plus(-2).exists():
                    residual(s.plus(-2))
                if one:
                    row_max(s.plus(1), 1)
                if one:
                    row_max(s.plus(1), 2)
                if s.plus(-2).exists():
                    norm(s.plus(-2))
                if one:
                    row_max(s.plus(1), 3)
                if one:
                    split_max(s.plus(1))
                if s.plus(-1).exists():
                    normalise(s.plus(-1))
                if one:
                    max_out(s.plus(1))

            for g in range(4):
                row_max(Step(0, 0), g)
            split_max(Step(0, 0))
            max_out(Step(0, 0))
            steps(dve, emit, 2)

        @block.scalar
        def _(act):
            act.wait_ge(w_s, 64)

            def emit(s):
                if s.plus(-1).exists():
                    act.wait_ge(ctx_ps, s.count(1, 0))
                    wait(act, ctxT_ps, s.count(1, -1))
                    nc.scalar.activation(ctxT[:], ps_ctx[:], ACT.Copy).then_inc(ctxT_s, 1)
                if s.exists():
                    for g in range(4):
                        act.wait_ge(st_ps, s.count(4, g + 1))
                        if g < 2:
                            wait(act, ctx_ps, s.count(1, 0))
                        else:
                            act.wait_ge(av_s, s.count(3, g - 1))
                        nc.scalar.activation(probs[g % 2][:], ps_st[g % 2][:].rearrange("p (h q) -> p h q", h=4),
                                             ACT.Exp, scale=1.0 / HD ** 0.5).then_inc(exp_s, 1)
                if s.plus(-2).exists():
                    act.wait_ge(xnT_ps, s.count(1, -1))
                    wait(act, lg_ps, s.count(1, -2))
                    nc.scalar.activation(xnT[:], ps_xnT.rearrange("p (h t) -> p h t", h=HALVES), ACT.Copy).then_inc(xnT_s, 1)
                if s.plus(-1).exists():
                    act.wait_ge(aT_ps, s.count(1, 0))
                    wait(act, o_ps, s.count(1, -1))
                    nc.scalar.activation(attnT[:], ps_aT.rearrange("p (h t) -> p h t", h=HALVES), ACT.Copy).then_inc(aT_s, 1)
                if s.plus(-2).exists():
                    act.wait_ge(lg_ps, s.count(1, -1))
                    nc.scalar.activation(S["logitsT"][:, bass.ds(s.plus(-2).tile() * P, P)], ps_lg, ACT.Identity,
                                         bias=br[:]).then_inc(lg_s, 1)

            steps(act, emit, 2)

        @block.tensor
        def _(pe):
            pe.wait_ge(ones_s, 32)

            def operand(t, s, h, rows):
                return t[s.k // 2 % 2][0:rows, h, s.k % 2 * P:(s.k % 2 + 1) * P]

            def scores(s, g):
                if g == 0 and s.k % 2 == 0:
                    pe.wait_ge(q_in[s.k // 2 % 2], s.dma(4, 3))
                    pe.wait_ge(k_in[s.k // 2 % 2], s.dma(4, 4))
                wait(pe, max_s, s.count(4, g - 1))
                for j in range(4):
                    ins = nc.tensor.matmul(ps_s[g % 2][:, j * P:(j + 1) * P], operand(qs, s, 4 * g + j, STACK),
                                           operand(ks, s, 4 * g + j, STACK), start=True, stop=True)
                ins.then_inc(s_ps, 1)

            def shifted(s, g):
                if g == 0:
                    pe.wait_ge(nmT_s, s.count(1, 1))
                wait(pe, exp_s, s.count(4, g - 1))
                for j in range(4):
                    out = ps_st[g % 2][:, j * P:(j + 1) * P]
                    nc.tensor.matmul(out, operand(ks, s, 4 * g + j, STACK), operand(qs, s, 4 * g + j, STACK), start=True, stop=False)
                    ins = nc.tensor.matmul(out, pick[:, 4 * g + j, :], nmT[:], start=False, stop=True)
                ins.then_inc(st_ps, 1)

            def context(s, g):
                pe.wait_ge(exp_s, s.count(4, g + 1))
                if g == 0:
                    pe.wait_ge(vw_s, s.count(1, 1))
                    wait(pe, ctxT_s, s.count(1, 0))
                for j in range(4):
                    ins = nc.tensor.matmul(ps_ctx[32 * j:32 * j + SLOTW, g * P:(g + 1) * P], v_wide[s.k % 2][:, 4 * g + j, :],
                                           probs[g % 2][:, j, :], start=True, stop=True)
                ins.then_inc(av_s if g < 3 else ctx_ps, 1)

            def emit(s):
                one = s.plus(1).exists()
                if s.exists():
                    shifted(s, 0)
                if s.plus(-2).exists():
                    pe.wait_ge(aT_s, s.count(1, -1))
                    wait(pe, xnT_s, s.count(1, -2))
                    for h in range(HALVES):
                        ins = nc.tensor.matmul(ps_o, attnT[:, h, :], wo[:, h, :], start=(h == 0), stop=(h == HALVES - 1))
                    ins.then_inc(o_ps, 1)
                if s.exists():
                    if one:
                        scores(s.plus(1), 0)
                        scores(s.plus(1), 1)
                    shifted(s, 1)
                    context(s, 0)
                    shifted(s, 2)
                    if one:
                        scores(s.plus(1), 2)
                    context(s, 1)
                    shifted(s, 3)
                    if one:
                        scores(s.plus(1), 3)
                    context(s, 2)
                if s.plus(-1).exists():
                    pe.wait_ge(ctxT_s, s.count(1, 0))
                    wait(pe, lg_s, s.count(1, -2))
                    for g in range(4):
                        ins = nc.tensor.transpose(ps_ctxT[:, g * P:(g + 1) * P], ctxT[:, g * P:(g + 1) * P], ident[:])
                    ins.then_inc(ctxT_ps, 1)
                if s.plus(-2).exists():
                    pe.wait_ge(xn_s, s.count(1, -1))
                    wait(pe, x1_s, s.count(1, -1))
                    for h in range(HALVES):
                        ins = nc.tensor.transpose(ps_xnT[:, h * P:(h + 1) * P], xn[s.k % 2][:, h * P:(h + 1) * P], ident[:])
                    ins.then_inc(xnT_ps, 1)
                if s.exists():
                    context(s, 3)
                if one:
                    max_T(s.plus(1))
                if s.plus(-1).exists():
                    pe.wait_ge(attn_s, s.count(1, 0))
                if s.plus(-1).exists():
                    wait(pe, nmT_s, min_tile(s.count(1, 2)))
                    for h in range(HALVES):
                        ins = nc.tensor.transpose(ps_aT[:, h * P:(h + 1) * P], attn[:, h * P:(h + 1) * P], ident[:])
                    ins.then_inc(aT_ps, 1)
                if s.plus(-2).exists():
                    pe.wait_ge(xnT_s, s.count(1, -1))
                    for h in range(HALVES):
                        ins = nc.tensor.matmul(ps_lg, wr[:, h, :], xnT[:, h, :], start=(h == 0), stop=(h == HALVES - 1))
                    ins.then_inc(lg_ps, 1)

            def min_tile(v):
                return min(v, TILES) if isinstance(v, int) else v

            def max_T(s):
                pe.wait_ge(nm_s, s.count(1, 1))
                wait(pe, aT_s, s.count(1, -2))
                nc.tensor.transpose(ps_nmT, nm_parts[:].rearrange("p a h -> p (a h)"), ident_b[:]).then_inc(nmT_ps, 1)

            for g in range(4):
                scores(Step(0, 0), g)
            max_T(Step(0, 0))
            pe.wait_ge(pick_s, 5)
            pe.wait_ge(w_s, 64)
            steps(pe, emit, 2)


ROW0 = D + EXPERTS
KEY_BITS = 30
ROUNDS = KEY_BITS // 2
UNROLL = 5
SEG = P // EXPERTS
TOK_T = TOKENS // P


def running_count(nc, mask, tri, ones, ps):
    nc.tensor.matmul(ps[:, 0:EXPERTS * TOK_T], tri[:], mask, start=True, stop=True)
    return nc.tensor.matmul(ps[:, EXPERTS * TOK_T:], ones[:], mask, start=True, stop=True)


def route_top_k(nc, S, T):
    E, TT, N = EXPERTS, TOK_T, EXPERTS * TOK_T
    with ExitStack() as ctx:
        sb = lambda n, s, d=F32: ctx.enter_context(nc.sbuf_tensor(n, s, d))
        sem = ctx.enter_context(Semaphores(nc)).new
        score = S["score"]
        s_et = score[:].rearrange("p t e -> p e t")
        tmax, tsum = sb("tmax", [P, TT]), sb("tsum", [P, TT])
        ex = sb("ex", [P, TT, E])
        keys = sb("keys", [P, 2 * P])
        junk = sb("junk", [P, 3, 2 * P], BF16)
        diff_i = sb("diff_i", [P, P], I32)
        same = sb("same", [P, P], BF16)
        shift_i, one_i, bit_i = (sb(n, [P, ROUNDS, 3], I32) for n in ("shift_i", "one_i", "bit_i"))
        bit_f = sb("bit_f", [P, ROUNDS])
        thr, cand, step = (sb(n, [P, w], I32) for n, w in (("thr", 1), ("cand", 3), ("step", 1)))
        count = sb("count", [P, 3], BF16)
        count_f = sb("count_f", [P, 3])
        reached, n_reached = sb("reached", [P, 3], BF16), sb("n_reached", [P, 1])
        thr_row = sb("thr_row", [E, P])
        thr_b = sb("thr_b", [P, E])
        above, equal, chosen, early = (sb(n, [P, E, TT], BF16) for n in ("above", "equal", "chosen", "early"))
        scan = sb("scan", [P, E, TT])
        rank = sb("rank", [P, E, TT])
        n_above = sb("n_above", [P, E])
        pos_i, dig_i = sb("pos_i", [P, E, TT], I32), sb("dig_i", [P, 2, E, TT], I32)
        dig = sb("dig", [P, 2, E, TT], BF16)
        ramp_i, ramp = sb("ramp_i", [P, 32], I32), sb("ramp", [P, 32], BF16)
        tile_i, tile_no = sb("tile_i", [P, TT, 16], I32), sb("tile_no", [P, TT, 16], BF16)
        part_i, part_no = sb("part_i", [P, 1], I32), sb("part_no", [P, 1])
        hot_a = [sb(f"hot_a{i}", [P, TT, 32], BF16) for i in range(2)]
        hot_b = [sb(f"hot_b{i}", [P, TT, 16], BF16) for i in range(2)]
        hot_v = [sb(f"hot_v{i}", [P, TT, 2, 16], BF16) for i in range(2)]
        idx_b = sb("idx_b", [32, 4, E, 2, 4], BF16)
        idx_f = sb("idx_f", [P, E, 2, 4])
        spread = sb("spread", [32, 4, P], BF16)
        ps = [ctx.enter_context(nc.psum_tensor(f"pc{i}", [P, 512], F32)) for i in range(6)]
        ps_l, ps_k, ps_n, ps_t, ps_c, ps_i = ps
        (lg_s, mx_s, sub_s, ex_s, sum_s, rec_s, sc_s, keyT_s, key_s, iota_s, tab_s, bit_s, thr0_s, cand_s, cnt_s, cntb_s, tot_s,
         step_s, thr_s, row_s, thrT_s, thrb_s, cmp_s, cnt1_s, red_s, scan_s, off_s, rank_s, early_s, mix_s, ch_s, cnt2_s, pos_s,
         posi_s, dg_s, dgb_s, hot_s, hotb_s, hotv_s, hott_s, idx_ps, idxf_s, idxi_s, out_s, in_s) = (
            sem("pc_" + n) for n in (
                "lg", "mx", "sub", "ex", "sum", "rec", "sc", "keyT", "key", "iota", "tab", "bit", "thr0", "cand", "cnt", "cntb",
                "tot", "step", "thr", "row", "thrT", "thrb", "cmp", "cnt1", "red", "scan", "off", "rank", "early", "mix",
                "ch", "cnt2", "pos", "posi", "dg", "dgb", "hot", "hotb", "hotv", "hott", "idx_ps", "idxf", "idxi", "out", "in"))
        cleared_s, reach_s, sel_s = sem("pc_cleared"), sem("pc_reach"), sem("pc_sel")
        spr_ps = sem("pc_spr_ps")
        block = ctx.enter_context(nc.Block())

        @block.sync
        def _(sp):
            sp.dma_start(T["slots"].rearrange("(t p) d -> p t d", p=P),
                         S["zero"][:].unsqueeze(1).broadcast_to([P, TOKENS // P, ROW1])).then_inc(cleared_s, 16)
            sp.wait_ge(sc_s, 1)
            sp.dma_start(T["rows0"].rearrange("(t p) d -> p t d", p=P)[:, :, D:ROW0], score[:]).then_inc(out_s, 16)
            sp.wait_ge(out_s, 16)
            sp.wait_ge(cleared_s, 16)

        @block.gpsimd
        def _(pool):
            nc.gpsimd.iota(diff_i[:], [[-1, P]], base=P, channel_multiplier=1).then_inc(iota_s, 1)
            nc.gpsimd.iota(shift_i[:], [[-2, ROUNDS], [0, 3]], base=KEY_BITS - 2, channel_multiplier=0).then_inc(iota_s, 1)
            nc.gpsimd.iota(one_i[:], [[0, ROUNDS], [1, 3]], base=1, channel_multiplier=0).then_inc(iota_s, 1)
            nc.gpsimd.iota(ramp_i[:], [[1, 32]], base=0, channel_multiplier=0).then_inc(iota_s, 1)
            nc.gpsimd.iota(tile_i[:], [[1, TT], [0, 16]], base=0, channel_multiplier=0).then_inc(iota_s, 1)
            nc.gpsimd.iota(part_i[:], [[0, 1]], base=0, channel_multiplier=1).then_inc(iota_s, 1)
            nc.gpsimd.memset(spread[:], 0.0).then_inc(sel_s, 1)
            nc.gpsimd.memset(S["ones_b"][:], 1.0).then_inc(tab_s, 1)
            nc.gpsimd.memset(S["before"][:], 1.0).then_inc(tab_s, 1)
            nc.gpsimd.memset(S["keep"][:], 1.0).then_inc(tab_s, 1)
            pool.wait_ge(tab_s, 3)
            nc.gpsimd.affine_select(out=S["before"][:], in_=S["before"][:], compare_op=ALU.is_gt, fill=0.0, base=0,
                                    pattern=[[1, P]], channel_multiplier=-1).then_inc(tab_s, 1)
            nc.gpsimd.affine_select(out=S["keep"][:], in_=S["keep"][:], compare_op=ALU.is_gt, fill=0.0, base=0,
                                    pattern=[[0, E], [1, TT]], channel_multiplier=0).then_inc(tab_s, 1)
            pool.wait_ge(sel_s, 1)
            nc.gpsimd.affine_select(out=spread[:], in_=spread[:], compare_op=ALU.not_equal, fill=1.0, base=0,
                                    pattern=[[-1, 4], [1, P]], channel_multiplier=-4).then_inc(sel_s, 1)
            for e in range(E):
                pool.wait_ge(hotb_s, e + 1)
                if e >= 2:
                    pool.wait_ge(idx_ps, e - 1)
                nc.gpsimd.tensor_tensor(hot_v[e % 2][:, :, 1, :], hot_b[e % 2][:], tile_no[:], ALU.mult).then_inc(hott_s, 1)

        @block.scalar
        def _(act):
            act.wait_ge(sub_s, 1)
            nc.scalar.activation(ex[:], ex[:], ACT.Exp).then_inc(ex_s, 1)
            act.wait_ge(keyT_s, 1)
            nc.scalar.activation(keys[:], ps_k[:, 0:2 * P], ACT.Copy).then_inc(key_s, 1)
            act.wait_ge(bit_s, 8)
            for e in range(E):
                act.wait_ge(hotb_s, e + 1)
                if e >= 2:
                    act.wait_ge(idx_ps, e - 1)
                nc.scalar.activation(hot_v[e % 2][:, :, 0, :], hot_b[e % 2][:], ACT.Copy, scale=part_no[:]).then_inc(hotv_s, 1)

        @block.vector
        def _(dve):
            V = nc.vector
            dve.wait_ge(iota_s, 6)
            V.tensor_scalar(diff_i[:], diff_i[:], E - 1, None, ALU.bitwise_and).then_inc(bit_s, 1)
            V.tensor_tensor(bit_i[:], one_i[:], shift_i[:], ALU.logical_shift_left).then_inc(bit_s, 1)
            dve.wait_ge(bit_s, 2)
            V.tensor_scalar(same[:], diff_i[:], 0.0, None, ALU.is_equal).then_inc(bit_s, 1)
            V.tensor_copy(bit_f[:], bit_i[:, :, 0]).then_inc(bit_s, 1)
            V.tensor_copy(ramp[:], ramp_i[:]).then_inc(bit_s, 1)
            V.tensor_copy(tile_no[:], tile_i[:]).then_inc(bit_s, 1)
            V.tensor_copy(part_no[:], part_i[:]).then_inc(bit_s, 1)
            V.memset(thr[:], 0).then_inc(bit_s, 1)
            dve.wait_ge(lg_s, 1)
            lg = ps_l[:, 0:N].rearrange("p (t e) -> p t e", e=E)
            V.tensor_reduce(tmax[:], lg, AX.X, ALU.max).then_inc(mx_s, 1)
            dve.wait_ge(mx_s, 1)
            V.tensor_tensor(ex[:], lg, tmax[:].unsqueeze(2).broadcast_to([P, TT, E]), ALU.subtract).then_inc(sub_s, 1)
            dve.wait_ge(ex_s, 1)
            V.tensor_reduce(tsum[:], ex[:], AX.X, ALU.add).then_inc(sum_s, 1)
            dve.wait_ge(sum_s, 1)
            V.reciprocal(tsum[:], tsum[:]).then_inc(rec_s, 1)
            dve.wait_ge(rec_s, 1)
            V.tensor_tensor(score[:], ex[:], tsum[:].unsqueeze(2).broadcast_to([P, TT, E]), ALU.mult).then_inc(sc_s, 1)

            dve.wait_ge(key_s, 1)
            dve.wait_ge(bit_s, 8)
            with dve.Fori(0, ROUNDS // UNROLL) as r:
                for u in range(UNROLL):
                    i = r * UNROLL + u
                    done = r * UNROLL + (u + 1)
                    V.tensor_tensor(cand[:], thr[:].broadcast_to([P, 3]), bit_i[:, bass.ds(i, 1), :].rearrange("p a c -> p (a c)"),
                                    ALU.bitwise_or).then_inc(cand_s, 1)
                    dve.wait_ge(cand_s, done)
                    for c in range(3):
                        V.tensor_scalar(junk[:, c, :], keys[:], cand[:, c:c + 1].bitcast(F32), None, ALU.is_ge, ALU.add,
                                        accum_out=count_f[:, c:c + 1]).then_inc(cnt_s, 1)
                    dve.wait_ge(cnt_s, r * (3 * UNROLL) + 3 * (u + 1))
                    V.tensor_copy(count[:], count_f[:]).then_inc(cntb_s, 1)
                    dve.wait_ge(tot_s, done)
                    V.tensor_scalar(reached[:], ps_n[:, 0:3], CAP - 0.5, None, ALU.is_ge, ALU.add,
                                    accum_out=n_reached[:]).then_inc(reach_s, 1)
                    dve.wait_ge(reach_s, done)
                    V.tensor_scalar(step[:], n_reached[:], bit_f[:, bass.ds(i, 1)], None, ALU.mult).then_inc(step_s, 1)
                    dve.wait_ge(step_s, done)
                    V.tensor_tensor(thr[:], thr[:], step[:], ALU.bitwise_or).then_inc(thr_s, 1)
                    dve.wait_ge(thr_s, done)

            V.tensor_copy(thr_row[:], thr[0:E, :].bitcast(F32).broadcast_to([E, P])).then_inc(row_s, 1)
            dve.wait_ge(thrT_s, 1)
            V.tensor_copy(thr_b[:], ps_t[:, 0:E]).then_inc(thrb_s, 1)
            dve.wait_ge(thrb_s, 1)
            thr_et = thr_b[:].unsqueeze(2).broadcast_to([P, E, TT])
            V.tensor_tensor(above[:], s_et, thr_et, ALU.is_gt).then_inc(cmp_s, 1)
            V.tensor_tensor(equal[:], s_et, thr_et, ALU.is_equal).then_inc(cmp_s, 1)

            def ranks(ps_c, done):
                tot = ps_c[:, N:]
                V.tensor_tensor_scan(scan[:].rearrange("p e t -> p (e t)"), S["keep"][:].rearrange("p e t -> p (e t)"), tot, 0.0,
                                     ALU.mult, ALU.add).then_inc(scan_s, 1)
                dve.wait_ge(scan_s, done + 1)
                V.tensor_tensor(scan[:], scan[:], tot.rearrange("p (e t) -> p e t", e=E), ALU.subtract).then_inc(off_s, 1)
                dve.wait_ge(off_s, done + 1)
                V.tensor_tensor(rank[:], scan[:], ps_c[:, 0:N].rearrange("p (e t) -> p e t", e=E), ALU.add).then_inc(rank_s, 1)
                dve.wait_ge(rank_s, done + 1)

            dve.wait_ge(cnt1_s, 1)
            dve.wait_ge(tab_s, 5)
            V.tensor_reduce(n_above[:], ps_t[:, N:2 * N].rearrange("p (e t) -> p e t", e=E), AX.X, ALU.add).then_inc(red_s, 1)
            ranks(ps_c, 0)
            dve.wait_ge(red_s, 1)
            V.tensor_tensor(rank[:], rank[:], n_above[:].unsqueeze(2).broadcast_to([P, E, TT]), ALU.add).then_inc(early_s, 1)
            dve.wait_ge(early_s, 1)
            V.scalar_tensor_tensor(early[:].rearrange("p e t -> p (e t)"), rank[:].rearrange("p e t -> p (e t)"), CAP - 0.5,
                                   equal[:].rearrange("p e t -> p (e t)"), ALU.is_lt, ALU.mult).then_inc(mix_s, 1)
            dve.wait_ge(mix_s, 1)
            V.tensor_tensor(chosen[:], early[:], above[:], ALU.add).then_inc(ch_s, 1)
            dve.wait_ge(cnt2_s, 1)
            ranks(ps_i, 1)
            V.tensor_scalar(rank[:], rank[:], 2.0 * TOKENS, None, ALU.add).then_inc(pos_s, 1)
            dve.wait_ge(pos_s, 1)
            V.scalar_tensor_tensor(pos_i[:].rearrange("p e t -> p (e t)"), chosen[:].rearrange("p e t -> p (e t)"), -2.0 * TOKENS,
                                   rank[:].rearrange("p e t -> p (e t)"), ALU.mult, ALU.add).then_inc(posi_s, 1)
            dve.wait_ge(posi_s, 1)
            V.tensor_scalar(dig_i[:, 0], pos_i[:], 4, None, ALU.logical_shift_right).then_inc(dg_s, 1)
            V.tensor_scalar(dig_i[:, 1], pos_i[:], 15, None, ALU.bitwise_and).then_inc(dg_s, 1)
            dve.wait_ge(dg_s, 2)
            V.tensor_copy(dig[:], dig_i[:]).then_inc(dgb_s, 1)
            dve.wait_ge(dgb_s, 1)
            for e in range(E):
                par = e % 2
                if e >= 2:
                    dve.wait_ge(idx_ps, e - 1)
                    dve.wait_ge(hott_s, e - 1)
                    dve.wait_ge(hotv_s, e - 1)
                V.tensor_tensor(hot_b[par][:], ramp[:, 0:16].unsqueeze(1).broadcast_to([P, TT, 16]),
                                dig[:, 1, e, :].unsqueeze(2).broadcast_to([P, TT, 16]), ALU.is_equal).then_inc(hotb_s, 1)
                V.tensor_tensor(hot_a[par][:], ramp[:].unsqueeze(1).broadcast_to([P, TT, 32]),
                                dig[:, 0, e, :].unsqueeze(2).broadcast_to([P, TT, 32]), ALU.is_equal).then_inc(hot_s, 1)
            dve.wait_ge(idx_ps, E)
            V.tensor_copy(idx_b[:].rearrange("a g e v c -> a e v g c"),
                          ps_n[0:32, 0:E * 32].rearrange("a (e v g c) -> a e v g c", e=E, v=2, g=4)).then_inc(idxf_s, 1)
            dve.wait_ge(spr_ps, 1)
            V.tensor_copy(idx_f[:], ps_c[:, 0:E * 8].rearrange("p (e v c) -> p e v c", e=E, v=2)).then_inc(idxi_s, 1)
            dve.wait_ge(idxi_s, 1)
            V.scalar_tensor_tensor(S["idx"][:], idx_f[:, :, 1, :], float(P), idx_f[:, :, 0, :], ALU.mult, ALU.add)

        @block.tensor
        def _(pe):
            for t in range(TT):
                ins = nc.tensor.transpose(ps_l[:, t * E:(t + 1) * E], S["logitsT"][:, t * P:(t + 1) * P], S["ident"][0:E, 0:E])
            ins.then_inc(lg_s, 1)
            pe.wait_ge(sc_s, 1)
            for j in range(2):
                ins = nc.tensor.transpose(ps_k[:, j * P:(j + 1) * P], score[:, j * SEG:(j + 1) * SEG, :].rearrange("p t e -> p (t e)"),
                                          S["ident"][:])
            ins.then_inc(keyT_s, 1)
            pe.wait_ge(bit_s, 8)
            with pe.Fori(0, ROUNDS) as i:
                pe.wait_ge(cntb_s, i + 1)
                nc.tensor.matmul(ps_n[:, 0:3], same[:], count[:], start=True, stop=True).then_inc(tot_s, 1)
            pe.wait_ge(row_s, 1)
            nc.tensor.transpose(ps_t[:, 0:E], thr_row[:], S["ident"][0:E, 0:E]).then_inc(thrT_s, 1)
            pe.wait_ge(cmp_s, 2)
            pe.wait_ge(tab_s, 5)
            pe.wait_ge(thrb_s, 1)
            flat = lambda m: m[:].rearrange("p e t -> p (e t)")
            nc.tensor.matmul(ps_t[:, N:2 * N], S["ones_b"][:], flat(above), start=True, stop=True)
            running_count(nc, flat(equal), S["before"], S["ones_b"], ps_c).then_inc(cnt1_s, 1)
            pe.wait_ge(ch_s, 1)
            running_count(nc, flat(chosen), S["before"], S["ones_b"], ps_i).then_inc(cnt2_s, 1)
            for e in range(E):
                pe.wait_ge(hot_s, e + 1)
                pe.wait_ge(hotv_s, e + 1)
                pe.wait_ge(hott_s, e + 1)
                for t in range(TT):
                    ins = nc.tensor.matmul(ps_n[0:32, e * 32:(e + 1) * 32], hot_a[e % 2][:, t, :],
                                           hot_v[e % 2][:, t].rearrange("p v b -> p (v b)"), start=(t == 0), stop=(t == TT - 1))
                ins.then_inc(idx_ps, 1)
            pe.wait_ge(idxf_s, 1)
            pe.wait_ge(sel_s, 2)
            for g in range(4):
                ins = nc.tensor.matmul(ps_c[:, 0:E * 8], spread[:, g, :], idx_b[:, g].rearrange("a e v c -> a (e v c)"),
                                       start=(g == 0), stop=(g == 3))
            ins.then_inc(spr_ps, 1)


def expert_choice_ffn(nc, S, T):
    MT = -(-FFN // P)
    LAST = FFN - (MT - 1) * P
    GROUPS = EXPERTS // 2
    ST = CAP // P
    with ExitStack() as ctx:
        sb = lambda n, s, d=F32: ctx.enter_context(nc.sbuf_tensor(n, s, d))
        sem = ctx.enter_context(Semaphores(nc)).new
        ident = S["ident"]
        rows = [sb(f"rows{i}", [P, ST, ROW0]) for i in range(2)]
        gate = [sb(f"gate{i}", [P, ST]) for i in range(2)]
        gT = [sb(f"gT{i}", [P, HALVES, CAP]) for i in range(2)]
        w_up = sb("w_up", [P, HALVES, FFN])
        b_up = sb("b_up", [P, MT])
        w_dn = [sb(f"w_dn{i}", [P, MT, D]) for i in range(2)]
        mid = [[sb(f"mid{i}_{m}", [P if m < MT - 1 else 64, CAP]) for m in range(MT)] for i in range(2)]
        y = [sb(f"y{i}", [P, ST, D]) for i in range(2)]
        banks = [ctx.enter_context(nc.psum_tensor(f"pd{i}", [P, 512], F32)) for i in range(8)]
        ps_t, ps_y = banks[0:2], banks[2:4]
        ps_u = banks[4:8]
        rows_in = [sem(f"pd_rows{i}") for i in range(2)]
        dn_in = [sem(f"pd_dn{i}") for i in range(2)]
        up_in = sem("pd_up")
        added = sem("pd_added")
        one_s, t_ps, gT_s, gate_s, u_ps, mid_s, y_ps, y_s, b_in = (sem("pd_" + n) for n in (
            "one", "t_ps", "gT", "gate", "u_ps", "mid", "y_ps", "y", "b_in"))
        block = ctx.enter_context(nc.Block())

        def groups(engine, emit):
            emit(0, True, False)
            with engine.Fori(1, GROUPS - 1) as g:
                emit(g, False, False)
            emit(GROUPS - 1, False, True)

        @block.sync
        def _(sp):
            sp.wait_ge(one_s, 2)

            def emit(g, first, last):
                if not first:
                    sp.wait_ge(u_ps, g * 2 * MT)
                sp.dma_start(w_up[:], T["W_up"][bass.ds(g, 1)].rearrange("a (h p) f -> p (a h) f", p=P)).then_inc(up_in, 16)
                if not first:
                    sp.wait_ge(mid_s, g * 2 * MT)
                sp.dma_start(b_up[:, 0:MT - 1], T["b_up"][bass.ds(g, 1), 0:(MT - 1) * P].rearrange("a (m p) -> p (a m)", p=P),
                             allow_slow_non_contiguous=True).then_inc(b_in, 16)
                sp.dma_start(b_up[0:LAST, MT - 1:MT], T["b_up"][bass.ds(g, 1), (MT - 1) * P:].rearrange("a p -> p a"),
                             allow_slow_non_contiguous=True).then_inc(b_in, 16)
                for par in range(2):
                    if not first:
                        sp.wait_ge(y_ps, (g * 2 + (par - 1)) * (ST // 2))
                    e = bass.ds(g * 2 + par, 1)
                    sp.dma_start(w_dn[par][:, 0:MT - 1, :], T["W_down"][e, 0:(MT - 1) * P].rearrange("a (m p) d -> p (a m) d", p=P)
                                 ).then_inc(dn_in[par], 16)
                    sp.dma_start(w_dn[par][0:LAST, MT - 1, :], T["W_down"][e, (MT - 1) * P:].rearrange("a p d -> p (a d)")
                                 ).then_inc(dn_in[par], 16)
                    sp.dma_start(w_dn[par][LAST:LAST + 1, MT - 1, :], T["b_down"][e]).then_inc(dn_in[par], 16)

            groups(sp, emit)

        @block.gpsimd
        def _(pool):
            def gather(e, par, first):
                if not first:
                    pool.wait_ge(t_ps, e - 1)
                    pool.wait_ge(gate_s, e - 1)
                for c in range(ST):
                    pool.indirect_dma_start(
                        out=rows[par][:, c, :], out_offset=None, in_=T["rows0"],
                        in_offset=bass.IndirectOffsetOnAxis(ap=S["idx"][:, e, c:c + 1], axis=0)).then_inc(rows_in[par], 16)

            def add(e, par):
                pool.wait_ge(y_s, (e + 1) * ST)
                if e:
                    pool.wait_ge(added, e * 16 * ST)
                for c in range(ST):
                    pool.indirect_dma_start(
                        out=T["resid"], out_offset=bass.IndirectOffsetOnAxis(ap=S["idx"][:, e, c:c + 1], axis=0),
                        in_=y[par][:, c, :], in_offset=None, compute_op=ALU.add).then_inc(added, 16)

            gather(0, 0, True)
            gather(1, 1, True)
            for e in range(EXPERTS):
                add(e, e % 2)
                if e + 2 < EXPERTS:
                    gather(e + 2, e % 2, False)
            pool.wait_ge(added, EXPERTS * 16 * ST)

        @block.vector
        def _(dve):
            for i in range(2):
                nc.vector.memset(mid[i][MT - 1][:], 1.0).then_inc(one_s, 1)

            def prepare(g, par, first):
                e = g * 2 + par
                dve.wait_ge(t_ps, e + 1)
                if not first:
                    dve.wait_ge(u_ps, (e - 1) * MT)
                nc.vector.tensor_copy(gT[par][:, 1, :], ps_t[1][:]).then_inc(gT_s, 1)
                dve.wait_ge(rows_in[par], (g + 1) * 16 * ST)
                nc.vector.tensor_scalar(gate[par][:], rows[par][:, :, bass.ds(g * 2 + (D + par), 1)].rearrange("p c a -> p (c a)"),
                                        S["tanh_g"][:, 2:3], None, ALU.mult).then_inc(gate_s, 1)

            def emit(g, first, last):
                for par in range(2):
                    e = g * 2 + par
                    if par == 0:
                        prepare(g, 1, first)
                    elif not last:
                        prepare(g + 1, 0, False)
                    dve.wait_ge(gate_s, e + 1)
                    for c in range(ST):
                        if c % 2 == 0:
                            dve.wait_ge(y_ps, e * (ST // 2) + (c // 2 + 1))
                        if not first and c == 0:
                            dve.wait_ge(added, (e - 1) * 16 * ST)
                        nc.vector.tensor_scalar(y[par][:, c, :], ps_y[c // 2][:, c % 2 * D:(c % 2 + 1) * D], gate[par][:, c:c + 1],
                                                None, ALU.mult).then_inc(y_s, 1)

            prepare(0, 0, True)
            groups(dve, emit)

        @block.scalar
        def _(act):
            act.wait_ge(one_s, 2)

            def emit(g, first, last):
                for par in range(2):
                    e = g * 2 + par
                    act.wait_ge(t_ps, e + 1)
                    if not first:
                        act.wait_ge(u_ps, (e - 1) * MT)
                    nc.scalar.activation(gT[par][:, 0, :], ps_t[0][:], ACT.Copy).then_inc(gT_s, 1)
                    act.wait_ge(b_in, (g + 1) * 32)
                    for m in range(MT):
                        n = P if m < MT - 1 else LAST
                        act.wait_ge(u_ps, e * MT + (m + 1))
                        if not first:
                            act.wait_ge(y_ps, (e - 1) * (ST // 2))
                        nc.scalar.activation(mid[par][m][0:n, :], ps_u[(par * MT + m) % 4][0:n, :], ACT.Silu,
                                             bias=b_up[0:n, m:m + 1]).then_inc(mid_s, 1)

            groups(act, emit)

        @block.tensor
        def _(pe):
            def turn(e, par, n16, first):
                pe.wait_ge(rows_in[par], n16)
                if not first:
                    pe.wait_ge(gT_s, e * 2)
                for h in range(HALVES):
                    for c in range(ST):
                        ins = nc.tensor.transpose(ps_t[h][:, c * P:(c + 1) * P], rows[par][:, c, h * P:(h + 1) * P], ident[:])
                ins.then_inc(t_ps, 1)

            def up(g, e, par, first):
                pe.wait_ge(up_in, (g + 1) * 16)
                pe.wait_ge(gT_s, (e + 1) * 2)
                for m in range(MT):
                    n = P if m < MT - 1 else LAST
                    k = par * MT + m
                    if not (first and k < 4):
                        pe.wait_ge(mid_s, e * MT + (m - 3))
                    for h in range(HALVES):
                        ins = nc.tensor.matmul(ps_u[k % 4][0:n, :], w_up[:, h, m * P:m * P + n], gT[par][:, h, :],
                                               start=(h == 0), stop=(h == HALVES - 1))
                    ins.then_inc(u_ps, 1)

            def down(g, e, par, first):
                pe.wait_ge(dn_in[par], (g + 1) * 48)
                pe.wait_ge(mid_s, (e + 1) * MT)
                for c in range(ST):
                    if c == 0 and not (first and par == 0):
                        pe.wait_ge(y_s, e * ST)
                    for m in range(MT):
                        n = P if m < MT - 1 else LAST + 1
                        ins = nc.tensor.matmul(ps_y[c // 2][:, c % 2 * D:(c % 2 + 1) * D], mid[par][m][0:n, c * P:(c + 1) * P],
                                               w_dn[par][0:n, m, :], start=(m == 0), stop=(m == MT - 1))
                    if c % 2:
                        ins.then_inc(y_ps, 1)

            def emit(g, first, last):
                for par in range(2):
                    e = g * 2 + par
                    up(g, e, par, first)
                    if not (last and par == 1):
                        turn(e + 1, 1 - par, (g + (1 + par)) * 16 * ST, False)
                    down(g, e, par, first)

            turn(0, 0, 16 * ST, True)
            groups(pe, emit)


ROW1 = D + 4
DROPPED = 2 * TOKENS


def deep_steps(engine, emit, head, tail):
    for k in range(-head, 8):
        emit(Step(0, k))
    with engine.Fori(2, TILES // 4 - 1) as base:
        for k in range(4):
            emit(Step(base, k))
    for k in range(4 + tail):
        emit(Step(TILES // 4 - 1, k))


def bidirectional_attention(nc, S, T):
    E, HEAD, TAIL = EXPERTS, 3, 10
    with ExitStack() as ctx:
        sb = lambda n, s, d=F32: ctx.enter_context(nc.sbuf_tensor(n, s, d))
        four = lambda n, s, d=F32: [sb(f"{n}{i}", s, d) for i in range(4)]
        sem = ctx.enter_context(Semaphores(nc)).new
        ident = S["ident"]
        w_f = sb("w_f", [P, 4, HALVES, D])
        w_sim = sb("w_sim", [P, 3, HALVES])
        w1_row, b_sim = sb("w1_row", [P, D]), sb("b_sim", [P, 1])
        b_qv = sb("b_qv", [P, D])
        wg = sb("wg", [P, HALVES, EXPERTS])
        x_in, c_in, xb = four("dx_in", [P, D]), four("dc_in", [P, D]), four("dxb", [P, D])
        enc = four("enc", [P, D + 1])
        stats, moments = four("d_stats", [P, 6]), four("d_moments", [P, 2])
        vareps, rstd = four("d_vareps", [P, 1]), four("d_rstd", [P, 1])
        stats4, moments4 = four("d_stats4", [P, 6]), four("d_moments4", [P, 2])
        vareps4 = four("d_vareps4", [P, 1])
        encT, encW, hqT, ehqT = (four(n, [P, HALVES, P]) for n in ("encT", "encW", "hqT", "ehqT"))
        cT = four("d_cT", [P, HALVES, P])
        neg_max, row_sum, inv = four("d_neg_max", [P, 1]), four("d_row_sum", [P, 1]), four("d_inv", [P, 1])
        a_w, a_n, aT = four("a_w", [P, P]), four("a_n", [P, P]), four("d_aT", [P, P])
        prod = four("d_prod", [P, D])
        s1, v, v_max, v_sub, v_exp = (four("d_" + n, [P, 1]) for n in ("s1", "v", "vmax", "vsub", "vexp"))
        inv_b, hc_row, hc_col = four("d_inv_b", [1, 1]), four("d_hc_row", [1, D + 1]), four("d_hc_col", [P, HALVES])
        w_c = four("d_w_c", [P, HALVES, D])
        row4 = four("d_row4", [P, D + 2])
        xn4, x4T = four("d_xn4", [P, D]), four("d_x4T", [P, HALVES, P])
        rows = sb("d_rows", [P, TILES, ROW1])
        lgT = sb("r_lgT", [EXPERTS, QUAD, P])
        prob, first = sb("r_prob", [P, QUAD, E]), sb("r_first", [P, QUAD, E])
        rev_i, rev = sb("r_rev_i", [P, QUAD, E], I32), sb("r_rev", [P, QUAD, E])
        base_i, base = sb("r_base_i", [P, QUAD, E], I32), sb("r_base", [P, QUAD, E])
        tok_i = sb("r_tok_i", [P, TILES], I32)
        tmax, tsum, inv_e, pmax, best = (sb("r_" + n, [P, QUAD]) for n in ("tmax", "tsum", "inv", "pmax", "best"))
        chosen = sb("r_chosen", [P, QUAD, E], BF16)
        seen = sb("r_seen", [P, E])
        rank, kept, place = sb("r_rank", [P, QUAD, E]), sb("r_kept", [P, QUAD, E]), sb("r_place", [P, QUAD, E])
        slot = sb("r_slot", [P, QUAD])
        dest = sb("r_dest", [P, QUAD, 1], I32)
        pool_spare, route_spare = sb("r_pool_spare", [P, 1]), sb("r_spare", [P, 1])
        ps = [ctx.enter_context(nc.psum_tensor(f"pe{i}", [P, 512], F32)) for i in range(8)]
        ps_t, ps_sim, ps_route, ps_hq, ps_out, ps_row, ps_col, ps_x4 = ps
        ps_a, ps_lg = ps_sim, ps_x4
        wf_s, w_s, one_s, thb_s, tab_s = sem("pe_wf"), sem("pe_w"), sem("pe_one"), sem("pe_thb"), sem("pe_tab")
        x_in_s, c_in_s = [sem(f"pe_xin{i}") for i in range(4)], [sem(f"pe_cin{i}") for i in range(4)]
        (t_ps, enc_s, encT_s, cT_s, encW_s, sim_ps, max_s, exp_s, inv_s, an_s, a_ps, aT_s, hq_ps, hqT_s, ehqT_s, prod_s, s1_s, v_s,
         vmax_s, vsub_s, vexp_s, row_ps, invb_s, row_s, col_ps, col_s, wc_s, out_ps, x3_s, st_s, mom_s, ve_s, rstd_s, st4_s,
         mom4_s, ve4_s, rstd4_s, xn4_s, x4_ps, x4T_s, lg_ps, lg_s, xb_s, keep_s, stored_s) = (sem("pe_" + n) for n in (
            "t_ps", "enc", "encT", "cT", "encW", "sim_ps", "max", "exp", "inv", "an", "a_ps", "aT", "hq_ps", "hqT", "ehqT",
            "prod", "s1", "v", "vmax", "vsub", "vexp", "row_ps", "invb", "row", "col_ps", "col", "wc", "out_ps", "x3", "st", "mom", "ve",
            "rstd", "st4", "mom4", "ve4", "rstd4", "xn4", "x4_ps", "x4T", "lg_ps", "lg", "xb", "keep", "stored"))
        lt_ps, sub_s, pexp_s, chosen_s, cnt_ps, dest_s, sent_s, free_s, chain = (sem("pr_" + n) for n in (
            "lt_ps", "sub", "exp", "chosen", "cnt_ps", "dest", "sent", "free", "chain"))
        block = ctx.enter_context(nc.Block())
        x_t = T["resid"].rearrange("(t p) d -> p t d", p=P)
        c_t = T["ctx"].rearrange("(t p) d -> p t d", p=P)
        out_t = T["out"].rearrange("(t p) d -> p t d", p=P)
        one = lambda ap: ap.rearrange("p a d -> p (a d)")

        def quad_of(s, k):
            return s.plus(-k)

        def at(u, per, extra):
            return u.base * per + (u.k // 4 * per + extra)

        @block.sync
        def _(sp):
            def load(s):
                slot4 = s.k % 4
                wait(sp, enc_s, s.count(1, -3))
                wait(sp, xb_s, s.count(1, -3))
                sp.dma_start(x_in[slot4][:], one(x_t[:, bass.ds(s.tile(), 1), :])).then_inc(x_in_s[slot4], 16)
                wait(sp, hq_ps, s.count(1, -3))
                sp.dma_start(c_in[slot4][:], one(c_t[:, bass.ds(s.tile(), 1), :])).then_inc(c_in_s[slot4], 16)

            load(Step(0, 0))
            load(Step(0, 1))
            sp.dma_start(w1_row[:], T["w_sim"][0:D].partition_broadcast(P)).then_inc(w_s, 16)
            sp.dma_start(w_sim[:], T["w_sim"].rearrange("(w h p) -> p w h", p=P, h=HALVES), allow_slow_non_contiguous=True).then_inc(w_s, 16)
            sp.dma_start(b_sim[:], T["b_sim"].partition_broadcast(P)).then_inc(w_s, 16)
            sp.dma_start(b_qv[:], T["b_qv"].partition_broadcast(P)).then_inc(w_s, 16)
            sp.dma_start(wg[:], T["wg"].rearrange("(h p) n -> p h n", p=P)).then_inc(w_s, 16)
            load(Step(0, 2))
            load(Step(0, 3))
            sp.dma_start(w_f[:], T["W_qv"].rearrange("(b h p) n -> p b h n", p=P, h=HALVES)).then_inc(wf_s, 16)

            def emit(s):
                if s.exists() and s.plus(4).exists():
                    load(s.plus(4))
                u = quad_of(s, 7)
                if s.k % 4 == 3 and u.exists():
                    sp.wait_ge(keep_s, u.count(1, 4))
                    sp.dma_start(out_t[:, bass.ds(u.tile(), QUAD), :], rows[:, bass.ds(u.tile(), QUAD), 0:D]).then_inc(stored_s, 16)

            deep_steps(sp, emit, 0, TAIL)
            sp.wait_ge(stored_s, 16 * TILES // QUAD)

        @block.gpsimd
        def _(pool):
            G = nc.gpsimd
            for i in range(4):
                G.memset(enc[i][:, D:D + 1], 1.0).then_inc(one_s, 1)
            G.iota(rev_i[:], [[0, QUAD], [-1, E]], base=E, channel_multiplier=0).then_inc(tab_s, 1)
            G.iota(base_i[:], [[0, QUAD], [CAP, E]], base=-DROPPED, channel_multiplier=0).then_inc(tab_s, 1)
            G.iota(tok_i[:], [[-P, TILES]], base=TOKENS, channel_multiplier=-1).then_inc(tab_s, 1)

            def power(u, mom, mom_sem, ve, ve_sem, out, out_sem):
                pool.wait_ge(mom_sem, u.count(1, 1))
                G.tensor_tensor(ve[u.k % 4][:], mom[u.k % 4][:, 1:2], S["eps"][:, 0:1], ALU.add).then_inc(ve_sem, 1)
                pool.wait_ge(ve_sem, u.count(1, 1))
                G.tensor_tensor(out[u.k % 4], ve[u.k % 4][:], S["minus_half"][:, 0:1], ALU.pow).then_inc(out_sem, 1)

            rstd_out = [t[:] for t in rstd]
            rstd4_out = [t[:, D + 1:D + 2] for t in row4]

            def emit(s):
                slot4 = s.k % 4
                u = quad_of(s, 14)
                if s.k % 4 == 2 and u.exists():
                    pool.wait_ge(sent_s, at(u, 16 * QUAD, 16 * QUAD))
                    G.memset(pool_spare[:], 0.0).then_inc(free_s, 1)
                u = s.plus(1)
                if u.exists():
                    pool.wait_ge(enc_s, u.count(1, 1))
                    wait(pool, s1_s, u.count(1, -3))
                    G.tensor_tensor(prod[u.k % 4][:], enc[u.k % 4][:, 0:D], w1_row[:], ALU.mult).then_inc(prod_s, 1)
                if s.exists():
                    pool.wait_ge(v_s, s.count(1, 1))
                    pool.wait_ge(x_in_s[slot4], s.dma(4))
                    wait(pool, x3_s, s.count(1, -3))
                    G.tensor_tensor(xb[slot4][:], x_in[slot4][:], b_qv[:], ALU.add).then_inc(xb_s, 1)
                    G.partition_all_reduce(v_max[slot4][:], v[slot4][:], P, REDUCE_MAX).then_inc(vmax_s, 1)
                u = s.plus(-3)
                if u.exists():
                    power(u, moments4, mom4_s, vareps4, ve4_s, rstd4_out, rstd4_s)
                if s.exists():
                    pool.wait_ge(hqT_s, s.count(1, 1))
                    G.tensor_tensor(ehqT[slot4][:], hqT[slot4][:], encT[slot4][:], ALU.mult).then_inc(ehqT_s, 1)
                u = s.plus(3)
                if u.exists():
                    power(u, moments, mom_s, vareps, ve_s, rstd_out, rstd_s)
                for k, sent in ((3, (0,)), (0, (1,)), (1, (2, 3))):
                    u = quad_of(s, 11 + (k + 1) % 4)
                    if s.k % 4 == k and u.exists():
                        pool.wait_ge(dest_s, at(u, 1, 1))
                        for j in sent:
                            pool.indirect_dma_start(out=T["slots"], out_offset=bass.IndirectOffsetOnAxis(ap=dest[:, j, :], axis=0),
                                                    in_=rows[:, u.tile() + j, :], in_offset=None,
                                                    bounds_check=TOKENS - 1, oob_is_err=False).then_inc(sent_s, 16)

            G.memset(pool_spare[:], 0.0).then_inc(free_s, 1)
            for tile in range(-HEAD, TILES + TAIL):
                if tile == -1:
                    pool.wait_ge(w_s, 80)
                    G.tensor_scalar(b_qv[:], b_qv[:], S["tanh_g"][:, 1:2], None, ALU.mult).then_inc(thb_s, 1)
                    pool.wait_ge(thb_s, 1)
                emit(Step(0, tile))
            pool.wait_ge(sent_s, 16 * TILES)

        @block.vector
        def _(dve):
            V = nc.vector

            def statistics(u):
                i = u.k % 4
                dve.wait_ge(x_in_s[i], u.dma(4))
                V.bn_stats(stats[i][:], x_in[i][:]).then_inc(st_s, 1)
                settle(nc, S, dve, st_s, u.count(1, 1))
                V.bn_aggr(moments[i][:], stats[i][:]).then_inc(mom_s, 1)

            def normalise(u):
                i = u.k % 4
                dve.wait_ge(mom_s, u.count(1, 1))
                dve.wait_ge(rstd_s, u.count(1, 1))
                V.tensor_scalar(enc[i][:, 0:D], x_in[i][:], moments[i][:, 0:1], rstd[i][:],
                                ALU.subtract, ALU.mult).then_inc(enc_s, 1)

            def weigh(u):
                dve.wait_ge(encT_s, u.count(1, 1))
                for h in range(HALVES):
                    V.tensor_scalar(encW[u.k % 4][:, h, :], encT[u.k % 4][:, h, :], w_sim[:, 2, h:h + 1], w_sim[:, 1, h:h + 1],
                                    ALU.mult, ALU.add).then_inc(encW_s, 1)

            def row_max(u):
                i = u.k % 4
                dve.wait_ge(sim_ps, u.count(1, 1))
                V.tensor_reduce(neg_max[i][:], ps_sim[:, 0:P], AX.X, ALU.max, negate=True).then_inc(max_s, 1)
                dve.wait_ge(s1_s, u.count(1, 1))
                dve.wait_ge(max_s, u.count(1, 1))
                V.tensor_scalar(v[i][:], s1[i][:], b_sim[:], neg_max[i][:], ALU.add, ALU.subtract).then_inc(v_s, 1)

            def sub_max(u):
                i = u.k % 4
                dve.wait_ge(vmax_s, u.count(1, 1))
                V.tensor_tensor(v_sub[i][:], v[i][:], v_max[i][:], ALU.subtract).then_inc(vsub_s, 1)

            def context_sum(u):
                i = u.k % 4
                dve.wait_ge(row_s, u.count(1, 1))
                V.reciprocal(inv_b[i][:], hc_row[i][:, D:D + 1]).then_inc(invb_s, 1)

            def fold(u):
                i = u.k % 4
                dve.wait_ge(col_ps, u.count(1, 1))
                V.tensor_copy(hc_col[i][:], ps_col[:, 0:HALVES]).then_inc(col_s, 1)
                dve.wait_ge(col_s, u.count(1, 1))
                for h in range(HALVES):
                    V.scalar_tensor_tensor(w_c[i][:, h, :], w_f[:, 3, h, :], hc_col[i][:, h:h + 1], w_f[:, 0, h, :],
                                           ALU.mult, ALU.add).then_inc(wc_s, 1)

            def invert_sum(u):
                i = u.k % 4
                dve.wait_ge(exp_s, u.count(1, 1))
                V.reciprocal(inv[i][:], row_sum[i][:]).then_inc(inv_s, 1)

            def residual(u):
                i = u.k % 4
                dve.wait_ge(out_ps, u.count(1, 1))
                dve.wait_ge(xb_s, u.count(1, 1))
                wait(dve, keep_s, u.count(1, -3))
                V.scalar_tensor_tensor(row4[i][:, 0:D], ps_out[:, 0:D], S["tanh_g"][:, 1:2], xb[i][:], ALU.mult, ALU.add).then_inc(x3_s, 1)
                dve.wait_ge(x3_s, u.count(1, 1))
                V.bn_stats(stats4[i][:], row4[i][:, 0:D]).then_inc(st4_s, 1)

            def aggregate(u):
                i = u.k % 4
                settle(nc, S, dve, st4_s, u.count(1, 1))
                V.bn_aggr(moments4[i][:], stats4[i][:]).then_inc(mom4_s, 1)

            def normalise4(u):
                i = u.k % 4
                dve.wait_ge(mom4_s, u.count(1, 1))
                dve.wait_ge(rstd4_s, u.count(1, 1))
                V.tensor_copy(row4[i][:, D:D + 1], moments4[i][:, 0:1])
                V.tensor_scalar(xn4[i][:], row4[i][:, 0:D], moments4[i][:, 0:1], row4[i][:, D + 1:D + 2],
                                ALU.subtract, ALU.mult).then_inc(xn4_s, 1)

            LINKS = 13
            over_e = lambda m: m[:].unsqueeze(2).broadcast_to([P, QUAD, E])
            flat = lambda m: m[:].rearrange("p t e -> p (t e)")
            route = lambda i: ps_route[:, i * QUAD * E:(i + 1) * QUAD * E].rearrange("p (t e) -> p t e", e=E)

            def link(u, i, ins):
                ins.then_inc(chain, 1)
                dve.wait_ge(chain, at(u, LINKS, i))

            def route_shift(u):
                dve.wait_ge(lt_ps, at(u, 1, 1))
                link(u, 1, V.tensor_reduce(tmax[:], route(0), AX.X, ALU.max))
                V.tensor_tensor(prob[:], route(0), over_e(tmax), ALU.subtract).then_inc(sub_s, 1)

            def route_choose(u):
                dve.wait_ge(pexp_s, at(u, 1, 1))
                link(u, 2, V.tensor_reduce(tsum[:], prob[:], AX.X, ALU.add))
                link(u, 3, V.reciprocal(inv_e[:], tsum[:]))
                link(u, 4, V.tensor_tensor(prob[:], prob[:], over_e(inv_e), ALU.mult))
                link(u, 5, V.tensor_reduce(pmax[:], prob[:], AX.X, ALU.max))
                link(u, 6, V.tensor_tensor(first[:], prob[:], over_e(pmax), ALU.is_equal))
                link(u, 7, V.tensor_tensor(first[:], first[:], rev[:], ALU.mult))
                link(u, 8, V.tensor_reduce(best[:], first[:], AX.X, ALU.max))
                V.tensor_tensor(chosen[:], first[:], over_e(best), ALU.is_equal).then_inc(chosen_s, 1)

            def route_place(u):
                dve.wait_ge(cnt_ps, at(u, 1, 1))
                link(u, 9, V.tensor_tensor(rank[:], route(1), seen[:].unsqueeze(1).broadcast_to([P, QUAD, E]), ALU.add))
                V.tensor_tensor(seen[:], seen[:], ps_route[:, 2 * QUAD * E:2 * QUAD * E + E], ALU.add)
                V.tensor_tensor(place[:], rank[:], base[:], ALU.add)
                link(u, 10, V.scalar_tensor_tensor(flat(kept), flat(rank), CAP - 0.5, flat(chosen), ALU.is_lt, ALU.mult))
                link(u, 11, V.tensor_tensor(place[:], place[:], kept[:], ALU.mult))
                V.tensor_scalar(rows[:, bass.ds(u.tile(), QUAD), D + 2], pmax[:], S["tanh_g"][:, 3:4], None, ALU.mult)
                link(u, 12, V.tensor_reduce(slot[:], place[:], AX.X, ALU.add))
                dve.wait_ge(free_s, at(u, 1, 1))
                link(u, 13, V.tensor_scalar(dest[:, :, 0], slot[:], float(DROPPED), None, ALU.add))
                dve.wait_ge(keep_s, u.count(1, 4))
                V.memset(route_spare[:], 0.0).then_inc(dest_s, 1)

            def emit(s):
                now = s.exists()
                if isinstance(s.base, int) and s.tile() == -1:
                    dve.wait_ge(w_s, 80)
                if isinstance(s.base, int) and s.tile() == 2:
                    dve.wait_ge(wf_s, 16)
                if now:
                    row_max(s)
                if s.plus(-4).exists():
                    normalise4(s.plus(-4))
                if now:
                    invert_sum(s)
                if s.plus(-2).exists():
                    context_sum(s.plus(-2))
                if s.plus(-1).exists():
                    sub_max(s.plus(-1))
                if s.plus(3).exists():
                    statistics(s.plus(3))
                if s.plus(2).exists():
                    normalise(s.plus(2))
                if s.plus(-3).exists():
                    residual(s.plus(-3))
                if s.plus(-3).exists():
                    aggregate(s.plus(-3))
                if s.plus(1).exists():
                    weigh(s.plus(1))
                if s.plus(-2).exists():
                    fold(s.plus(-2))
                if s.k % 4 == 0 and quad_of(s, 8).exists():
                    route_shift(quad_of(s, 8))
                if s.k % 4 == 1 and quad_of(s, 9).exists():
                    route_choose(quad_of(s, 9))
                if s.k % 4 == 2 and quad_of(s, 10).exists():
                    route_place(quad_of(s, 10))

            dve.wait_ge(one_s, 4)
            dve.wait_ge(tab_s, 3)
            V.tensor_copy(rev[:], rev_i[:])
            V.tensor_copy(base[:], base_i[:])
            V.memset(seen[:], 0.0)
            V.tensor_copy(rows[:, :, D + 3], tok_i[:]).then_inc(tab_s, 1)
            dve.wait_ge(tab_s, 4)
            deep_steps(dve, emit, HEAD, TAIL)

        @block.scalar
        def _(act):
            def copy(dst, src, s_):
                nc.scalar.activation(dst, src, ACT.Copy).then_inc(s_, 1)

            def emit(s):
                halves = lambda p: p.rearrange("p (h t) -> p h t", h=HALVES)
                i = s.k % 4
                u4 = s.plus(-4)
                j = u4.k % 4
                if s.exists():
                    act.wait_ge(prod_s, s.count(1, 1))
                    nc.scalar.activation(prod[i][:], prod[i][:], ACT.Copy, accum_out=s1[i][:]).then_inc(s1_s, 1)
                    act.wait_ge(max_s, s.count(1, 1))
                    nc.scalar.activation(a_w[i][:], ps_sim[:, 0:P], ACT.Exp, bias=neg_max[i][:], accum_out=row_sum[i][:]).then_inc(exp_s, 1)
                    act.wait_ge(inv_s, s.count(1, 1))
                    nc.scalar.activation(a_n[i][:], a_w[i][:], ACT.Copy, scale=inv[i][:]).then_inc(an_s, 1)
                if u4.exists():
                    act.wait_ge(xn4_s, u4.count(1, 1))
                    copy(one(rows[:, bass.ds(u4.tile(), 1), 0:D + 2]), row4[j][:], keep_s)
                if s.plus(-1).exists():
                    v_i = (s.k - 1) % 4
                    act.wait_ge(vsub_s, s.count(1, 0))
                    nc.scalar.activation(v_exp[v_i][:], v_sub[v_i][:], ACT.Exp).then_inc(vexp_s, 1)
                u = s.plus(1)
                if u.exists():
                    act.wait_ge(t_ps, u.count(1, 1))
                    copy(encT[u.k % 4][:], halves(ps_t[:, 0:D]), encT_s)
                    copy(cT[u.k % 4][:], halves(ps_t[:, D:2 * D]), cT_s)
                if s.exists():
                    act.wait_ge(a_ps, s.count(1, 1))
                    copy(aT[i][:], ps_a[:, P:2 * P], aT_s)
                if u4.exists():
                    act.wait_ge(x4_ps, u4.count(1, 1))
                    copy(x4T[j][:], halves(ps_x4[:, 0:D]), x4T_s)
                if s.exists():
                    act.wait_ge(hq_ps, s.count(1, 1))
                    copy(hqT[i][:], halves(ps_hq[:, 0:D]), hqT_s)
                u = s.plus(-1)
                if u.exists():
                    act.wait_ge(row_ps, u.count(1, 1))
                    copy(hc_row[u.k % 4][:], ps_row[0:1, 0:D + 1], row_s)
                if u4.exists():
                    act.wait_ge(lg_ps, u4.count(1, 1))
                    wait(act, lt_ps, at(u4.plus(-j), 1, 0))
                    copy(lgT[:, j, :], ps_lg[0:EXPERTS, D:D + P], lg_s)
                u = quad_of(s, 8)
                if s.k % 4 == 0 and u.exists():
                    act.wait_ge(sub_s, at(u, 1, 1))
                    nc.scalar.activation(prob[:], prob[:], ACT.Exp).then_inc(pexp_s, 1)

            deep_steps(act, emit, HEAD, TAIL)

        @block.tensor
        def _(pe):
            M = nc.tensor

            def emit(s):
                i = s.k % 4
                if isinstance(s.base, int) and s.tile() == 3:
                    pe.wait_ge(w_s, 80)
                    pe.wait_ge(wf_s, 16)
                if s.exists():
                    pe.wait_ge(encW_s, s.count(2, 2))
                    pe.wait_ge(cT_s, s.count(1, 1))
                    wait(pe, aT_s, s.count(1, 0))
                    for h in range(HALVES):
                        ins = M.matmul(ps_sim[:, 0:P], encW[i][:, h, :], cT[i][:, h, :], start=(h == 0), stop=(h == HALVES - 1))
                    ins.then_inc(sim_ps, 1)
                u = s.plus(-3)
                if u.exists():
                    pe.wait_ge(ehqT_s, u.count(1, 1))
                    pe.wait_ge(wc_s, u.count(2, 2))
                    wait(pe, x3_s, u.count(1, 0))
                    n, j = 0, u.k % 4
                    for op, w in ((hqT[j], w_f[:, 1]), (ehqT[j], w_f[:, 2]), (encT[j], w_c[j][:])):
                        for h in range(HALVES):
                            ins = M.matmul(ps_out[:, 0:D], op[:, h, :], w[:, h, :], start=(n == 0), stop=(n == 5))
                            n += 1
                    ins.then_inc(out_ps, 1)
                u = s.plus(1)
                if u.exists():
                    j = u.k % 4
                    pe.wait_ge(enc_s, u.count(1, 1))
                    pe.wait_ge(c_in_s[j], u.dma(4))
                    wait(pe, cT_s, u.count(1, 0))
                    for h in range(HALVES):
                        M.transpose(ps_t[:, h * P:(h + 1) * P], enc[j][:, h * P:(h + 1) * P], ident[:])
                    for h in range(HALVES):
                        ins = M.transpose(ps_t[:, D + h * P:D + (h + 1) * P], c_in[j][:, h * P:(h + 1) * P], ident[:])
                    ins.then_inc(t_ps, 1)
                if s.exists():
                    pe.wait_ge(an_s, s.count(1, 1))
                    M.transpose(ps_a[:, P:2 * P], a_n[i][:], ident[:]).then_inc(a_ps, 1)
                u = s.plus(-4)
                if u.exists():
                    pe.wait_ge(xn4_s, u.count(1, 1))
                    wait(pe, lg_s, u.count(1, 0))
                    for h in range(HALVES):
                        ins = M.transpose(ps_x4[:, h * P:(h + 1) * P], xn4[u.k % 4][:, h * P:(h + 1) * P], ident[:])
                    ins.then_inc(x4_ps, 1)
                u = s.plus(-1)
                if u.exists():
                    pe.wait_ge(vexp_s, u.count(1, 1))
                    wait(pe, row_s, u.count(1, 0))
                    M.matmul(ps_row[0:1, 0:D + 1], v_exp[u.k % 4][:], enc[u.k % 4][:], start=True, stop=True).then_inc(row_ps, 1)
                u = s.plus(-2)
                if u.exists():
                    pe.wait_ge(row_s, u.count(1, 1))
                    pe.wait_ge(invb_s, u.count(1, 1))
                    wait(pe, col_s, u.count(1, 0))
                    for h in range(HALVES):
                        ins = M.matmul(ps_col[:, h:h + 1], hc_row[u.k % 4][:, h * P:(h + 1) * P], inv_b[u.k % 4][:], start=True, stop=True)
                    ins.then_inc(col_ps, 1)
                if s.exists():
                    pe.wait_ge(aT_s, s.count(1, 1))
                    wait(pe, hqT_s, s.count(1, 0))
                    for h in range(HALVES):
                        ins = M.matmul(ps_hq[:, h * P:(h + 1) * P], c_in[i][:, h * P:(h + 1) * P], aT[i][:], start=True, stop=True)
                    ins.then_inc(hq_ps, 1)
                u = s.plus(-4)
                if u.exists():
                    pe.wait_ge(x4T_s, u.count(1, 1))
                    for h in range(HALVES):
                        ins = M.matmul(ps_lg[0:EXPERTS, D:D + P], wg[:, h, :], x4T[u.k % 4][:, h, :], start=(h == 0), stop=(h == HALVES - 1))
                    ins.then_inc(lg_ps, 1)
                u = quad_of(s, 7)
                if s.k % 4 == 3 and u.exists():
                    pe.wait_ge(lg_s, u.count(1, 4))
                    wait(pe, chain, at(u, 13, -3))
                    M.matmul(ps_route[:, 0:E], lgT[:, 0, :], ident[0:E, 0:E], start=True, stop=True)
                    for t in range(1, QUAD):
                        ins = M.transpose(ps_route[:, t * E:(t + 1) * E], lgT[:, t, :], ident[0:E, 0:E])
                    ins.then_inc(lt_ps, 1)
                u = quad_of(s, 10)
                if s.k % 4 == 2 and u.exists():
                    pe.wait_ge(chosen_s, at(u, 1, 1))
                    C = QUAD * E
                    for t in range(QUAD):
                        M.matmul(ps_route[:, C + t * E:C + (t + 1) * E], S["before"][:], chosen[:, t, :], start=True, stop=(t == 0))
                        for r in range(t):
                            M.matmul(ps_route[:, C + t * E:C + (t + 1) * E], S["ones_b"][:], chosen[:, r, :], start=False, stop=(r == t - 1))
                    for t in range(QUAD):
                        ins = M.matmul(ps_route[:, 2 * C:2 * C + E], S["ones_b"][:], chosen[:, t, :], start=(t == 0), stop=(t == QUAD - 1))
                    ins.then_inc(cnt_ps, 1)

            deep_steps(pe, emit, HEAD, TAIL)


def first_choice_ffn(nc, S, T):
    ST = CAP // P
    with ExitStack() as ctx:
        sb = lambda n, s, d=F32: ctx.enter_context(nc.sbuf_tensor(n, s, d))
        two = lambda n, s, d=F32: [sb(f"{n}{i}", s, d) for i in range(2)]
        sem = ctx.enter_context(Semaphores(nc)).new
        rows, xn = [sb(f"g_rows{i}", [P, ST, ROW1]) for i in range(4)], [sb(f"g_xn{i}", [P, ST, D]) for i in range(3)]
        rT = two("g_rT", [P, HALVES, CAP])
        w, bias = ([sb(f"g_{n}{i}", s) for i in range(4)] for n, s in (("w", [P, HALVES, D]), ("b", [P, D])))
        yb, y, idx = two("g_yb", [P, ST, D]), two("g_y", [P, ST, D]), two("g_idx", [P, ST], I32)
        ps = [ctx.enter_context(nc.psum_tensor(f"pg{i}", [P, 512], F32)) for i in range(8)]
        sent = [sem(f"pg_sent{i}") for i in range(2)]
        in_s, w_in = ([sem(f"pg_{n}{i}") for i in range(4)] for n in ("in", "w"))
        xn_s, t_ps, rT_s, y_ps, yb_s, y_s, idx_s = (sem("pg_" + n) for n in ("xn", "t_ps", "rT", "y_ps", "yb", "y", "idx"))
        block = ctx.enter_context(nc.Block())
        slots_t = T["slots"].rearrange("(c p) d -> p c d", p=P)

        @block.sync
        def _(sp):
            def emit(e, par, first, last):
                if e >= 4:
                    sp.wait_ge(y_s, (e - 3) * ST)
                sp.dma_start(rows[e % 4][:], slots_t[:, bass.ds(e * ST, ST), :]).then_inc(in_s[e % 4], 16)
                sp.dma_start(w[e % 4][:], T["W1"][bass.ds(e, 1)].rearrange("a (h p) n -> p (a h) n", p=P)).then_inc(w_in[e % 4], 16)
                sp.dma_start(bias[e % 4][:], T["b1"][bass.ds(e, 1), :].rearrange("a n -> (a n)").partition_broadcast(P)).then_inc(w_in[e % 4], 16)

            for e in range(EXPERTS):
                emit(e, e % 2, e < 2, e == EXPERTS - 1)

        @block.gpsimd
        def _(pool):
            for e in range(EXPERTS):
                pool.wait_ge(idx_s, e + 1)
                for c in range(ST):
                    pool.wait_ge(y_s, e * ST + c + 1)
                    pool.indirect_dma_start(out=T["out"], out_offset=bass.IndirectOffsetOnAxis(ap=idx[e % 2][:, c:c + 1], axis=0),
                                            in_=y[e % 2][:, c, :], in_offset=None,
                                            bounds_check=TOKENS - 1, oob_is_err=False).then_inc(sent[e % 2], 16)
            for par in range(2):
                pool.wait_ge(sent[par], 16 * ST * EXPERTS // 2)

        @block.scalar
        def _(act):
            def emit(e, par, first, last):
                for h in range(HALVES):
                    act.wait_ge(t_ps, e + 1)
                    if not first:
                        act.wait_ge(y_ps, (e - 1) * 2)
                    nc.scalar.activation(rT[par][:, h, :], ps[par * 2 + h][:], ACT.Copy).then_inc(rT_s, 1)

            for e in range(EXPERTS):
                emit(e, e % 2, e < 2, e == EXPERTS - 1)

        @block.vector
        def _(dve):
            def norm(e):
                dve.wait_ge(in_s[e % 4], 16 * (e // 4 + 1))
                if e >= 3:
                    dve.wait_ge(t_ps, e - 2)
                for c in range(ST):
                    nc.vector.tensor_scalar(xn[e % 3][:, c, :], rows[e % 4][:, c, 0:D], rows[e % 4][:, c, D:D + 1], rows[e % 4][:, c, D + 1:D + 2],
                                            ALU.subtract, ALU.mult).then_inc(xn_s, 1)

            def emit(e, par, first, last):
                if e + 2 < EXPERTS:
                    norm(e + 2)
                if not first:
                    dve.wait_ge(sent[par], 16 * (e // 2) * ST)
                nc.vector.tensor_scalar(idx[par][:], rows[e % 4][:, :, D + 3], -1.0, float(TOKENS), ALU.mult, ALU.add).then_inc(idx_s, 1)
                dve.wait_ge(w_in[e % 4], 32 * (e // 4 + 1))
                for j in range(2):
                    dve.wait_ge(y_ps, e * 2 + (j + 1))
                    nc.vector.tensor_tensor(yb[par][:, 2 * j:2 * j + 2, :], ps[4 + par * 2 + j][:].rearrange("p (c d) -> p c d", c=2),
                                            bias[e % 4][:].unsqueeze(1).broadcast_to([P, 2, D]), ALU.add).then_inc(yb_s, 1)
                    dve.wait_ge(yb_s, e * 2 + (j + 1))
                    for c in (2 * j, 2 * j + 1):
                        nc.vector.scalar_tensor_tensor(y[par][:, c, :], yb[par][:, c, :], rows[e % 4][:, c, D + 2:D + 3],
                                                       rows[e % 4][:, c, 0:D], ALU.mult, ALU.add).then_inc(y_s, 1)

            norm(0)
            norm(1)
            for e in range(EXPERTS):
                emit(e, e % 2, e < 2, e == EXPERTS - 1)

        @block.tensor
        def _(pe):
            def turn(e, par, first):
                pe.wait_ge(xn_s, (e + 1) * ST)
                if not first:
                    pe.wait_ge(rT_s, (e - 1) * 2)
                for h in range(HALVES):
                    for c in range(ST):
                        ins = nc.tensor.transpose(ps[par * 2 + h][:, c * P:(c + 1) * P], xn[e % 3][:, c, h * P:(h + 1) * P], S["ident"][:])
                ins.then_inc(t_ps, 1)

            def emit(e, par, first, last):
                if not last:
                    turn(e + 1, 1 - par, first and par == 0)
                pe.wait_ge(rT_s, (e + 1) * 2)
                pe.wait_ge(w_in[e % 4], 32 * (e // 4 + 1))
                if not first:
                    pe.wait_ge(yb_s, (e - 1) * 2)
                for c in range(ST):
                    for h in range(HALVES):
                        ins = nc.tensor.matmul(ps[4 + par * 2 + c // 2][:, c % 2 * D:(c % 2 + 1) * D], rT[par][:, h, c * P:(c + 1) * P],
                                               w[e % 4][:, h, :], start=(h == 0), stop=(h == HALVES - 1))
                    if c % 2:
                        ins.then_inc(y_ps, 1)

            turn(0, 0, True)
            for e in range(EXPERTS):
                emit(e, e % 2, e < 2, e == EXPERTS - 1)


def program(nc, T):
    with ExitStack() as ctx:
        def keep(name, shape, dtype=F32):
            return ctx.enter_context(nc.sbuf_tensor("s_" + name, shape, dtype))

        S = {name: keep(name, shape, dtype) for name, shape, dtype in (
            ("ident", [P, P], F32), ("ident_b", [P, P], BF16), ("minus_half", [P, QUAD], F32), ("eps", [P, QUAD], F32), ("spare", [P, 1], F32), ("tanh_g", [P, 4], F32),
            ("zero", [P, ROW1], F32), ("logitsT", [EXPERTS, TOKENS], F32), ("ones_b", [P, P], BF16), ("before", [P, P], BF16),
            ("keep", [P, EXPERTS, TILES], F32))}
        setup(nc, S, T)
        project_qkv(nc, S, T)
        attention(nc, S, T)
        with ExitStack() as routed:
            S["score"] = routed.enter_context(nc.sbuf_tensor("s_score", [P, TILES, EXPERTS], F32))
            S["idx"] = routed.enter_context(nc.sbuf_tensor("s_idx", [P, EXPERTS, CAP // P], I32))
            route_top_k(nc, S, T)
            expert_choice_ffn(nc, S, T)
        bidirectional_attention(nc, S, T)
        first_choice_ffn(nc, S, T)


def kernel(**inputs):
    import concourse.bacc as bacc
    from concourse.bass_utils import run_bass_kernel_spmd

    laid = {
        "x": inputs["x"].reshape(TOKENS, D), "ctx": inputs["ctx_1024"].reshape(TOKENS, D), "mask": inputs["mask_BxS2_ik0"],
        "g_xattn": inputs["g_xattn"], "g_ffn": inputs["g_ffn"],
    }
    for name in ("Wq", "bq", "Wk", "bk", "Wv", "bv", "Wo", "bo"):
        laid[name] = inputs["L0_xattn_" + name]
    for name in ("Wr", "br", "W_up", "b_up", "W_down", "b_down"):
        laid[name] = inputs["L0_ffn_" + name]
    for name in ("w_sim", "b_sim", "W_qv", "b_qv"):
        laid[name] = inputs["L1_xattn_" + name]
    laid["wg"] = inputs["L1_ffn_wg"]
    laid["W1"] = inputs["L1_ffn_W"].transpose(0, 2, 1)
    laid["b1"] = inputs["L1_ffn_b"]

    nc = bacc.Bacc("TRN2", target_bir_lowering=False, num_devices=1)
    arrays, T = {}, {}
    for name, a in laid.items():
        a = np.ascontiguousarray(a)
        arrays["in_" + name] = a
        T[name] = nc.dram_tensor("in_" + name, a.shape, mybir.dt.from_np(a.dtype), kind="ExternalInput").ap()
    for name, shape, dtype in (
            ("mask_row", (TOKENS,), BF16), ("ones_row", (TOKENS,), BF16), ("qparts", (2, D, TOKENS), BF16), ("kparts", (2, D, TOKENS), BF16), ("v", (TOKENS, D), F32),
            ("resid", (TOKENS, D), F32), ("rows0", (TOKENS, ROW0), F32), 
            ("slots", (TOKENS, ROW1), F32)):
        T[name] = nc.dram_tensor("scratch_" + name, shape, dtype, kind="Internal").ap()
    T["out"] = nc.dram_tensor("result", (TOKENS, D), F32, kind="ExternalOutput").ap()
    program(nc, T)
    r = run_bass_kernel_spmd(nc, [arrays], core_ids=[0])
    return r.results[0]["result"].reshape(BATCHES, SEQ, D)
```
